# Optimizing a Trainium2 kernel written in Bass

```python
import numpy as np
import jax
import jax.numpy as jnp

def _softmax(x, axis=-1):
    return jax.nn.softmax(x, axis=axis)

def _gelu(x):
    return jax.nn.gelu(x, approximate=True)

def _silu(x):
    return jax.nn.silu(x)

def _sigmoid(x):
    return jax.nn.sigmoid(x)

def _layernorm(x, axis=-1, eps=1e-05):
    m = jnp.mean(x, axis=axis, keepdims=True)
    v = jnp.var(x, axis=axis, keepdims=True)
    return (x - m) / jnp.sqrt(v + eps)

def _scatter_add(tgt, idx, src, axis=0):
    return tgt.at[idx].add(src)

def _segment_sum(src, seg, n):
    return jax.ops.segment_sum(src, seg, n)
kernel_name = 'mk_adaln_d2_jaxref_r4_fc2bb1'

def setup_inputs(seed: int=0):
    np.random.seed(seed)
    _w = jnp.asarray

    def _L0_attn_setup():
        import jax, jax.numpy as jnp
        import numpy as np
        DIM = 256
        NUM_HEADS = 16
        HEAD_DIM = DIM // NUM_HEADS
        WINDOW = 64
        B, L = (2, 512)
        EPS = 1e-05
        INIT_STD = 0.01

        def rmsnorm(x, w):
            x = jnp.clip(x, -10000.0, 10000.0)
            rms = jnp.sqrt(jnp.maximum(jnp.mean(x * x, axis=-1, keepdims=True), EPS) + EPS)
            out = x / rms * w
            return jnp.where(jnp.isfinite(out), out, jnp.zeros_like(out))
        key = jax.random.key(seed)
        ks = jax.random.split(key, 6)
        return {'x': jax.random.normal(ks[0], (B, L, DIM), dtype=jnp.float32), 'wq_w': jax.random.normal(ks[1], (DIM, DIM), dtype=jnp.float32) * INIT_STD, 'wq_b': jnp.zeros((DIM,), jnp.float32), 'wk_w': jax.random.normal(ks[2], (DIM, DIM), dtype=jnp.float32) * INIT_STD, 'wk_b': jnp.zeros((DIM,), jnp.float32), 'wv_w': jax.random.normal(ks[3], (DIM, DIM), dtype=jnp.float32) * INIT_STD, 'wv_b': jnp.zeros((DIM,), jnp.float32), 'wo_w': jax.random.normal(ks[4], (DIM, DIM), dtype=jnp.float32) * INIT_STD, 'wo_b': jnp.zeros((DIM,), jnp.float32), 'qn_w': jnp.ones((HEAD_DIM,), jnp.float32), 'kn_w': jnp.ones((HEAD_DIM,), jnp.float32)}
    _L0_attn_in = _L0_attn_setup()

    def _L0_ffn_setup():
        import jax, jax.numpy as jnp
        import numpy as np
        B, S, D, H, E = (4, 512, 256, 1024, 8)
        EPS = 1e-12

        def _wn(v, g):
            n = jnp.sqrt(jnp.sum(v * v, axis=-1, keepdims=True))
            return v / jnp.maximum(n, EPS) * g[:, None]
        key = jax.random.key(seed)
        ks = jax.random.split(key, 8)
        return {'x': jax.random.normal(ks[0], (B, S, D), dtype=jnp.float32), 'gate_v': jax.random.normal(ks[1], (E, D), dtype=jnp.float32), 'gate_g': jnp.ones((E,), dtype=jnp.float32), 'gate_b': jnp.zeros((E,), dtype=jnp.float32), 'w1_v': jax.random.normal(ks[2], (E, H, D), dtype=jnp.float32), 'w1_g': jnp.ones((E, H), dtype=jnp.float32), 'b1': jnp.zeros((E, H), dtype=jnp.float32), 'w2_v': jax.random.normal(ks[3], (E, D, H), dtype=jnp.float32), 'w2_g': jnp.ones((E, D), dtype=jnp.float32), 'b2': jnp.zeros((E, D), dtype=jnp.float32)}
    _L0_ffn_in = _L0_ffn_setup()
    _L0_c = _w((lambda *s: np.random.randn(*s).astype(np.float32) * 0.05)(4, 256))
    _L0_wmod = _w((lambda *s: np.random.randn(*s).astype(np.float32) * 0.05)(256, 6 * 256) * 256 ** (-0.5))

    def _L1_attn_setup():
        import jax, jax.numpy as jnp
        import numpy as np
        ROPE_THETA = 10000.0
        N_HEAD = 16

        def _rope(x, theta):
            T, D = (x.shape[-2], x.shape[-1])
            pos = jnp.arange(T, dtype=jnp.float32)
            inv_freq = 1.0 / theta ** (jnp.arange(0, D, 2, dtype=jnp.float32) / D)
            freqs = pos[:, None] * inv_freq[None, :]
            cos = jnp.cos(freqs).astype(x.dtype)[None, None]
            sin = jnp.sin(freqs).astype(x.dtype)[None, None]
            x_even = x[..., ::2]
            x_odd = x[..., 1::2]
            rot = jnp.stack((x_even * cos - x_odd * sin, x_even * sin + x_odd * cos), axis=-1)
            return rot.reshape(x.shape)
        key = jax.random.key(seed)
        ks = jax.random.split(key, 5)
        B, T, E = (4, 512, 256)
        s = 0.02
        return {'x': jax.random.normal(ks[0], (B, T, E), jnp.float32), 'Wqkv': jax.random.normal(ks[1], (E, 3 * E), jnp.float32) * s, 'bqkv': jax.random.normal(ks[2], (3 * E,), jnp.float32) * s, 'Wproj': jax.random.normal(ks[3], (E, E), jnp.float32) * s, 'bproj': jax.random.normal(ks[4], (E,), jnp.float32) * s}
    _L1_attn_in = _L1_attn_setup()

    def _L1_ffn_setup():
        import jax, jax.numpy as jnp
        import numpy as np
        E = 8
        TOP_K = 2
        LN_EPS = 1e-05

        def _layernorm(x, g, b):
            mu = jnp.mean(x, axis=-1, keepdims=True)
            var = jnp.var(x, axis=-1, keepdims=True)
            return (x - mu) * jax.lax.rsqrt(var + LN_EPS) * g + b
        key = jax.random.key(seed)
        ks = jax.random.split(key, 4)
        B, T, H, HF = (4, 512, 256, 512)
        s_in = 1.0 / np.sqrt(H)
        s_hid = 1.0 / np.sqrt(HF)
        return {'x': jax.random.normal(ks[0], (B, T, H), dtype=jnp.float32), 'ln_g': jnp.ones((H,), dtype=jnp.float32), 'ln_b': jnp.zeros((H,), dtype=jnp.float32), 'rW': jax.random.normal(ks[1], (H, E), dtype=jnp.float32) * s_in, 'rb': jnp.zeros((E,), dtype=jnp.float32), 'W1': jax.random.normal(ks[2], (E, H, HF), dtype=jnp.float32) * s_in, 'b1': jnp.zeros((E, HF), dtype=jnp.float32), 'W2': jax.random.normal(ks[3], (E, HF, H), dtype=jnp.float32) * s_hid, 'b2': jnp.zeros((E, H), dtype=jnp.float32)}
    _L1_ffn_in = _L1_ffn_setup()
    _L1_c = _w((lambda *s: np.random.randn(*s).astype(np.float32) * 0.05)(4, 256))
    _L1_wmod = _w((lambda *s: np.random.randn(*s).astype(np.float32) * 0.05)(256, 6 * 256) * 256 ** (-0.5))
    _d = {'L0_attn_x': _L0_attn_in['x'], 'L0_attn_wq_w': _L0_attn_in['wq_w'], 'L0_attn_wq_b': _L0_attn_in['wq_b'], 'L0_attn_wk_w': _L0_attn_in['wk_w'], 'L0_attn_wk_b': _L0_attn_in['wk_b'], 'L0_attn_wv_w': _L0_attn_in['wv_w'], 'L0_attn_wv_b': _L0_attn_in['wv_b'], 'L0_attn_wo_w': _L0_attn_in['wo_w'], 'L0_attn_wo_b': _L0_attn_in['wo_b'], 'L0_attn_qn_w': _L0_attn_in['qn_w'], 'L0_attn_kn_w': _L0_attn_in['kn_w'], 'L0_ffn_gate_v': _L0_ffn_in['gate_v'], 'L0_ffn_gate_g': _L0_ffn_in['gate_g'], 'L0_ffn_gate_b': _L0_ffn_in['gate_b'], 'L0_ffn_w1_v': _L0_ffn_in['w1_v'], 'L0_ffn_w1_g': _L0_ffn_in['w1_g'], 'L0_ffn_b1': _L0_ffn_in['b1'], 'L0_ffn_w2_v': _L0_ffn_in['w2_v'], 'L0_ffn_w2_g': _L0_ffn_in['w2_g'], 'L0_ffn_b2': _L0_ffn_in['b2'], 'L0_c': _L0_c, 'L0_wmod': _L0_wmod, 'L1_attn_Wqkv': _L1_attn_in['Wqkv'], 'L1_attn_bqkv': _L1_attn_in['bqkv'], 'L1_attn_Wproj': _L1_attn_in['Wproj'], 'L1_attn_bproj': _L1_attn_in['bproj'], 'L1_ffn_ln_g': _L1_ffn_in['ln_g'], 'L1_ffn_ln_b': _L1_ffn_in['ln_b'], 'L1_ffn_rW': _L1_ffn_in['rW'], 'L1_ffn_rb': _L1_ffn_in['rb'], 'L1_ffn_W1': _L1_ffn_in['W1'], 'L1_ffn_b1': _L1_ffn_in['b1'], 'L1_ffn_W2': _L1_ffn_in['W2'], 'L1_ffn_b2': _L1_ffn_in['b2'], 'L1_c': _L1_c, 'L1_wmod': _L1_wmod}
    _x0 = _d['L0_attn_x']
    _d['L0_attn_x'] = jax.random.normal(jax.random.fold_in(jax.random.key(seed), 1), (4, 1024, 256), dtype=_x0.dtype)
    del _x0
    return _d

def reference(L0_attn_x, L0_attn_wq_w, L0_attn_wq_b, L0_attn_wk_w, L0_attn_wk_b, L0_attn_wv_w, L0_attn_wv_b, L0_attn_wo_w, L0_attn_wo_b, L0_attn_qn_w, L0_attn_kn_w, L0_ffn_gate_v, L0_ffn_gate_g, L0_ffn_gate_b, L0_ffn_w1_v, L0_ffn_w1_g, L0_ffn_b1, L0_ffn_w2_v, L0_ffn_w2_g, L0_ffn_b2, L0_c, L0_wmod, L1_attn_Wqkv, L1_attn_bqkv, L1_attn_Wproj, L1_attn_bproj, L1_ffn_ln_g, L1_ffn_ln_b, L1_ffn_rW, L1_ffn_rb, L1_ffn_W1, L1_ffn_b1, L1_ffn_W2, L1_ffn_b2, L1_c, L1_wmod):

    def _L0_attn_ref(x, wq_w, wq_b, wk_w, wk_b, wv_w, wv_b, wo_w, wo_b, qn_w, kn_w):
        import jax, jax.numpy as jnp
        import numpy as np
        DIM = 256
        NUM_HEADS = 16
        HEAD_DIM = DIM // NUM_HEADS
        WINDOW = 64
        B, L = (2, 512)
        EPS = 1e-05
        INIT_STD = 0.01

        def rmsnorm(x, w):
            x = jnp.clip(x, -10000.0, 10000.0)
            rms = jnp.sqrt(jnp.maximum(jnp.mean(x * x, axis=-1, keepdims=True), EPS) + EPS)
            out = x / rms * w
            return jnp.where(jnp.isfinite(out), out, jnp.zeros_like(out))
        b, l, d = x.shape
        x = x.astype(jnp.float32)

        def proj(w, bias):
            return (x @ w.T + bias).reshape(b, l, NUM_HEADS, HEAD_DIM).transpose(0, 2, 1, 3)
        q = rmsnorm(proj(wq_w, wq_b), qn_w)
        k = rmsnorm(proj(wk_w, wk_b), kn_w)
        v = proj(wv_w, wv_b)
        scale = HEAD_DIM ** (-0.5)
        i = jnp.arange(l)
        allowed = (i[None, :] <= i[:, None]) & (i[:, None] - i[None, :] < WINDOW)
        scores = jnp.einsum('bhqd,bhkd->bhqk', q, k) * scale
        scores = jnp.where(allowed[None, None], scores, -jnp.inf)
        attn = jax.nn.softmax(scores, axis=-1)
        out = jnp.einsum('bhqk,bhkd->bhqd', attn, v)
        out = jnp.where(jnp.isfinite(out), out, jnp.zeros_like(out))
        out = out.transpose(0, 2, 1, 3).reshape(b, l, d)
        return out @ wo_w.T + wo_b

    def _L0_ffn_ref(x, gate_v, gate_g, gate_b, w1_v, w1_g, b1, w2_v, w2_g, b2):
        import jax, jax.numpy as jnp
        import numpy as np
        B, S, D, H, E = (4, 512, 256, 1024, 8)
        EPS = 1e-12

        def _wn(v, g):
            n = jnp.sqrt(jnp.sum(v * v, axis=-1, keepdims=True))
            return v / jnp.maximum(n, EPS) * g[:, None]
        b, s, d = x.shape
        xf = x.reshape(-1, d)
        gw = _wn(gate_v, gate_g)
        gates = jax.nn.softmax(xf @ gw.T + gate_b, axis=-1)
        top_k = min(2, E)
        _, top_idx = jax.lax.top_k(gates, top_k)
        out = jnp.zeros_like(xf)
        for i in range(E):
            mask = jnp.any(top_idx == i, axis=1).astype(xf.dtype)[:, None]
            xm = xf * mask
            W1 = _wn(w1_v[i], w1_g[i])
            h = xm @ W1.T + b1[i]
            h = h * jax.nn.sigmoid(h)
            W2 = _wn(w2_v[i], w2_g[i])
            out = out + mask * (h @ W2.T + b2[i])
        return out.reshape(b, s, d)

    def _L1_attn_ref(x, Wqkv, bqkv, Wproj, bproj):
        import jax, jax.numpy as jnp
        import numpy as np
        ROPE_THETA = 10000.0
        N_HEAD = 16

        def _rope(x, theta):
            T, D = (x.shape[-2], x.shape[-1])
            pos = jnp.arange(T, dtype=jnp.float32)
            inv_freq = 1.0 / theta ** (jnp.arange(0, D, 2, dtype=jnp.float32) / D)
            freqs = pos[:, None] * inv_freq[None, :]
            cos = jnp.cos(freqs).astype(x.dtype)[None, None]
            sin = jnp.sin(freqs).astype(x.dtype)[None, None]
            x_even = x[..., ::2]
            x_odd = x[..., 1::2]
            rot = jnp.stack((x_even * cos - x_odd * sin, x_even * sin + x_odd * cos), axis=-1)
            return rot.reshape(x.shape)
        B, T, E = x.shape
        H = N_HEAD
        D = E // H
        qkv = x @ Wqkv + bqkv
        q, k, v = jnp.split(qkv, 3, axis=-1)
        q = q.reshape(B, T, H, D).transpose(0, 2, 1, 3)
        k = k.reshape(B, T, H, D).transpose(0, 2, 1, 3)
        v = v.reshape(B, T, H, D).transpose(0, 2, 1, 3)
        q = _rope(q, ROPE_THETA)
        k = _rope(k, ROPE_THETA)
        scores = jnp.einsum('bhqd,bhkd->bhqk', q, k) * D ** (-0.5)
        causal = jnp.tril(jnp.ones((T, T), dtype=bool))
        scores = jnp.where(causal[None, None], scores, -jnp.inf)
        weights = jax.nn.softmax(scores, axis=-1)
        out = jnp.einsum('bhqk,bhkd->bhqd', weights, v)
        out = out.transpose(0, 2, 1, 3).reshape(B, T, E)
        return out @ Wproj + bproj

    def _L1_ffn_ref(x, ln_g, ln_b, rW, rb, W1, b1, W2, b2):
        import jax, jax.numpy as jnp
        import numpy as np
        E = 8
        TOP_K = 2
        LN_EPS = 1e-05

        def _layernorm(x, g, b):
            mu = jnp.mean(x, axis=-1, keepdims=True)
            var = jnp.var(x, axis=-1, keepdims=True)
            return (x - mu) * jax.lax.rsqrt(var + LN_EPS) * g + b
        z = _layernorm(x, ln_g, ln_b)
        logits = jnp.einsum('bth,he->bte', z, rW) + rb
        probs = jax.nn.softmax(logits, axis=-1)
        topv, topi = jax.lax.top_k(probs, TOP_K)
        mask = jnp.sum(jax.nn.one_hot(topi, E, dtype=probs.dtype) * topv[..., None], axis=-2)
        denom = jnp.maximum(jnp.sum(mask, axis=-1, keepdims=True), 1e-08)
        w = mask / denom
        hid = jax.nn.gelu(jnp.einsum('bth,ehf->btef', z, W1) + b1, approximate=False)
        outs = jnp.einsum('btef,efh->bteh', hid, W2) + b2
        mixed = jnp.sum(outs * w[..., None], axis=2)
        return x + mixed
    x = L0_attn_x
    mod = (_silu(L0_c) @ L0_wmod).reshape(L0_c.shape[0], 6, 1, -1)
    sa, ca, ga, sb, cb, gb = (mod[:, 0], mod[:, 1], mod[:, 2], mod[:, 3], mod[:, 4], mod[:, 5])
    ga = (2 * (ga >= 0) - 1) * jnp.maximum(jnp.abs(ga), 0.25)
    gb = (2 * (gb >= 0) - 1) * jnp.maximum(jnp.abs(gb), 0.25)
    h = _layernorm(x, axis=-1) * (1 + ca) + sa
    x = x + ga * _L0_attn_ref(h, L0_attn_wq_w, L0_attn_wq_b, L0_attn_wk_w, L0_attn_wk_b, L0_attn_wv_w, L0_attn_wv_b, L0_attn_wo_w, L0_attn_wo_b, L0_attn_qn_w, L0_attn_kn_w)
    h = _layernorm(x, axis=-1) * (1 + cb) + sb
    x = x + gb * _L0_ffn_ref(h, L0_ffn_gate_v, L0_ffn_gate_g, L0_ffn_gate_b, L0_ffn_w1_v, L0_ffn_w1_g, L0_ffn_b1, L0_ffn_w2_v, L0_ffn_w2_g, L0_ffn_b2)
    mod = (_silu(L1_c) @ L1_wmod).reshape(L1_c.shape[0], 6, 1, -1)
    sa, ca, ga, sb, cb, gb = (mod[:, 0], mod[:, 1], mod[:, 2], mod[:, 3], mod[:, 4], mod[:, 5])
    ga = (2 * (ga >= 0) - 1) * jnp.maximum(jnp.abs(ga), 0.25)
    gb = (2 * (gb >= 0) - 1) * jnp.maximum(jnp.abs(gb), 0.25)
    h = _layernorm(x, axis=-1) * (1 + ca) + sa
    x = x + ga * _L1_attn_ref(h, L1_attn_Wqkv, L1_attn_bqkv, L1_attn_Wproj, L1_attn_bproj)
    h = _layernorm(x, axis=-1) * (1 + cb) + sb
    x = x + gb * _L1_ffn_ref(h, L1_ffn_ln_g, L1_ffn_ln_b, L1_ffn_rW, L1_ffn_rb, L1_ffn_W1, L1_ffn_b1, L1_ffn_W2, L1_ffn_b2)
    return x

_drawn_inputs = setup_inputs


def setup_inputs(seed=0):
    import zlib

    import numpy as np

    out = dict(_drawn_inputs(seed))
    spreads = {'L0_attn_wq_b': (0.0, 0.8),
     'L0_attn_wk_b': (0.0, 0.8),
     'L0_attn_wv_b': (0.0, 0.507),
     'L0_attn_wo_b': (0.0, 0.1),
     'L0_attn_qn_w': (1.0, 0.6),
     'L0_attn_kn_w': (1.0, 0.6),
     'L0_ffn_gate_g': (1.0, 0.2),
     'L0_ffn_gate_b': (0.0, 0.1),
     'L0_ffn_w1_g': (1.0, 0.2),
     'L0_ffn_b1': (0.0, 0.308),
     'L0_ffn_w2_g': (1.0, 0.2),
     'L0_ffn_b2': (0.0, 0.1),
     'L1_ffn_ln_g': (1.0, 0.2),
     'L1_ffn_ln_b': (0.0, 0.268),
     'L1_ffn_rb': (0.0, 0.269),
     'L1_ffn_b1': (0.0, 0.661),
     'L1_ffn_b2': (0.0, 0.45)}
    factors = {'L0_attn_wq_w': 8.0,
     'L0_attn_wk_w': 7.089,
     'L0_attn_wv_w': 6.74,
     'L0_attn_wo_w': 3.813,
     'L1_attn_Wqkv': 8.0,
     'L1_attn_bqkv': 8.0,
     'L1_attn_Wproj': 8.0,
     'L1_attn_bproj': 7.753}
    for name, (base, spread) in spreads.items():
        noise = np.random.default_rng([zlib.crc32(name.encode()), seed]).standard_normal(out[name].shape)
        drawn = base * np.exp(spread * noise) if base else spread * noise
        out[name] = jnp.asarray(drawn.astype(out[name].dtype))
    for name, factor in factors.items():
        out[name] = (out[name] * factor).astype(out[name].dtype)
    return out
```

```python
from contextlib import ExitStack

import numpy as np

import concourse.bass as bass
from concourse import mybir

ACT = mybir.ActivationFunctionType
ALU = mybir.AluOpType
AX = mybir.AxisListType
F32 = mybir.dt.float32
BF16 = mybir.dt.bfloat16
F16 = mybir.dt.float16
U32 = mybir.dt.uint32
I32 = mybir.dt.int32

P = 128
B, L, D = 4, 1024, 256
N_TOK = B * L
TILES = N_TOK // P
TPB = L // P
DC = D // P
HEADS, HD = 16, 16
HG = 4
STEPS = B * HEADS // HG
WINDOW = 64
EXPERTS = 8
ROWS = 256
XT = 2 * N_TOK // ROWS + EXPERTS
EPS = 1e-5
NEG = -1e30
SLOTS = 6
KROWS = SLOTS * HD
KAUG = KROWS + 3
QK = 4
HALF = 512
HT = HALF // P


def constants():
    r = np.arange(P)
    out = {}
    out["c_ident"] = np.eye(P, dtype=np.float32)
    out["c_heads"] = (r[:, None] // HD == r[None, :] // HD).astype(np.float32)
    out["c_swap"] = ((r[:, None] ^ 1) == r[None, :]).astype(np.float32)
    q, k = r[:, None], r[None, :]
    causal = np.where(k <= q, 0.0, NEG).astype(np.float32)
    out["c_causal"] = np.stack([causal, causal.T], 1)
    prev = np.where(q - (k - P) < WINDOW, 0.0, NEG)
    diag = np.where((k <= q) & (q - k < WINDOW), 0.0, NEG)
    out["c_window"] = np.stack([np.concatenate([prev, diag], 1), np.concatenate([diag.T, prev.T], 1)], 1).astype(np.float32)
    out["c_iota"] = np.tile(np.arange(64, dtype=np.float32), (P, 1))
    out["c_before"] = (r[:, None] < r[None, :]).astype(np.float32)
    inv = (1.0 / np.float32(10000.0) ** (np.arange(0, HD, 2, dtype=np.float32) / np.float32(HD))).astype(np.float32)
    ang = (np.arange(L, dtype=np.float32)[None, :] * inv[(r % HD) // 2][:, None]).astype(np.float32)
    sign = np.where(r % 2 == 0, -1.0, 1.0).astype(np.float32)[:, None]
    out["c_rope"] = np.stack([np.cos(ang), np.sin(ang) * sign], 1).astype(np.float32)
    return out


class Program:

    def __init__(self, nc, dram, out):
        self.nc, self.dram, self.out = nc, dram, out
        self.ctx = ExitStack()

    def sb(self, ctx, name, shape, dt=F32):
        return ctx.enter_context(self.nc.sbuf_tensor(name, shape, dt))

    def ps(self, ctx, name, shape, dt=F32):
        return ctx.enter_context(self.nc.psum_tensor(name, shape, dt))

    def sem(self, ctx, name):
        handle = ctx.enter_context(self.nc.semaphore(name))
        ctx.callback(lambda: self.nc.gpsimd.sem_clear(handle))
        return handle

    def build(self, stop=None):
        with self.ctx as ctx:
            self.resident(ctx)
            self.setup()
            for layer in (0, 1):
                self.project(layer)
                with ExitStack() as hold:
                    self.attn = self.sb(hold, f"attn{layer}", [P, TILES, D])
                    self.attend(layer)
                    self.out_project(layer)
                if stop == f"attn{layer}":
                    break
                self.moe(layer)
                if stop == f"moe{layer}":
                    break
            self.store()

    def resident(self, ctx):
        self.x = self.sb(ctx, "x_res", [P, TILES, D])
        self.ident = self.sb(ctx, "ident", [P, P])
        self.ident_bf = self.sb(ctx, "ident_bf", [P, P], BF16)
        self.ident_h = self.sb(ctx, "ident_h", [P, P], F16)
        self.causal = self.sb(ctx, "causal", [P, 2, P], BF16)
        self.window = self.sb(ctx, "window", [P, 2, 2 * P], BF16)
        self.mod_col = self.sb(ctx, "mod_col", [P, 2, 12, B])
        nc = self.nc
        keep = lambda n: ctx.enter_context(nc.semaphore(n))
        self.zero_out, self.sent, self.got_in = keep("zero_out"), [keep("sent0"), keep("sent1")], [keep(f"got_in{i}") for i in range(4)]
        self.mod_d = nc.dram_tensor("mod_d", (P, 2, 4, B, D), F32, kind="Internal").ap()
        self.parts_d = nc.dram_tensor("parts_d", (2, 3, QK * P, N_TOK), BF16, kind="Internal").ap()
        self.v_d = nc.dram_tensor("v_d", (2, N_TOK, 2 * D), F32, kind="Internal").ap()

    def setup(self):
        nc, d = self.nc, self.dram
        with ExitStack() as ctx:
            cT = self.sb(ctx, "cT", [P, 2, DC, B])
            sT = self.sb(ctx, "sT", [P, 2, DC, B])
            sgm = self.sb(ctx, "sgm", [P, 2, DC, B])
            sbc = self.sb(ctx, "sbc", [P, 2, DC, B, P])
            wmod = self.sb(ctx, "wmod", [P, 2, DC, 6 * D])
            stage = self.sb(ctx, "stage", [P, 6 * P])
            gtmp = self.sb(ctx, "gtmp", [P, 2, D])
            mod_row = self.sb(ctx, "mod_row", [P, 2, 4, B, D])
            mod_out = self.sem(ctx, "mod_out")
            ones = self.sb(ctx, "ones", [P, P])
            pcol = self.ps(ctx, "pcol", [P, 2, 512])
            prow = self.ps(ctx, "prow", [P, 4, 512])
            x_in = self.sem(ctx, "x_in")
            mod_in = self.sem(ctx, "mod_in")
            const_in = self.sem(ctx, "const_in")
            cast = self.sem(ctx, "cast")
            ones_set = self.sem(ctx, "ones_set")
            sig = self.sem(ctx, "sig")
            silu = self.sem(ctx, "silu")
            spread = self.sem(ctx, "spread")
            col_mm = self.sem(ctx, "col_mm")
            row_mm = self.sem(ctx, "row_mm")
            row_ev = self.sem(ctx, "row_ev")
            mod_ch = self.sem(ctx, "mod_ch")
            with nc.Block() as block:
                @block.sync
                def _(sp):
                    for l in range(2):
                        for c in range(DC):
                            with nc.allow_non_contiguous_dma(reason="a small transposed load"):
                                sp.dma_start(cT[:, l, c, :], d[f"L{l}_c"][:, c * P:(c + 1) * P].rearrange("b p -> p b")).then_inc(mod_in, 16)
                        sp.dma_start(wmod[:, l, :, :], d[f"L{l}_wmod"].rearrange("(c p) n -> p c n", p=P)).then_inc(mod_in, 16)
                    sp.dma_start(self.ident[:, :], d["c_ident"]).then_inc(const_in, 16)
                    sp.dma_start(stage[:, 0:2 * P], d["c_causal"].rearrange("p a n -> p (a n)")).then_inc(const_in, 16)
                    sp.dma_start(stage[:, 2 * P:6 * P], d["c_window"].rearrange("p a n -> p (a n)")).then_inc(const_in, 16)
                    sp.dma_start(self.x[:, :, :], d["L0_attn_x"].rearrange("b (t p) d -> p (b t) d", p=P)).then_inc(x_in, 16)
                    sp.wait_ge(row_ev, 16)
                    sp.dma_start(self.mod_d, mod_row[:, :, :, :, :]).then_inc(mod_out, 16)
                    sp.wait_ge(mod_out, 16)
                    sp.wait_ge(x_in, 16)

                @block.gpsimd
                def _(pool):
                    pool.memset(ones[:, :], 1.0).then_inc(ones_set, 1)
                    pool.wait_ge(const_in, 48)
                    pool.tensor_copy(self.ident_bf[:, :], self.ident[:, :]).then_inc(cast, 1)
                    pool.tensor_copy(self.ident_h[:, :], self.ident[:, :]).then_inc(cast, 1)
                    pool.tensor_copy(self.causal[:, :, :].rearrange("p a n -> p (a n)"), stage[:, 0:2 * P]).then_inc(cast, 1)
                    pool.tensor_copy(self.window[:, :, :].rearrange("p a n -> p (a n)"), stage[:, 2 * P:6 * P]).then_inc(cast, 1)

                @block.scalar
                def _(act):
                    act.wait_ge(mod_in, 16 * 6)
                    nc.scalar.activation(sgm[:, :, :, :], cT[:, :, :, :], ACT.Sigmoid).then_inc(sig, 1)

                @block.vector
                def _(dve):
                    dve.wait_ge(sig, 1)
                    nc.vector.tensor_tensor(sT[:, :, :, :], cT[:, :, :, :], sgm[:, :, :, :], ALU.mult).then_inc(silu, 1)
                    dve.wait_ge(silu, 1)
                    dve.wait_ge(ones_set, 1)
                    for l in range(2):
                        for c in range(DC):
                            for b in range(B):
                                nc.vector.tensor_scalar(sbc[:, l, c, b, :], ones[:, :], sT[:, l, c, b:b + 1], None, ALU.mult).then_inc(spread, 1)
                    for l in range(2):
                        dve.wait_ge(col_mm, l + 1)
                        cols = pcol[:, l, 0:12 * B].rearrange("p (m b) -> p m b", b=B)
                        nc.vector.tensor_copy(self.mod_col[:, l, :, :], cols).then_inc(mod_ch, 1)
                        dve.wait_ge(mod_ch, 2 * l + 1)
                        ca = self.mod_col[:, l, :, :].rearrange("p (g six) b -> p g six b", six=6)[:, :, 2:4, :]
                        nc.vector.tensor_scalar(ca, ca, 1.0, None, ALU.add).then_inc(mod_ch, 1)
                    n = 0
                    for l in range(2):
                        for kind in range(4):
                            for bp in range(B // 2):
                                dve.wait_ge(row_mm, n + 1)
                                src = prow[:, n % 4, :].rearrange("p (b d) -> p b d", d=D)
                                dst = mod_row[:, l, kind, 2 * bp:2 * bp + 2, :]
                                if kind >= 2:
                                    nc.vector.tensor_scalar(dst, src, float(kind - 2), None, ALU.add).then_inc(row_ev, 1)
                                else:
                                    dve.wait_ge(row_ev, n)
                                    m = 4 + 3 * (l * 4 + kind * 2 + bp)
                                    nc.vector.tensor_scalar(gtmp[:, :, :], src, 0.0, 2.0, ALU.is_ge, ALU.mult).then_inc(mod_ch, 1)
                                    dve.wait_ge(mod_ch, m + 1)
                                    nc.vector.tensor_scalar(gtmp[:, :, :], gtmp[:, :, :], -1.0, None, ALU.add).then_inc(mod_ch, 1)
                                    dve.wait_ge(mod_ch, m + 2)
                                    nc.vector.tensor_tensor(dst, gtmp[:, :, :], src, ALU.mult).then_inc(mod_ch, 1)
                                    dve.wait_ge(mod_ch, m + 3)
                                    nc.vector.scalar_tensor_tensor(out=dst, in0=dst, scalar=0.25, in1=gtmp[:, :, :], op0=ALU.max, op1=ALU.mult).then_inc(row_ev, 1)
                                n += 1

                @block.tensor
                def _(pe):
                    pe.wait_ge(silu, 1)
                    for l in range(2):
                        for m in range(12):
                            for c in range(DC):
                                mm = nc.tensor.matmul(pcol[:, l, m * B:(m + 1) * B], wmod[:, l, c, m * P:(m + 1) * P], sT[:, l, c, :],
                                                      start=(c == 0), stop=(c == DC - 1))
                        mm.then_inc(col_mm, 1)
                    pe.wait_ge(spread, 2 * DC * B)
                    n = 0
                    for l in range(2):
                        for kind, at in enumerate((2, 5, 3, 4)):
                            for bp in range(B // 2):
                                if n >= 4:
                                    pe.wait_ge(row_ev, n - 3)
                                for bb in range(2):
                                    for c in range(DC):
                                        mm = nc.tensor.matmul(prow[:, n % 4, bb * D:(bb + 1) * D], sbc[:, l, c, 2 * bp + bb, :],
                                                              wmod[:, l, c, at * D:(at + 1) * D], start=(c == 0), stop=(c == DC - 1))
                                mm.then_inc(row_mm, 1)
                                n += 1

    def project(self, layer):
        nc, d = self.nc, self.dram
        rope = layer == 1
        with ExitStack() as ctx:
            T = f"p{layer}_"
            sb = lambda n, s, t=F32: self.sb(ctx, T + n, s, t)
            sem = lambda n: self.sem(ctx, T + n)
            w = sb("w", [P, DC, 3 * D])
            bias = sb("bias", [P, QK])
            nw = sb("nw", [P, 2])
            bv = sb("bv", [P, D])
            aux = sb("aux", [P, P])
            cs = sb("cs", [P, 2, L]) if rope else None
            stats = sb("stats", [P, HT, nc.vector.BN_STATS_DIM])
            mv = sb("mv", [P, HT, 2])
            sd = sb("sd", [P, HT])
            rstd = sb("rstd", [P, HT])
            eps = sb("eps", [P, 1])
            modb = sb("modb", [P, 2, DC])
            xn = sb("xn", [P, 2, HT, D])
            hT = sb("hT", [P, 2, DC, HALF])
            u = sb("u", [P, 2, HALF])
            sq = sb("sq", [P, 2, HALF])
            rn = sb("rn", [P, 2, HALF])
            un = sb("un", [P, 2, HALF])
            rem = sb("rem", [P, 2, HALF])
            part = sb("part", [P, 2, QK, 3, HALF], BF16)
            vt = sb("vt", [P, 2, HT, HEADS, 2 * HD])
            ptr = self.ps(ctx, T + "ptr", [P, 2, 512])
            pqk = self.ps(ctx, T + "pqk", [P, 2, 512])
            pax = self.ps(ctx, T + "pax", [P, 2, 512])
            pv = self.ps(ctx, T + "pv", [P, 2, 512])
            w_in, vt_set, sd_ready, rstd_ready, rn_ready = (sem(n) for n in ("w_in", "vt_set", "sd_ready", "rstd_ready", "rn_ready"))
            ln, modc = sem("ln"), sem("modc")
            xn_ready, tr_done, h_ready, qk_done, v_done = (sem(n) for n in ("xn_ready", "tr_done", "h_ready", "qk_done", "v_done"))
            u_ready, sq_ready, aux_done, post, un_ready = (sem(n) for n in ("u_ready", "sq_ready", "aux_done", "post", "un_ready"))
            hi_ready, rem_ready, mid_ready, lo_ready, v_ready = (sem(n) for n in ("hi_ready", "rem_ready", "mid_ready", "lo_ready", "v_ready"))
            part_out = [sem("part_out0"), sem("part_out1")]
            v_out = [sem("v_out0"), sem("v_out1")]
            stats_seen = sem("stats_seen")
            weights = 16 * (9 if not rope else 5)
            POST = 2 if rope else 3

            with nc.Block() as block:
                @block.sync
                def _(sp):
                    with nc.allow_non_contiguous_dma(reason="bias and norm columns"):
                        if rope:
                            sp.dma_start(w[:, :, :], d["L1_attn_Wqkv"].rearrange("(c p) n -> p c n", p=P)).then_inc(w_in, 16)
                            sp.dma_start(bias[:, :], d["L1_attn_bqkv"][0:2 * D].rearrange("(c p) -> p c", p=P)).then_inc(w_in, 16)
                            sp.dma_start(bv[:, :], d["L1_attn_bqkv"][2 * D:3 * D].partition_broadcast(P)).then_inc(w_in, 16)
                            sp.dma_start(cs[:, :, :], d["c_rope"]).then_inc(w_in, 16)
                            sp.dma_start(aux[:, :], d["c_swap"]).then_inc(w_in, 16)
                        else:
                            for j, n in enumerate("qkv"):
                                sp.dma_start(w[:, :, j * D:(j + 1) * D], d[f"L0_attn_w{n}_wT"].rearrange("(c p) n -> p c n", p=P)).then_inc(w_in, 16)
                            for j, n in enumerate("qk"):
                                sp.dma_start(bias[:, 2 * j:2 * j + 2], d[f"L0_attn_w{n}_b"].rearrange("(c p) -> p c", p=P)).then_inc(w_in, 16)
                            sp.dma_start(bv[:, :], d["L0_attn_wv_b"].partition_broadcast(P)).then_inc(w_in, 16)
                            sp.dma_start(nw[:, 0:1], d["qn_rep"].rearrange("(p a) -> p a", a=1)).then_inc(w_in, 16)
                            sp.dma_start(nw[:, 1:2], d["kn_rep"].rearrange("(p a) -> p a", a=1)).then_inc(w_in, 16)
                            sp.dma_start(aux[:, :], d["c_heads"]).then_inc(w_in, 16)
                    for half in range(2):
                        sp.sem_inc(v_out[half], 16)
                        sp.sem_inc(part_out[half], 16)
                    pd = self.parts_d[layer].rearrange("s (c p) n -> p c s n", p=P)
                    vd = self.v_d[layer].rearrange("(t p) n -> p t n", p=P)
                    with sp.Fori(0, B) as b:
                        for half in range(2):
                            n = 2 * b + half
                            sp.wait_ge(v_ready, HT * n + HT)
                            sp.dma_start(vd[:, bass.ds(n * HT, HT), :], vt[:, half, :, :, :].rearrange("p t h e -> p t (h e)")).then_inc(v_out[half], 16)
                            sp.wait_ge(lo_ready, QK * n + QK)
                            for ch in range(QK):
                                sp.dma_start(pd[:, ch, :, bass.ds(n * HALF, HALF)], part[:, half, ch, :, :]).then_inc(part_out[half], 16)
                    for half in range(2):
                        sp.wait_ge(v_out[half], 16 * B + 16)
                        sp.wait_ge(part_out[half], 16 * QK * B + 16)

                @block.gpsimd
                def _(pool):
                    pool.memset(vt[:, :, :, :, HD + 1:2 * HD], 0.0).then_inc(vt_set, 1)
                    pool.memset(vt[:, :, :, :, HD:HD + 1], 1.0).then_inc(vt_set, 1)
                    pool.memset(eps[:, :], EPS).then_inc(vt_set, 1)

                @block.vector
                def _(dve):
                    dve.wait_ge(w_in, weights)
                    dve.wait_ge(vt_set, 2)
                    with dve.Fori(0, B) as b:
                        for half in range(2):
                            n = 2 * b + half
                            xt = lambda t: self.x[:, bass.ds(TPB * b + HT * half + t, 1), :].rearrange("p a d -> p (a d)")
                            K = 2 * HT
                            for t in range(HT):
                                nc.vector.bn_stats(stats[:, t, :], xt(t)).then_inc(ln, 1)
                            dve.wait_ge(ln, K * n + HT)
                            dve.sem_inc(stats_seen, 1)
                            for t in range(HT):
                                nc.vector.bn_aggr(mv[:, t, :], stats[:, t, :]).then_inc(ln, 1)
                            dve.wait_ge(ln, K * n + 2 * HT)
                            dve.wait_ge(sd_ready, n + 1)
                            nc.vector.reciprocal(rstd[:, :], sd[:, :]).then_inc(rstd_ready, 1)
                            dve.wait_ge(rstd_ready, n + 1)
                            for t in range(HT):
                                nc.vector.tensor_scalar(xn[:, half, t, :], xt(t), mv[:, t, 0:1], rstd[:, t:t + 1], ALU.subtract, ALU.mult).then_inc(xn_ready, 1)
                            for t in range(HT):
                                dve.wait_ge(v_done, HT * n + t + 1)
                                if t == 0:
                                    dve.wait_ge(v_out[half], 16 * b + 16)
                                nc.vector.tensor_tensor(vt[:, half, t, :, 0:HD], pv[:, t % 2, 0:D].rearrange("p (h e) -> p h e", e=HD),
                                                        bv[:, :].rearrange("p (h e) -> p h e", e=HD), ALU.add).then_inc(v_ready, 1)
                                m = QK * n + t
                                ch, g = t, t % 2
                                if not rope:
                                    dve.wait_ge(qk_done, m + 1)
                                    nc.vector.tensor_scalar(un[:, g, :], pqk[:, g, :], bias[:, ch:ch + 1], 1e4, ALU.add, ALU.min).then_inc(post, 1)
                                    dve.wait_ge(post, POST * m + 1)
                                    nc.vector.tensor_scalar(u[:, g, :], un[:, g, :], -1e4, None, ALU.max).then_inc(u_ready, 1)
                                    dve.wait_ge(aux_done, m + 1)
                                    nc.vector.tensor_scalar(rn[:, g, :], pax[:, g, :], 1.0 / HD, EPS, ALU.mult, ALU.max).then_inc(post, 1)
                                    dve.wait_ge(rn_ready, m + 1)
                                    nc.vector.reciprocal(rn[:, g, :], rn[:, g, :]).then_inc(post, 1)
                                    dve.wait_ge(post, POST * m + 3)
                                    nc.vector.scalar_tensor_tensor(out=un[:, g, :], in0=u[:, g, :], scalar=nw[:, ch // 2:ch // 2 + 1], in1=rn[:, g, :],
                                                                   op0=ALU.mult, op1=ALU.mult).then_inc(un_ready, 1)
                                else:
                                    dve.wait_ge(u_ready, m + 1)
                                    nc.vector.tensor_tensor(sq[:, g, :], u[:, g, :], cs[:, 0, half * HALF:(half + 1) * HALF], ALU.mult).then_inc(post, 1)
                                    dve.wait_ge(aux_done, m + 1)
                                    nc.vector.tensor_tensor(rn[:, g, :], pax[:, g, :], cs[:, 1, half * HALF:(half + 1) * HALF], ALU.mult).then_inc(post, 1)
                                    dve.wait_ge(post, POST * m + 2)
                                    nc.vector.tensor_tensor(un[:, g, :], sq[:, g, :], rn[:, g, :], ALU.add).then_inc(un_ready, 1)
                                dve.wait_ge(hi_ready, m + 1)
                                nc.vector.tensor_tensor(rem[:, g, :], un[:, g, :], part[:, half, ch, 0, :], ALU.subtract).then_inc(rem_ready, 1)
                                dve.wait_ge(mid_ready, m + 1)
                                nc.vector.tensor_tensor(part[:, half, ch, 2, :], rem[:, g, :], part[:, half, ch, 1, :], ALU.subtract).then_inc(lo_ready, 1)

                @block.scalar
                def _(act):
                    act.wait_ge(w_in, weights)
                    act.wait_ge(vt_set, 3)
                    with act.Fori(0, B) as b:
                        for half in range(2):
                            n = 2 * b + half
                            if half == 0:
                                for j in range(2):
                                    nc.scalar.activation(modb[:, j, :], self.mod_col[:, layer, 2 * j:2 * j + 2, bass.ds(b, 1)].rearrange("p c a -> p (c a)"),
                                                         ACT.Copy).then_inc(modc, 1)
                                act.wait_ge(modc, 2 * b + 2)
                            act.wait_ge(ln, 2 * HT * n + 2 * HT)
                            nc.scalar.activation(sd[:, :], mv[:, :, 1], ACT.Sqrt, bias=eps[:, :]).then_inc(sd_ready, 1)
                            for t in range(HT):
                                act.wait_ge(tr_done, HT * n + t + 1)
                                for c in range(DC):
                                    a = nc.scalar.activation(hT[:, half, c, t * P:(t + 1) * P], ptr[:, t % 2, c * P:(c + 1) * P], ACT.Identity,
                                                             bias=modb[:, 0, c:c + 1], scale=modb[:, 1, c:c + 1])
                                a.then_inc(h_ready, 1)
                            for ch in range(QK):
                                m, g = QK * n + ch, ch % 2
                                if not rope:
                                    act.wait_ge(u_ready, m + 1)
                                    nc.scalar.activation(sq[:, g, :], u[:, g, :], ACT.Square).then_inc(sq_ready, 1)
                                    act.wait_ge(post, POST * m + 2)
                                    nc.scalar.activation(rn[:, g, :], rn[:, g, :], ACT.Sqrt, bias=eps[:, :]).then_inc(rn_ready, 1)
                                else:
                                    act.wait_ge(qk_done, m + 1)
                                    nc.scalar.activation(u[:, g, :], pqk[:, g, :], ACT.Identity, bias=bias[:, ch:ch + 1]).then_inc(u_ready, 1)
                                act.wait_ge(un_ready, m + 1)
                                if ch == 0:
                                    act.wait_ge(part_out[half], 16 * QK * b + 16)
                                nc.scalar.activation(part[:, half, ch, 0, :], un[:, g, :], ACT.Copy).then_inc(hi_ready, 1)
                                act.wait_ge(rem_ready, m + 1)
                                nc.scalar.activation(part[:, half, ch, 1, :], rem[:, g, :], ACT.Copy).then_inc(mid_ready, 1)

                @block.tensor
                def _(pe):
                    pe.wait_ge(w_in, weights)
                    with pe.Fori(0, B) as b:
                        for half in range(2):
                            n = 2 * b + half
                            for t in range(HT):
                                pe.wait_ge(xn_ready, HT * n + t + 1)
                                if t >= 2:
                                    pe.wait_ge(h_ready, HT * n + t - 1)
                                for c in range(DC):
                                    tr = nc.tensor.transpose(ptr[:, t % 2, c * P:(c + 1) * P], xn[:, half, t, c * P:(c + 1) * P], self.ident[:, :])
                                tr.then_inc(tr_done, 1)
                            pe.wait_ge(h_ready, HT * n + HT)
                            for t in range(HT):
                                ch, g = t, t % 2
                                m = QK * n + ch
                                if t >= 2:
                                    pe.wait_ge(un_ready, m - 1)
                                for c in range(DC):
                                    mm = nc.tensor.matmul(pqk[:, g, :], w[:, c, ch * P:(ch + 1) * P], hT[:, half, c, :], start=(c == 0), stop=(c == DC - 1))
                                mm.then_inc(qk_done, 1)
                                if t >= 2:
                                    pe.wait_ge(v_ready, HT * n + t - 1)
                                for c in range(DC):
                                    mm = nc.tensor.matmul(pv[:, t % 2, 0:D], hT[:, half, c, t * P:(t + 1) * P], w[:, c, 2 * D:3 * D], start=(c == 0), stop=(c == DC - 1))
                                mm.then_inc(v_done, 1)
                                if not rope:
                                    pe.wait_ge(sq_ready, m + 1)
                                    nc.tensor.matmul(pax[:, g, :], aux[:, :], sq[:, g, :], start=True, stop=True).then_inc(aux_done, 1)
                                else:
                                    pe.wait_ge(u_ready, m + 1)
                                    nc.tensor.matmul(pax[:, g, :], aux[:, :], u[:, g, :], start=True, stop=True).then_inc(aux_done, 1)

    def max_units(self, layer):
        out = []
        for i in range(TPB):
            if layer == 0:
                ks = list(range(max(0, i - 1), i + 1))
                for h0 in range(0, HG, 4 // len(ks)):
                    out.append((i, range(h0, h0 + 4 // len(ks)), ks, 0))
            else:
                n = i + 1
                per = 4 if n == 1 else 2 if n == 2 else 1
                for h0 in range(0, HG, per):
                    out.append((i, range(h0, h0 + per), list(range(0, min(n, 4))), 0))
                    if n > 4:
                        out.append((i, range(h0, h0 + per), list(range(4, n)), 1))
        return out

    def exp_units(self, layer):
        out = []
        for c in range(2):
            unit = []
            for j in range(TPB):
                lo, hi = j, (TPB if layer else j + 2)
                lo, hi = max(lo, 4 * c), min(hi, 4 * c + 4)
                if lo < hi:
                    unit.append((j, (lo - 4 * c) * P, (hi - 4 * c) * P))
            out.append(unit)
        return out

    def attend(self, layer):
        nc = self.nc
        with ExitStack() as ctx:
            T = f"a{layer}_"
            sb = lambda n, s, t=F32: self.sb(ctx, T + n, s, t)
            sem = lambda n: self.sem(ctx, T + n)
            Ks = [sb(f"Ks{i}", [KAUG, HG, L], BF16) for i in range(2)]
            Qs = [sb(f"Qs{i}", [KAUG, HG, L], BF16) for i in range(2)]
            V4 = [sb(f"V4{i}", [P, TPB, HG, 2 * HD]) for i in range(2)]
            NP = 4
            probs = sb("probs", [P, NP, 2, HALF])
            mx = sb("mx", [P, 2, HG, TPB])
            nm = sb("nm", [P, HG * TPB])
            nmr = sb("nmr", [HG * TPB, P])
            nmp = sb("nmp", [HG * TPB, 3, P], BF16)
            oT = sb("oT", [P, HALF])
            rden = sb("rden", [P, 4, HG])
            pst = self.ps(ctx, T + "pst", [P, 4, 512])
            pmx = self.ps(ctx, T + "pmx", [P, 2, 512])
            pacc = self.ps(ctx, T + "pacc", [P, 512])
            pms = self.ps(ctx, T + "pms", [P, 512])
            ones_set = sem("ones_set")
            kq_in = [sem("kq_in0"), sem("kq_in1")]
            max_in = [sem("max_in0"), sem("max_in1")]
            s_done, m_done, nm_ch, nm_ready, nmT_done, nmp_ready = (sem(n) for n in ("s_done", "m_done", "nm_ch", "nm_ready", "nmT_done", "nmp_ready"))
            st_done, exp_done, pv_done, acc_out, oT_done, norm_ch, norm_done = (sem(n) for n in ("st_done", "exp_done", "pv_done", "acc_out", "oT_done", "norm_ch", "norm_done"))
            nm_mid = sem("nm_mid")
            maxu = self.max_units(layer)
            NM = len(maxu)
            halves = self.exp_units(layer)
            expu = [(c, k, j, q0, q1, pr) for c in range(2) for k, (j, q0, q1) in enumerate(halves[c]) for pr in range(2)]
            NE = len(expu)
            NV = NE // 2
            mask = self.causal if layer else self.window
            loads = 2 * SLOTS + 1
            SLOT_Q, SLOT_K = (0, 0, 0, 1, 1, 2), (0, 1, 2, 0, 1, 0)

            def load(sp, par, b, hg):
                pd = self.parts_d[layer]
                row = lambda base: bass.ds(hg * (HG * HD) + base, HG * HD)
                for dst, base, slots in ((Qs[par], 0, SLOT_Q), (Ks[par], D, SLOT_K)):
                    for s, part in enumerate(slots):
                        src = pd[part, row(base), bass.ds(b * L, L)].rearrange("(g e) n -> e g n", e=HD)
                        sp.dma_start(dst[s * HD:(s + 1) * HD, :, :], src).then_inc(kq_in[par], 16)
                vsrc = self.v_d[layer][bass.ds(b * L, L), bass.ds(hg * (HG * 2 * HD), HG * 2 * HD)].rearrange("(t p) n -> p t n", p=P)
                sp.dma_start(V4[par][:, :, :, :].rearrange("p t h e -> p t (h e)"), vsrc).then_inc(kq_in[par], 16)

            def send_max(sp, par, s):
                sp.wait_ge(nmp_ready, s + 1)
                for p in range(3):
                    sp.dma_start(Qs[par][KROWS + p:KROWS + p + 1, :, :].rearrange("a h (i q) -> a (h i) q", q=P), nmp[:, p, :]).then_inc(max_in[par], 16)

            def pe_max(pe, par, s, u):
                i, hs, ks, part = maxu[u]
                if u >= 2:
                    pe.wait_ge(m_done, NM * s + u - 1)
                cols = len(ks) * P
                for n, h in enumerate(hs):
                    o = n * cols
                    diag = i in ks
                    mm = nc.tensor.matmul(pmx[:, u % 2, o:o + cols], Qs[par][0:KROWS, h, i * P:(i + 1) * P],
                                          Ks[par][0:KROWS, h, ks[0] * P:ks[0] * P + cols], start=True, stop=not diag, skip_group_check=True)
                    if diag and layer:
                        mm = nc.tensor.matmul(pmx[:, u % 2, o + cols - P:o + cols], self.ident_bf[:, :], mask[:, 0, :], start=False, stop=True, skip_group_check=True)
                    elif diag:
                        mm = nc.tensor.matmul(pmx[:, u % 2, o:o + cols], self.ident_bf[:, :], mask[:, 0, 2 * P - cols:2 * P], start=False, stop=True, skip_group_check=True)
                mm.then_inc(s_done, 1)

            def pe_nmT(pe, s):
                pe.wait_ge(nm_ready, s + 1)
                nc.tensor.transpose(pms[0:HG * TPB, 0:P], nm[:, :], self.ident[:, :]).then_inc(nmT_done, 1)

            def pe_st(pe, par, s, u):
                c, k, j, q0, q1, pr = expu[u]
                if u >= 2:
                    pe.wait_ge(exp_done, NE * s + u - 1)
                for hh in range(2):
                    h = 2 * pr + hh
                    out = pst[:, 2 * (u % 2) + hh, :]
                    g0, g1 = c * HALF + q0, c * HALF + q1
                    diag = j * P - c * HALF if layer else q0
                    masked = (0 <= diag) if layer else True
                    mm = nc.tensor.matmul(out[:, q0:q1], Ks[par][:, h, j * P:(j + 1) * P], Qs[par][:, h, g0:g1], start=True, stop=not masked, skip_group_check=True)
                    if masked and layer:
                        mm = nc.tensor.matmul(out[:, diag:diag + P], self.ident_bf[:, :], mask[:, 1, :], start=False, stop=True, skip_group_check=True)
                    elif masked:
                        m0 = g0 - j * P
                        mm = nc.tensor.matmul(out[:, q0:q1], self.ident_bf[:, :], mask[:, 1, m0:m0 + q1 - q0], start=False, stop=True, skip_group_check=True)
                mm.then_inc(st_done, 1)

            def pe_pv(pe, par, s, v):
                c, k, j, q0, q1, _ = expu[2 * v]
                pe.wait_ge(exp_done, NE * s + 2 * v + 2)
                if k == 0 and v > 0:
                    pe.wait_ge(acc_out, 2 * s + 1)
                for h in range(HG):
                    mm = nc.tensor.matmul(pacc[32 * h:32 * h + 32, q0:q1], V4[par][:, j, h, :], probs[:, (2 * v + h // 2) % NP, h % 2, q0:q1],
                                          start=(k == 0), stop=(k == len(halves[c]) - 1), skip_group_check=True)
                mm.then_inc(pv_done, 1)

            def pe_oT(pe, s, c):
                pe.wait_ge(acc_out, 2 * s + c + 1)
                for t in range(4):
                    tr = nc.tensor.transpose(pms[:, t * P:(t + 1) * P], oT[:, t * P:(t + 1) * P], self.ident[:, :])
                tr.then_inc(oT_done, 1)

            def pe_body(pe, par, s, maxes):
                seq = []
                for v in range(NV):
                    seq += [(pe_st, 2 * v), (pe_st, 2 * v + 1)]
                    if v:
                        seq.append((pe_pv, v - 1))
                    if v == len(halves[0]) + 1:
                        seq.append((pe_oT, 0))
                seq.append((pe_pv, NV - 1))
                m = 0
                for n, (stage, a) in enumerate(seq):
                    if stage is pe_oT:
                        pe_oT(pe, s, a)
                    else:
                        stage(pe, par, s, a)
                    while maxes and m < (n + 1) * NM // len(seq):
                        pe_max(pe, 1 - par, s + 1, m)
                        m += 1
                pe.wait_ge(norm_done, 2 * s + 1)
                pe_oT(pe, s, 1)
                if maxes:
                    pe.wait_ge(norm_done, 2 * s + 2)
                    pe_nmT(pe, s + 1)

            def dve_max(dve, s, u):
                i, hs, ks, part = maxu[u]
                dve.wait_ge(s_done, NM * s + u + 1)
                cols = len(ks) * P
                src = pmx[:, u % 2, 0:len(hs) * cols].rearrange("p (h n) -> p h n", n=cols)
                nc.vector.tensor_reduce(mx[:, part, hs[0]:hs[0] + len(hs), i], src, AX.X, ALU.max).then_inc(m_done, 1)

            def dve_nm(dve, s):
                dve.wait_ge(m_done, NM * s + NM)
                if layer:
                    nc.vector.tensor_tensor(mx[:, 0, :, 4:8], mx[:, 0, :, 4:8], mx[:, 1, :, 4:8], ALU.max).then_inc(nm_ch, 1)
                    dve.wait_ge(nm_ch, 3 * s + 1)
                c0 = 3 * s + 1 if layer else 2 * s
                nc.vector.tensor_scalar(nm[:, :], mx[:, 0, :, :].rearrange("p h i -> p (h i)"), -1.0, None, ALU.mult).then_inc(nm_ready, 1)
                dve.wait_ge(nmT_done, s + 1)
                src = pms[0:HG * TPB, 0:P]
                nc.vector.tensor_copy(nmp[:, 0, :], src).then_inc(nm_ch, 1)
                dve.wait_ge(nm_ch, c0 + 1)
                nc.vector.tensor_tensor(nmr[:, :], src, nmp[:, 0, :], ALU.subtract).then_inc(nm_ch, 1)
                dve.wait_ge(nm_ch, c0 + 2)
                nc.vector.tensor_copy(nmp[:, 1, :], nmr[:, :]).then_inc(nm_mid, 1)
                dve.wait_ge(nm_mid, s + 1)
                nc.vector.tensor_tensor(nmp[:, 2, :], nmr[:, :], nmp[:, 1, :], ALU.subtract).then_inc(nmp_ready, 1)

            def dve_norm(dve, s, c, tile, col):
                dve.wait_ge(oT_done, 2 * s + c + 1)
                src = pms[:, :].rearrange("p (t h e) -> p t h e", t=4, e=2 * HD)
                nc.vector.reciprocal(rden[:, :, :], src[:, :, :, HD]).then_inc(norm_ch, 1)
                dve.wait_ge(norm_ch, 2 * s + c + 1)
                dst = self.attn[:, bass.ds(tile, 4), bass.ds(col, HG * HD)].rearrange("p t (h e) -> p t h e", e=HD)
                nc.vector.tensor_tensor(dst, src[:, :, :, 0:HD], rden[:, :, :].unsqueeze(3).broadcast_to([P, 4, HG, HD]), ALU.mult).then_inc(norm_done, 1)

            def dve_step(dve, s, tile, col, maxes, exps):
                for u in range(NM if maxes else 0):
                    if exps and u == (NM * (len(halves[0]) + 3)) // NV:
                        dve_norm(dve, s, 0, tile, col)
                    dve_max(dve, s + 1, u)
                if exps:
                    if not maxes:
                        dve_norm(dve, s, 0, tile, col)
                    dve_norm(dve, s, 1, tile + 4, col)
                if maxes:
                    dve_nm(dve, s + 1)

            def act_step(act, s):
                for u, (c, k, j, q0, q1, pr) in enumerate(expu):
                    act.wait_ge(st_done, NE * s + u + 1)
                    if u >= NP:
                        act.wait_ge(pv_done, NV * s + (u - NP) // 2 + 1)
                    bank = 2 * (u % 2)
                    nc.scalar.activation(probs[:, u % NP, :, q0:q1], pst[:, bank:bank + 2, q0:q1], ACT.Exp, scale=HD ** -0.5).then_inc(exp_done, 1)
                    if u in (2 * len(halves[0]) + 1, NE - 1):
                        c_ = 0 if u < NE - 1 else 1
                        act.wait_ge(pv_done, NV * s + (len(halves[0]) if c_ == 0 else NV))
                        nc.scalar.activation(oT[:, :], pacc[:, :], ACT.Copy).then_inc(acc_out, 1)

            with nc.Block() as block:
                @block.gpsimd
                def _(pool):
                    for i in range(2):
                        pool.memset(Ks[i][KROWS:KAUG, :, :], 1.0).then_inc(ones_set, 1)

                TURNS = STEPS // 2

                @block.sync
                def _(sp):
                    load(sp, 0, 0, 0)
                    load(sp, 1, 0, 1)
                    send_max(sp, 0, 0)
                    with sp.Fori(0, TURNS - 1) as r:
                        for par in range(2):
                            s = 2 * r + par
                            send_max(sp, 1 - par, s + 1)
                            sp.wait_ge(pv_done, NV * s + NV)
                            s2 = 2 * r + par + 2
                            load(sp, par, s2 // HG, s2 % HG)
                    send_max(sp, 1, STEPS - 1)

                @block.tensor
                def _(pe):
                    pe.wait_ge(ones_set, 2)
                    pe.wait_ge(kq_in[0], 16 * loads)
                    for u in range(NM):
                        pe_max(pe, 0, 0, u)
                    pe_nmT(pe, 0)
                    with pe.Fori(0, TURNS - 1) as r:
                        for par in range(2):
                            s = 2 * r + par
                            pe.wait_ge(max_in[par], 48 * r + 48)
                            pe.wait_ge(kq_in[1 - par], 16 * loads * (r + par) + 16 * loads)
                            pe_body(pe, par, s, True)
                    r = TURNS - 1
                    pe.wait_ge(max_in[0], 48 * r + 48)
                    pe.wait_ge(kq_in[1], 16 * loads * r + 16 * loads)
                    pe_body(pe, 0, STEPS - 2, True)
                    pe.wait_ge(max_in[1], 48 * r + 48)
                    pe_body(pe, 1, STEPS - 1, False)

                @block.vector
                def _(dve):
                    for u in range(NM):
                        dve_max(dve, 0, u)
                    dve_nm(dve, 0)
                    with dve.Fori(0, TURNS - 1) as r:
                        for par in range(2):
                            s = 2 * r + par
                            dve_step(dve, s, (s // HG) * TPB, (s % HG) * (HG * HD), True, True)
                    for s in (STEPS - 2, STEPS - 1):
                        dve_step(dve, s, (s // HG) * TPB, (s % HG) * (HG * HD), s < STEPS - 1, True)

                @block.scalar
                def _(act):
                    with act.Fori(0, STEPS) as s:
                        act_step(act, s)

    def out_project(self, layer):
        nc, d = self.nc, self.dram
        with ExitStack() as ctx:
            T = f"o{layer}_"
            sb = lambda n, s, t=F32: self.sb(ctx, T + n, s, t)
            sem = lambda n: self.sem(ctx, T + n)
            wo = sb("wo", [P, DC, D])
            bo = sb("bo", [P, D])
            at = sb("at", [P, 2, D])
            aT = sb("aT", [P, 2, DC, P])
            y = sb("y", [P, 2, D])
            gate = sb("gate", [P, B, D])
            ptr = self.ps(ctx, T + "ptr", [P, 2, 512])
            py = self.ps(ctx, T + "py", [P, 2, 512])
            w_in, copied, tr_done, aT_ready, y_done, y_ch, x_done = (sem(n) for n in ("w_in", "copied", "tr_done", "aT_ready", "y_done", "y_ch", "x_done"))
            wname, bname = ("L0_attn_wo_wT", "L0_attn_wo_b") if layer == 0 else ("L1_attn_Wproj", "L1_attn_bproj")
            with nc.Block() as block:
                @block.sync
                def _(sp):
                    sp.dma_start(wo[:, :, :], d[wname].rearrange("(c p) n -> p c n", p=P)).then_inc(w_in, 16)
                    sp.dma_start(bo[:, :], d[bname].partition_broadcast(P)).then_inc(w_in, 16)
                    sp.dma_start(gate[:, :, :], self.mod_d[:, layer, 0, :, :]).then_inc(w_in, 16)

                @block.scalar
                def _(act):
                    with act.Fori(0, TILES // 2) as r:
                        for par in range(2):
                            t = 2 * r + par
                            nc.scalar.activation(at[:, par, :], self.attn[:, bass.ds(t, 1), :].rearrange("p a d -> p (a d)"), ACT.Copy).then_inc(copied, 1)
                            act.wait_ge(tr_done, t + 1)
                            nc.scalar.activation(aT[:, par, :, :].rearrange("p c n -> p (c n)"), ptr[:, par, 0:D], ACT.Copy).then_inc(aT_ready, 1)

                @block.tensor
                def _(pe):
                    pe.wait_ge(w_in, 48)
                    with pe.Fori(0, TILES // 2) as r:
                        for par in range(2):
                            t = 2 * r + par
                            pe.wait_ge(copied, t + 1)
                            for c in range(DC):
                                tr = nc.tensor.transpose(ptr[:, par, c * P:(c + 1) * P], at[:, par, c * P:(c + 1) * P], self.ident[:, :])
                            tr.then_inc(tr_done, 1)
                            pe.wait_ge(aT_ready, t + 1)
                            pe.wait_ge(x_done, t + 1)
                            for c in range(DC):
                                mm = nc.tensor.matmul(py[:, par, 0:D], aT[:, par, c, :], wo[:, c, :], start=(c == 0), stop=(c == DC - 1))
                            mm.then_inc(y_done, 1)

                @block.vector
                def _(dve):
                    dve.wait_ge(w_in, 48)
                    dve.sem_inc(x_done, 2)
                    with dve.Fori(0, B) as b:
                        with dve.Fori(0, TPB // 2) as r:
                            for par in range(2):
                                t = b * TPB + 2 * r + par
                                dve.wait_ge(y_done, t + 1)
                                nc.vector.tensor_tensor(y[:, par, :], py[:, par, 0:D], bo[:, :], ALU.add).then_inc(y_ch, 1)
                                dve.wait_ge(y_ch, 2 * t + 1)
                                ga = gate[:, bass.ds(b, 1), :].rearrange("p a d -> p (a d)")
                                nc.vector.tensor_tensor(y[:, par, :], y[:, par, :], ga, ALU.mult).then_inc(y_ch, 1)
                                dve.wait_ge(y_ch, 2 * t + 2)
                                xt = self.x[:, bass.ds(t, 1), :].rearrange("p a d -> p (a d)")
                                nc.vector.tensor_tensor(xt, xt, y[:, par, :], ALU.add).then_inc(x_done, 1)

    def moe(self, layer):
        nc = self.nc
        with ExitStack() as ctx:
            T = f"m{layer}_"
            self.T = T
            self.H = 1024 if layer == 0 else 512
            self.NH = self.H // P
            NH = self.NH
            self.w1 = self.sb(ctx, T + "w1", [P, EXPERTS, DC, 2, self.H], F16)
            self.w2 = self.sb(ctx, T + "w2", [P, EXPERTS, NH, 2, D], F16)
            self.s1 = self.sb(ctx, T + "s1", [P, EXPERTS, NH])
            self.b1 = self.sb(ctx, T + "b1", [P, EXPERTS, NH])
            self.gw = self.sb(ctx, T + "gw", [P, DC, EXPERTS])
            self.gs = self.sb(ctx, T + "gs", [P, EXPERTS])
            self.gb = self.sb(ctx, T + "gb", [P, EXPERTS])
            self.slot = self.sb(ctx, T + "slot", [P, 2, TILES], U32)
            self.wt = self.sb(ctx, T + "wt", [P, 2, TILES])
            self.owner = self.sb(ctx, T + "owner", [P, XT], I32)
            self.xs_d = nc.dram_tensor(T + "xs_d", (XT * ROWS, 2 * D), F16, kind="Internal").ap()
            self.ys_d = nc.dram_tensor(T + "ys_d", (XT * ROWS, D), F32, kind="Internal").ap()
            self.moe_weights(layer)
            with ExitStack() as inner:
                self.zh = self.sb(inner, T + "zh", [P, TILES, 2, D], F16)
                self.lg = self.sb(inner, T + "lg", [P, TILES, EXPERTS])
                self.moe_input(layer)
                self.moe_route(layer)
                self.moe_scatter(layer)
            self.moe_tiles(layer)
            self.moe_combine(layer)

    def moe_weights(self, layer):
        nc, d, T, H, NH = self.nc, self.dram, self.T, self.H, self.NH
        normed = layer == 0
        w1_src = d["L0_w1T"] if normed else d["L1_ffn_W1"]
        w2_src = d["L0_w2T"] if normed else d["L1_ffn_W2"]
        with ExitStack() as ctx:
            sb = lambda n, s, t=F32: self.sb(ctx, T + n, s, t)
            sem = lambda n: self.sem(ctx, T + n)
            st1 = sb("st1", [P, DC, H])
            st2 = sb("st2", [P, NH, D])
            sq = sb("sq", [P, 2048])
            rt = sb("rt", [P, D])
            g2 = sb("g2", [P, D])
            ones = sb("ones", [P, P])
            g1 = sb("g1", [P, EXPERTS, NH])
            gg = sb("gg", [P, EXPERTS])
            zero = sb("zero", [P, 2 * D], F16)
            pss = self.ps(ctx, T + "pss", [P, 512])
            pbc = self.ps(ctx, T + "pbc", [P, 512])
            pgs = self.ps(ctx, T + "pgs", [P, 512])
            small_in, w1_in, w2_in, g2_in, ones_set = (sem(n) for n in ("small_in", "w1_in", "w2_in", "g2_in", "ones_set"))
            sq1, ss1, sq2, ss2, root, w2_scaled, hi1, lo1, hi2, lo2, ch, gsq, gss, groot, zeroed = (
                sem(n) for n in ("sq1", "ss1", "sq2", "ss2", "root", "w2_scaled", "hi1", "lo1", "hi2", "lo2", "wch", "gsq", "gss", "groot", "zeroed"))
            zero_out, sqrt1_done = self.zero_out, sem("sqrt1_done")
            smalls = 16 * (5 if normed else 3)
            with nc.Block() as block:
                @block.sync
                def _(sp):
                    sp.dma_start(self.b1[:, :, :], d[f"L{layer}_b1c"]).then_inc(small_in, 16)
                    sp.dma_start(self.gw[:, :, :], d["L0_gateT" if normed else "L1_ffn_rW"].rearrange("(c p) e -> p c e", p=P)).then_inc(small_in, 16)
                    sp.dma_start(self.gb[:, :], d["L0_ffn_gate_b" if normed else "L1_ffn_rb"].partition_broadcast(P)).then_inc(small_in, 16)
                    if normed:
                        sp.dma_start(g1[:, :, :], d["L0_g1c"]).then_inc(small_in, 16)
                        sp.dma_start(gg[:, :], d["L0_ffn_gate_g"].partition_broadcast(P)).then_inc(small_in, 16)
                    sp.sem_inc(lo1, 1)
                    sp.sem_inc(lo2, 1)
                    with sp.Fori(0, EXPERTS) as e:
                        sp.wait_ge(lo1, e + 1)
                        sp.dma_start(st1[:, :, :], w1_src[bass.ds(e, 1), :, :].rearrange("a (c p) n -> p (a c) n", p=P)).then_inc(w1_in, 16)
                        sp.wait_ge(lo2, e + 1)
                        sp.dma_start(st2[:, :, :], w2_src[bass.ds(e, 1), :, :].rearrange("a (c p) n -> p (a c) n", p=P)).then_inc(w2_in, 16)
                        if normed:
                            sp.dma_start(g2[:, :], d["L0_ffn_w2_g"][bass.ds(e, 1), :].rearrange("a n -> (a n)").partition_broadcast(P)).then_inc(g2_in, 16)

                @block.gpsimd
                def _(pool):
                    pool.memset(ones[:, :], 1.0).then_inc(ones_set, 1)
                    pool.memset(zero[:, :], 0.0).then_inc(zeroed, 1)
                    pool.wait_ge(zeroed, 1)
                    A = 16
                    for j in range(XT * ROWS // (A * P)):
                        dst = self.xs_d[j * A * P:(j + 1) * A * P, :].rearrange("(a p) n -> p a n", p=P)
                        pool.dma_start(dst, zero[:, :].unsqueeze(1).broadcast_to([P, A, 2 * D])).then_inc(zero_out, 16)
                    pool.wait_ge(zero_out, 16 * (XT * ROWS // (A * P)) * (layer + 1))

                @block.scalar
                def _(act):
                    if normed:
                        act.wait_ge(small_in, smalls)
                        nc.scalar.activation(sq[:, 0:DC * EXPERTS], self.gw[:, :, :].rearrange("p c e -> p (c e)"), ACT.Square).then_inc(gsq, 1)
                        act.wait_ge(gss, 1)
                        nc.scalar.activation(self.gs[:, :], pgs[:, 0:EXPERTS], ACT.Sqrt).then_inc(groot, 1)
                    with act.Fori(0, EXPERTS) as e:
                        act.wait_ge(w1_in, 16 * e + 16)
                        if normed:
                            nc.scalar.activation(sq[:, :], st1[:, :, :].rearrange("p c n -> p (c n)"), ACT.Square).then_inc(sq1, 1)
                        nc.scalar.activation(self.w1[:, bass.ds(e, 1), :, 0, :].rearrange("p a c n -> p (a c) n"), st1[:, :, :], ACT.Copy).then_inc(hi1, 1)
                        act.wait_ge(w2_in, 16 * e + 16)
                        if normed:
                            act.wait_ge(ss1, e + 1)
                            nc.scalar.activation(sq[:, :], st2[:, :, :].rearrange("p c n -> p (c n)"), ACT.Square).then_inc(sq2, 1)
                            act.wait_ge(ss2, e + 1)
                            nc.scalar.activation(rt[:, :], pbc[:, 0:D], ACT.Sqrt).then_inc(root, 1)
                            act.wait_ge(w2_scaled, e + 1)
                        nc.scalar.activation(self.w2[:, bass.ds(e, 1), :, 0, :].rearrange("p a c n -> p (a c) n"), st2[:, :, :], ACT.Copy).then_inc(hi2, 1)
                    if normed:
                        act.wait_ge(ss1, EXPERTS)
                        nc.scalar.activation(self.s1[:, :, :].rearrange("p e m -> p (e m)"), pss[:, 0:EXPERTS * NH], ACT.Sqrt).then_inc(sqrt1_done, 1)

                @block.tensor
                def _(pe):
                    if not normed:
                        return
                    pe.wait_ge(ones_set, 1)
                    pe.wait_ge(gsq, 1)
                    for c in range(DC):
                        mm = nc.tensor.matmul(pgs[:, 0:EXPERTS], ones[:, :], sq[:, c * EXPERTS:(c + 1) * EXPERTS], start=(c == 0), stop=(c == DC - 1))
                    mm.then_inc(gss, 1)
                    with pe.Fori(0, EXPERTS) as e:
                        pe.wait_ge(sq1, e + 1)
                        for m in range(NH):
                            for c in range(DC):
                                mm = nc.tensor.matmul(pss[:, bass.ds(e * NH + m, 1)], sq[:, c * H + m * P:c * H + m * P + P], ones[:, 0:1],
                                                      start=(c == 0), stop=(c == DC - 1), skip_group_check=True)
                        mm.then_inc(ss1, 1)
                        pe.wait_ge(sq2, e + 1)
                        for m in range(NH):
                            mm = nc.tensor.matmul(pbc[:, 0:D], ones[:, :], sq[:, m * D:(m + 1) * D], start=(m == 0), stop=(m == NH - 1))
                        mm.then_inc(ss2, 1)

                @block.vector
                def _(dve):
                    n = [0]

                    def link(ins):
                        n[0] += 1
                        ins.then_inc(ch, 1)
                        dve.wait_ge(ch, n[0])

                    dve.wait_ge(small_in, smalls)
                    if normed:
                        dve.wait_ge(groot, 1)
                        link(nc.vector.tensor_scalar(self.gs[:, :], self.gs[:, :], 1e-12, None, ALU.max))
                        link(nc.vector.reciprocal(self.gs[:, :], self.gs[:, :]))
                        link(nc.vector.tensor_tensor(self.gs[:, :], self.gs[:, :], gg[:, :], ALU.mult))
                    n0 = n[0]
                    with dve.Fori(0, EXPERTS) as e:
                        dve.wait_ge(hi1, e + 1)
                        w1e = lambda w: self.w1[:, bass.ds(e, 1), :, w, :].rearrange("p a c n -> p (a c) n")
                        w2e = lambda w: self.w2[:, bass.ds(e, 1), :, w, :].rearrange("p a c n -> p (a c) n")
                        nc.vector.tensor_tensor(w1e(1), st1[:, :, :], w1e(0), ALU.subtract).then_inc(lo1, 1)
                        if normed:
                            dve.wait_ge(root, e + 1)
                            nc.vector.tensor_scalar(rt[:, :], rt[:, :], 1e-12, None, ALU.max).then_inc(ch, 1)
                            dve.wait_ge(ch, n0 + 3 * e + 1)
                            nc.vector.reciprocal(rt[:, :], rt[:, :]).then_inc(ch, 1)
                            dve.wait_ge(ch, n0 + 3 * e + 2)
                            dve.wait_ge(g2_in, 16 * e + 16)
                            nc.vector.tensor_tensor(rt[:, :], rt[:, :], g2[:, :], ALU.mult).then_inc(ch, 1)
                            dve.wait_ge(ch, n0 + 3 * e + 3)
                            nc.vector.tensor_tensor(st2[:, :, :], st2[:, :, :], rt[:, :].unsqueeze(1).broadcast_to([P, NH, D]), ALU.mult).then_inc(w2_scaled, 1)
                        dve.wait_ge(hi2, e + 1)
                        nc.vector.tensor_tensor(w2e(1), st2[:, :, :], w2e(0), ALU.subtract).then_inc(lo2, 1)
                    if normed:
                        n[0] += 3 * EXPERTS
                        dve.wait_ge(sqrt1_done, 1)
                        s1 = self.s1[:, :, :]
                        link(nc.vector.tensor_scalar(s1, s1, 1e-12, None, ALU.max))
                        link(nc.vector.reciprocal(s1, s1))
                        link(nc.vector.tensor_tensor(s1, s1, g1[:, :, :], ALU.mult))

    def moe_input(self, layer):
        nc, d, T = self.nc, self.dram, self.T
        twice = layer == 1
        with ExitStack() as ctx:
            sb = lambda n, s, t=F32: self.sb(ctx, T + n, s, t)
            sem = lambda n: self.sem(ctx, T + n)
            rows = sb("rows", [P, 3 if twice else 2, D])
            lnr = sb("lnr", [P, 2, D]) if twice else None
            stats = sb("stats", [P, HT, nc.vector.BN_STATS_DIM])
            mv = sb("mv", [P, HT, 2])
            sd = sb("sd", [P, HT])
            rstd = sb("rstd", [P, HT])
            eps = sb("eps", [P, 1])
            z = sb("z", [P, HT, D])
            zT = sb("zT", [P, 2, DC, P])
            lt = sb("lt", [P, HT, EXPERTS])
            gh = sb("gh", [P, HT, D]) if twice else None
            ptr = self.ps(ctx, T + "ptr", [P, 2, 512])
            plg = self.ps(ctx, T + "plg", [P, 512])
            rows_in, lnr_in, eps_set, ch, var_ready, sd_ready, z_ready, tr_done, zT_ready, lg_done, lg_out, hi_done, lo_done = (
                sem(n) for n in ("rows_in", "lnr_in", "eps_set", "ich", "var_ready", "sd_ready", "z_ready", "tr_done", "zT_ready", "lg_done", "lg_out", "hi_done", "lo_done"))
            stats_seen = sem("stats_seen")
            NORMS = 2 if twice else 1
            ROWS_IN = 48 if twice else 32
            K = 2 * (3 * HT + 1) + 5 if twice else 3 * HT + 1 + 2
            with nc.Block() as block:
                @block.gpsimd
                def _(pool):
                    pool.memset(eps[:, :], EPS).then_inc(eps_set, 1)

                @block.sync
                def _(sp):
                    if twice:
                        sp.dma_start(lnr[:, 0, :], d["L1_ffn_ln_g"].partition_broadcast(P)).then_inc(lnr_in, 16)
                        sp.dma_start(lnr[:, 1, :], d["L1_ffn_ln_b"].partition_broadcast(P)).then_inc(lnr_in, 16)
                    sp.sem_inc(lo_done, 1)
                    with sp.Fori(0, B) as b:
                        sp.wait_ge(lo_done, 2 * b + 1)
                        for j, kind in enumerate((2, 3, 1) if twice else (2, 3)):
                            sp.dma_start(rows[:, j, :], self.mod_d[:, layer, kind, bass.ds(b, 1), :].rearrange("p a d -> p (a d)")).then_inc(rows_in, 16)

                @block.scalar
                def _(act):
                    act.wait_ge(eps_set, 1)
                    with act.Fori(0, 2 * B) as n:
                        for k in range(NORMS):
                            act.wait_ge(var_ready, NORMS * n + k + 1)
                            nc.scalar.activation(sd[:, :], mv[:, :, 1], ACT.Sqrt, bias=eps[:, :]).then_inc(sd_ready, 1)
                        act.wait_ge(z_ready, n + 1)
                        nc.scalar.activation(self.zh[:, bass.ds(HT * n, HT), 0, :], z[:, :, :], ACT.Copy).then_inc(hi_done, 1)
                        for t in range(HT):
                            act.wait_ge(tr_done, HT * n + t + 1)
                            nc.scalar.activation(zT[:, t % 2, :, :], ptr[:, t % 2, 0:D].rearrange("p (c n) -> p c n", c=DC), ACT.Copy).then_inc(zT_ready, 1)

                @block.tensor
                def _(pe):
                    with pe.Fori(0, 2 * B) as n:
                        pe.wait_ge(z_ready, n + 1)
                        for t in range(HT + 1):
                            if t < HT:
                                for c in range(DC):
                                    tr = nc.tensor.transpose(ptr[:, t % 2, c * P:(c + 1) * P], z[:, t, c * P:(c + 1) * P], self.ident[:, :])
                                tr.then_inc(tr_done, 1)
                            if t >= 1:
                                pe.wait_ge(zT_ready, HT * n + t)
                                for c in range(DC):
                                    mm = nc.tensor.matmul(plg[:, (t - 1) * EXPERTS:t * EXPERTS], zT[:, (t - 1) % 2, c, :], self.gw[:, c, :],
                                                          start=(c == 0), stop=(c == DC - 1), skip_group_check=True)
                        mm.then_inc(lg_done, 1)

                @block.vector
                def _(dve):
                    if twice:
                        dve.wait_ge(lnr_in, 32)
                    with dve.Fori(0, B) as b:
                        dve.wait_ge(rows_in, ROWS_IN * (b + 1))
                        for half in range(2):
                            n = 2 * b + half
                            cnt = [0]

                            def step(ins, wait=True):
                                cnt[0] += 1
                                ins.then_inc(ch, 1)
                                if wait:
                                    dve.wait_ge(ch, K * n + cnt[0])

                            xh = self.x[:, bass.ds(TPB * b + HT * half, HT), :]
                            row = lambda j, src=rows: src[:, j, :].unsqueeze(1).broadcast_to([P, HT, D])

                            def norm(k, src):
                                for t in range(HT):
                                    step(nc.vector.bn_stats(stats[:, t, :], src(t)), t == HT - 1)
                                dve.sem_inc(stats_seen, 1)
                                for t in range(HT):
                                    ins = nc.vector.bn_aggr(mv[:, t, :], stats[:, t, :])
                                    step(ins, t == HT - 1)
                                dve.sem_inc(var_ready, 1)
                                dve.wait_ge(sd_ready, NORMS * n + k + 1)
                                step(nc.vector.reciprocal(rstd[:, :], sd[:, :]))
                                for t in range(HT):
                                    step(nc.vector.tensor_scalar(z[:, t, :], src(t), mv[:, t, 0:1], rstd[:, t:t + 1], ALU.subtract, ALU.mult), t == HT - 1)

                            norm(0, lambda t: self.x[:, bass.ds(TPB * b + HT * half + t, 1), :].rearrange("p a d -> p (a d)"))
                            step(nc.vector.tensor_tensor(z[:, :, :], z[:, :, :], row(1), ALU.mult))
                            if not twice:
                                nc.vector.tensor_tensor(z[:, :, :], z[:, :, :], row(0), ALU.add).then_inc(z_ready, 1)
                                dve.wait_ge(z_ready, n + 1)
                            else:
                                step(nc.vector.tensor_tensor(z[:, :, :], z[:, :, :], row(0), ALU.add))
                                step(nc.vector.tensor_tensor(gh[:, :, :], z[:, :, :], row(2), ALU.mult))
                                step(nc.vector.tensor_tensor(xh, xh, gh[:, :, :], ALU.add))
                                norm(1, lambda t: z[:, t, :])
                                step(nc.vector.tensor_tensor(z[:, :, :], z[:, :, :], row(0, lnr), ALU.mult))
                                nc.vector.tensor_tensor(z[:, :, :], z[:, :, :], row(1, lnr), ALU.add).then_inc(z_ready, 1)
                                dve.wait_ge(z_ready, n + 1)
                            dve.wait_ge(hi_done, n + 1)
                            nc.vector.tensor_tensor(self.zh[:, bass.ds(TPB * b + HT * half, HT), 1, :], z[:, :, :],
                                                    self.zh[:, bass.ds(TPB * b + HT * half, HT), 0, :], ALU.subtract).then_inc(lo_done, 1)
                            dve.wait_ge(lg_done, n + 1)
                            out = self.lg[:, bass.ds(TPB * b + HT * half, HT), :]
                            src = plg[:, 0:HT * EXPERTS].rearrange("p (t e) -> p t e", e=EXPERTS)
                            erow = lambda a: a[:, :].unsqueeze(1).broadcast_to([P, HT, EXPERTS])
                            if not twice:
                                step(nc.vector.tensor_tensor(lt[:, :, :], src, erow(self.gs), ALU.mult))
                                nc.vector.tensor_tensor(out, lt[:, :, :], erow(self.gb), ALU.add).then_inc(lg_out, 1)
                            else:
                                nc.vector.tensor_tensor(out, src, erow(self.gb), ALU.add).then_inc(lg_out, 1)
                            assert cnt[0] == K

    def moe_route(self, layer):
        nc, d, T = self.nc, self.dram, self.T
        TE = TILES * EXPERTS
        with ExitStack() as ctx:
            sb = lambda n, s, t=F32: self.sb(ctx, T + n, s, t)
            sem = lambda n: self.sem(ctx, T + n)
            iota = sb("iota", [P, 64])
            low = sb("low", [P, P])
            ones = sb("rones", [P, TE])
            te = {n: sb("te_" + n, [P, TILES, EXPERTS]) for n in ("eq", "oh1", "oh2", "mask")}
            et = {n: sb("et_" + n, [P, EXPERTS, TILES]) for n in ("cnt", "sum", "slot")}
            best = sb("best", [P, 2, TILES])
            at = sb("at", [P, TILES])
            i99 = sb("i99", [P, EXPERTS])
            e8 = {n: sb("e8_" + n, [P, EXPERTS]) for n in ("prev", "n", "incl", "base")}
            M = N_TOK // ROWS
            work = sb("work", [P, max(TE, XT * (EXPERTS - 1))])
            te["tmp"] = work[:, 0:TE].rearrange("p (t e) -> p t e", e=EXPERTS)
            cmp16 = work[:, 0:EXPERTS * M].rearrange("p (e m) -> p e m", m=M)
            cmpj = work[:, 0:XT * (EXPERTS - 1)].rearrange("p (j e) -> p j e", e=EXPERTS - 1)
            thr = sb("thr", [P, N_TOK // ROWS])
            fl = sb("fl", [P, 2, TILES])
            oj = et["cnt"][:, :, :].rearrange("p e t -> p (e t)")[:, 0:XT]
            pw = self.ps(ctx, T + "pw", [P, 512])
            pc = self.ps(ctx, T + "pc", [P, 512])
            const_in, ones_set, mask_ready, sums, ch, shifted, ex_ready = (sem(n) for n in ("const_in", "rones_set", "mask_ready", "sums", "rch", "shifted", "ex_ready"))
            with nc.Block() as block:
                @block.sync
                def _(sp):
                    sp.dma_start(iota[:, :], d["c_iota"]).then_inc(const_in, 16)
                    sp.dma_start(low[:, :], d["c_before"]).then_inc(const_in, 16)

                @block.gpsimd
                def _(pool):
                    pool.memset(ones[:, :], 1.0).then_inc(ones_set, 1)

                @block.scalar
                def _(act):
                    if layer == 1:
                        act.wait_ge(shifted, 1)
                        nc.scalar.activation(te["tmp"][:, :, :], te["tmp"][:, :, :], ACT.Exp).then_inc(ex_ready, 1)

                @block.tensor
                def _(pe):
                    pe.wait_ge(const_in, 32)
                    pe.wait_ge(ones_set, 1)
                    pe.wait_ge(mask_ready, 1)
                    mask = te["mask"][:, :, :].rearrange("p t e -> p e t")
                    nc.tensor.matmul(pw[:, 0:TE], low[:, :], mask, start=True, stop=True)
                    nc.tensor.matmul(pc[:, 0:TE], ones[:, 0:P], mask, start=True, stop=True).then_inc(sums, 1)

                @block.vector
                def _(dve):
                    n = [0]

                    def link(ins):
                        n[0] += 1
                        ins.then_inc(ch, 1)
                        dve.wait_ge(ch, n[0])

                    tt, ts = nc.vector.tensor_tensor, nc.vector.tensor_scalar
                    lg = self.lg[:, :, :]
                    eq, oh1, oh2, mask, tmp = (te[k][:, :, :] for k in ("eq", "oh1", "oh2", "mask", "tmp"))
                    over_e = lambda a: a.unsqueeze(2).broadcast_to([P, TILES, EXPERTS])
                    over_t = lambda a: a.unsqueeze(1).broadcast_to([P, TILES, EXPERTS])
                    dve.wait_ge(const_in, 32)
                    dve.wait_ge(ones_set, 1)
                    link(ts(i99[:, :], iota[:, 0:EXPERTS], -99.0, None, ALU.add))

                    def choose(src, k, oh):
                        link(nc.vector.tensor_reduce(best[:, k, :], src, AX.X, ALU.max))
                        link(tt(eq, src, over_e(best[:, k, :]), ALU.is_equal))
                        link(tt(eq, eq, over_t(i99[:, :]), ALU.mult))
                        link(nc.vector.tensor_reduce(at[:, :], eq, AX.X, ALU.min))
                        link(tt(oh, over_t(i99[:, :]), over_e(at[:, :]), ALU.is_equal))

                    choose(lg, 0, oh1)
                    link(nc.vector.scalar_tensor_tensor(out=tmp, in0=oh1, scalar=-1e38, in1=lg, op0=ALU.mult, op1=ALU.add))
                    choose(tmp, 1, oh2)
                    tt(mask, oh1, oh2, ALU.add).then_inc(mask_ready, 1)
                    if layer == 1:
                        tt(tmp, lg, over_e(best[:, 0, :]), ALU.subtract).then_inc(shifted, 1)
                        dve.wait_ge(ex_ready, 1)
                        link(nc.vector.tensor_reduce(at[:, :], tmp, AX.X, ALU.add))
                        link(nc.vector.reciprocal(at[:, :], at[:, :]))
                        link(tt(tmp, tmp, over_e(at[:, :]), ALU.mult))
                        for k, oh in enumerate((oh1, oh2)):
                            link(tt(eq, tmp, oh, ALU.mult))
                            link(nc.vector.tensor_reduce(self.wt[:, k, :], eq, AX.X, ALU.add))
                        link(tt(at[:, :], self.wt[:, 0, :], self.wt[:, 1, :], ALU.add))
                        link(ts(at[:, :], at[:, :], 1e-8, None, ALU.max))
                        link(nc.vector.reciprocal(at[:, :], at[:, :]))
                        link(tt(self.wt[:, :, :], self.wt[:, :, :], at[:, :].unsqueeze(1).broadcast_to([P, 2, TILES]), ALU.mult))
                    dve.wait_ge(sums, 1)
                    cnt, tot, slot = (et[k][:, :, :] for k in ("cnt", "sum", "slot"))
                    flat = lambda a: a.rearrange("p e t -> p (e t)")
                    prev, ne, incl, base = (e8[k][:, :] for k in ("prev", "n", "incl", "base"))
                    link(nc.vector.tensor_copy(flat(cnt), pc[:, 0:TE]))
                    link(nc.vector.tensor_tensor_scan(flat(tot), ones[:, 0:TE], flat(cnt), 0.0, ALU.mult, ALU.add))
                    link(nc.vector.memset(prev, 0.0))
                    link(nc.vector.tensor_copy(e8["prev"][:, 1:EXPERTS], et["sum"][:, 0:EXPERTS - 1, TILES - 1]))
                    link(tt(ne, et["sum"][:, :, TILES - 1], prev, ALU.subtract))
                    link(ts(thr[:, :], iota[:, 0:M], float(ROWS), None, ALU.mult))
                    link(tt(cmp16[:, :, :], ne.unsqueeze(2).broadcast_to([P, EXPERTS, M]), thr[:, :].unsqueeze(1).broadcast_to([P, EXPERTS, M]), ALU.is_gt))
                    link(nc.vector.tensor_reduce(ne, cmp16[:, :, :], AX.X, ALU.add))
                    link(nc.vector.tensor_tensor_scan(incl, ones[:, 0:EXPERTS], ne, 0.0, ALU.mult, ALU.add))
                    link(tt(base, incl, ne, ALU.subtract))
                    link(nc.vector.scalar_tensor_tensor(out=base, in0=base, scalar=float(ROWS), in1=prev, op0=ALU.mult, op1=ALU.subtract))
                    link(tt(slot, tot, cnt, ALU.subtract))
                    link(tt(slot, slot, base.unsqueeze(2).broadcast_to([P, EXPERTS, TILES]), ALU.add))
                    link(tt(flat(slot), flat(slot), pw[:, 0:TE], ALU.add))
                    for k, oh in enumerate((oh1, oh2)):
                        link(tt(eq, oh, slot.rearrange("p e t -> p t e"), ALU.mult))
                        link(nc.vector.tensor_reduce(fl[:, k, :], eq, AX.X, ALU.add))
                    link(nc.vector.tensor_copy(self.slot[:, :, :], fl[:, :, :]))
                    E1 = EXPERTS - 1
                    link(tt(cmpj[:, :, :], e8["incl"][:, 0:E1].unsqueeze(1).broadcast_to([P, XT, E1]), iota[:, 0:XT].unsqueeze(2).broadcast_to([P, XT, E1]), ALU.is_le))
                    link(nc.vector.tensor_reduce(oj, cmpj[:, :, :], AX.X, ALU.add))
                    link(nc.vector.tensor_copy(self.owner[:, :], oj))

    def moe_scatter(self, layer):
        nc, T = self.nc, self.T
        with ExitStack() as ctx:
            sent = self.sent
            with nc.Block() as block:
                @block.gpsimd
                def _(pool):
                    for t in range(TILES):
                        for k in range(2):
                            pool.indirect_dma_start(self.xs_d[:, :], bass.IndirectOffsetOnAxis(ap=self.slot[:, k, t:t + 1], axis=0),
                                                    self.zh[:, t, :, :].rearrange("p a d -> p (a d)"), None).then_inc(sent[k], 16)
                    for k in range(2):
                        pool.wait_ge(sent[k], 16 * TILES * (layer + 1))

    def moe_tiles(self, layer):
        nc, d, T, H, NH = self.nc, self.dram, self.T, self.H, self.NH
        func = ACT.Silu if layer == 0 else ACT.Gelu
        PAIRS = ((0, 0), (0, 1), (1, 0))
        with ExitStack() as ctx:
            sb = lambda n, s, t=F32: self.sb(ctx, T + n, s, t)
            sem = lambda n: self.sem(ctx, T + n)
            b2 = sb("b2", [P, EXPERTS, D])
            xr = sb("xr", [P, 2, 2, 2 * D], F16)
            xT = sb("xT", [P, 2, 2, DC, ROWS], F16)
            hf = sb("hf", [P, 2, 2, ROWS])
            hh = sb("hh", [P, 2, NH, 2, ROWS], F16)
            y = sb("y", [P, 2, 2, D])
            pt = self.ps(ctx, T + "pt", [P, 2, 1024], F16)
            ph = self.ps(ctx, T + "ph", [P, 4, 512])
            py = self.ps(ctx, T + "py", [P, 2, 512])
            b2_in, tr_done, xT_ready, h_done, act_done, hi_done, lo_done, y_done, y_taken = (
                sem(n) for n in ("b2_in", "ttr_done", "xT_ready", "h_done", "act_done", "thi_done", "tlo_done", "y_done", "y_taken"))
            x_in = [sem(f"x_in{i}") for i in range(2)]
            y_out = [sem(f"y_out{i}") for i in range(2)]
            G = NH // 2
            with nc.Block() as block:
                @block.sync
                def _(sp):
                    sp.dma_start(b2[:, :, :], d[f"L{layer}_ffn_b2"].rearrange("e n -> (e n)").partition_broadcast(P).rearrange("p (e n) -> p e n", e=EXPERTS)).then_inc(b2_in, 16)
                    for par in range(2):
                        sp.sem_inc(y_out[par], 16)
                        sp.dma_start(xr[:, par, :, :], self.xs_d[par * ROWS:(par + 1) * ROWS, :].rearrange("(a p) n -> p a n", p=P)).then_inc(x_in[par], 16)

                    def turn(j, par, more):
                        if more:
                            sp.wait_ge(tr_done, j + 1)
                            sp.dma_start(xr[:, par, :, :], self.xs_d[bass.ds((j + 2) * ROWS, ROWS), :].rearrange("(a p) n -> p a n", p=P)).then_inc(x_in[par], 16)
                        sp.wait_ge(y_taken, 2 * j + 4)
                        sp.dma_start(self.ys_d[bass.ds(j * ROWS, ROWS), :].rearrange("(a p) n -> p a n", p=P), y[:, par, :, :]).then_inc(y_out[par], 16)

                    with sp.Fori(0, XT // 2 - 1) as r:
                        for par in range(2):
                            turn(2 * r + par, par, True)
                    for par in range(2):
                        turn(XT - 2 + par, par, False)
                        sp.wait_ge(y_out[par], 16 * (XT // 2) + 16)

                @block.tensor
                def _(pe):
                    def first(j, par, n_in):
                        e = nc.tensor.value_load(self.owner[0:1, bass.ds(j, 1)], min_val=0, max_val=EXPERTS - 1)
                        pe.wait_ge(x_in[par], n_in)
                        for hl in range(2):
                            for c in range(DC):
                                for a in range(2):
                                    o = ((hl * DC + c) * 2 + a) * P
                                    tr = nc.tensor.transpose(pt[:, par, o:o + P], xr[:, par, a, hl * D + c * P:hl * D + (c + 1) * P], self.ident_h[:, :])
                        tr.then_inc(tr_done, 1)
                        pe.wait_ge(xT_ready, j + 1)
                        for m in range(NH):
                            g, q = m // 2, m % 2
                            if q == 0:
                                pe.wait_ge(act_done, NH * j + m + 2)
                            for c in range(DC):
                                for i, (wp, xp) in enumerate(PAIRS):
                                    mm = nc.tensor.matmul(ph[:, (G * par + g) % 4, q * ROWS:(q + 1) * ROWS], self.w1[:, bass.ds(e, 1), c, wp, m * P:(m + 1) * P].rearrange("p a n -> p (a n)"),
                                                          xT[:, par, xp, c, :], start=(c == 0 and i == 0), stop=(c == DC - 1 and i == 2), skip_group_check=True)
                            mm.then_inc(h_done, 1)

                    def second(j, par):
                        e = nc.tensor.value_load(self.owner[0:1, bass.ds(j, 1)], min_val=0, max_val=EXPERTS - 1)
                        for a in range(2):
                            pe.wait_ge(y_taken, 2 * j + a + 1)
                            for m in range(NH):
                                if a == 0 and m % 2 == 0:
                                    pe.wait_ge(lo_done, G * j + m // 2 + 3)
                                for i, (wp, hp) in enumerate(PAIRS):
                                    mm = nc.tensor.matmul(py[:, a, 0:D], hh[:, par, m, hp, a * P:(a + 1) * P],
                                                          self.w2[:, bass.ds(e, 1), m, wp, :].rearrange("p a n -> p (a n)"), start=(m == 0 and i == 0), stop=(m == NH - 1 and i == 2))
                            mm.then_inc(y_done, 1)

                    first(0, 0, 16)
                    with pe.Fori(0, XT // 2 - 1) as r:
                        for par in range(2):
                            first(2 * r + par + 1, 1 - par, 16 * (r + par) + 16)
                            second(2 * r + par, par)
                    first(XT - 1, 1, 16 * (XT // 2))
                    second(XT - 2, 0)
                    second(XT - 1, 1)

                @block.scalar
                def _(act):
                    act.sem_inc(act_done, 8)
                    with act.Fori(0, XT // 2) as r:
                        for par in range(2):
                            j = 2 * r + par
                            e = nc.scalar.value_load(self.owner[0:1, bass.ds(j, 1)], min_val=0, max_val=EXPERTS - 1)
                            for m in range(NH):
                                g, q = m // 2, m % 2
                                if q == 0:
                                    act.wait_ge(h_done, NH * j + m + 2)
                                    act.wait_ge(lo_done, G * j + g + 1)
                                col = lambda a: a[:, bass.ds(e, 1), m:m + 1].rearrange("p a m -> p (a m)")
                                if layer == 0:
                                    nc.scalar.activation(hf[:, g % 2, q, :], ph[:, (G * par + g) % 4, q * ROWS:(q + 1) * ROWS], func, bias=col(self.b1), scale=col(self.s1)).then_inc(act_done, 1)
                                else:
                                    nc.scalar.activation(hf[:, g % 2, q, :], ph[:, (G * par + g) % 4, q * ROWS:(q + 1) * ROWS], func, bias=col(self.b1)).then_inc(act_done, 1)

                @block.vector
                def _(dve):
                    dve.sem_inc(lo_done, 2)
                    dve.sem_inc(y_taken, 2)
                    dve.wait_ge(b2_in, 16)

                    def out(j, par, n_out):
                        e = nc.vector.value_load(self.owner[0:1, bass.ds(j, 1)], min_val=0, max_val=EXPERTS - 1)
                        dve.wait_ge(y_out[par], n_out)
                        for a in range(2):
                            dve.wait_ge(y_done, 2 * j + a + 1)
                            nc.vector.tensor_tensor(y[:, par, a, :], py[:, a, 0:D], b2[:, bass.ds(e, 1), :].rearrange("p a n -> p (a n)"), ALU.add).then_inc(y_taken, 1)

                    def tile(j, par):
                        dve.wait_ge(tr_done, j + 1)
                        nc.vector.tensor_copy(xT[:, par, :, :, :].rearrange("p h c n -> p (h c n)"), pt[:, par, :]).then_inc(xT_ready, 1)
                        for g in range(G):
                            dve.wait_ge(act_done, NH * j + 2 * g + 2 + 8)
                            hi, lo = (hh[:, par, 2 * g:2 * g + 2, w, :] for w in range(2))
                            nc.vector.tensor_copy(hi, hf[:, g % 2, :, :]).then_inc(hi_done, 1)
                            dve.wait_ge(hi_done, G * j + g + 1)
                            nc.vector.tensor_tensor(lo, hf[:, g % 2, :, :], hi, ALU.subtract).then_inc(lo_done, 1)

                    tile(0, 0)
                    with dve.Fori(0, XT // 2 - 1) as r:
                        for par in range(2):
                            tile(2 * r + par + 1, 1 - par)
                            out(2 * r + par, par, 16 * r + 16)
                    tile(XT - 1, 1)
                    out(XT - 2, 0, 16 * (XT // 2))
                    out(XT - 1, 1, 16 * (XT // 2))

    def moe_combine(self, layer):
        nc, T = self.nc, self.T
        with ExitStack() as ctx:
            sb = lambda n, s, t=F32: self.sb(ctx, T + n, s, t)
            NG = len(self.got_in)
            gate = sb("gate", [P, B, D])
            got = sb("got", [P, NG, 2, D])
            gate_in = self.sem(ctx, T + "gate_in")
            got_in = self.got_in
            got0 = layer * 32 * (TILES // NG)
            ch, done = self.sem(ctx, T + "cch"), self.sem(ctx, T + "cdone")
            with nc.Block() as block:
                @block.sync
                def _(sp):
                    sp.dma_start(gate[:, :, :], self.mod_d[:, layer, 1, :, :]).then_inc(gate_in, 16)

                @block.gpsimd
                def _(pool):
                    for t in range(TILES):
                        if t >= NG:
                            pool.wait_ge(done, t - NG + 1)
                        for k in range(2):
                            pool.indirect_dma_start(got[:, t % NG, k, :], None, self.ys_d[:, :],
                                                    bass.IndirectOffsetOnAxis(ap=self.slot[:, k, t:t + 1], axis=0)).then_inc(got_in[t % NG], 16)

                @block.vector
                def _(dve):
                    n = [0]

                    def link(ins):
                        n[0] += 1
                        ins.then_inc(ch, 1)
                        dve.wait_ge(ch, n[0])

                    dve.wait_ge(gate_in, 16)
                    for t in range(TILES):
                        dve.wait_ge(got_in[t % NG], got0 + 32 * (t // NG) + 32)
                        g0, g1 = got[:, t % NG, 0, :], got[:, t % NG, 1, :]
                        if layer == 0:
                            link(nc.vector.tensor_tensor(g0, g0, g1, ALU.add))
                        else:
                            link(nc.vector.tensor_scalar(g0, g0, self.wt[:, 0, t:t + 1], None, ALU.mult))
                            link(nc.vector.scalar_tensor_tensor(out=g0, in0=g1, scalar=self.wt[:, 1, t:t + 1], in1=g0, op0=ALU.mult, op1=ALU.add))
                        link(nc.vector.tensor_tensor(g0, g0, gate[:, t // TPB, :], ALU.mult))
                        nc.vector.tensor_tensor(self.x[:, t, :], self.x[:, t, :], g0, ALU.add).then_inc(done, 1)


    def store(self):
        nc = self.nc
        with ExitStack() as ctx:
            stored = self.sem(ctx, "stored")
            with nc.Block() as block:
                @block.sync
                def _(sp):
                    sp.dma_start(self.out.rearrange("b (t p) d -> p (b t) d", p=P), self.x[:, :, :]).then_inc(stored, 16)
                    sp.wait_ge(stored, 16)


def host_layout(inputs):
    a = {n: np.ascontiguousarray(v) for n, v in inputs.items()}
    for n in "qkvo":
        a[f"L0_attn_w{n}_wT"] = np.ascontiguousarray(a.pop(f"L0_attn_w{n}_w").T)
    for n in "qk":
        a[f"{n}n_rep"] = np.tile(a.pop(f"L0_attn_{n}n_w"), P // HD)
    columns = lambda v: np.ascontiguousarray(v.reshape(EXPERTS, -1, P).transpose(2, 0, 1))
    a["L0_gateT"] = np.ascontiguousarray(a.pop("L0_ffn_gate_v").T)
    a["L0_w1T"] = np.ascontiguousarray(a.pop("L0_ffn_w1_v").transpose(0, 2, 1))
    a["L0_w2T"] = np.ascontiguousarray(a.pop("L0_ffn_w2_v").transpose(0, 2, 1))
    a["L0_b1c"], a["L0_g1c"], a["L1_b1c"] = columns(a.pop("L0_ffn_b1")), columns(a.pop("L0_ffn_w1_g")), columns(a.pop("L1_ffn_b1"))
    a.update(constants())
    return a


def kernel(**inputs):
    import concourse.bacc as bacc
    from concourse.bass_utils import run_bass_kernel_spmd

    nc = bacc.Bacc("TRN2", target_bir_lowering=False, num_devices=1)
    arrays = host_layout(inputs)
    dram = {n: nc.dram_tensor(n, a.shape, mybir.dt.from_np(a.dtype), kind="ExternalInput").ap() for n, a in arrays.items()}
    out = nc.dram_tensor("out", (B, L, D), F32, kind="ExternalOutput").ap()
    Program(nc, dram, out).build()
    return run_bass_kernel_spmd(nc, [arrays], core_ids=[0]).results[0]["out"]
```

```python
from contextlib import ExitStack

import numpy as np

import concourse.bass as bass
from concourse import mybir

ACT = mybir.ActivationFunctionType
ALU = mybir.AluOpType
AX = mybir.AxisListType
F32 = mybir.dt.float32
BF16 = mybir.dt.bfloat16
F16 = mybir.dt.float16
U32 = mybir.dt.uint32
I32 = mybir.dt.int32

P = 128
B, L, D = 4, 1024, 256
N_TOK = B * L
TILES = N_TOK // P
TPB = L // P
DC = D // P
HEADS, HD = 16, 16
HG = 4
STEPS = B * HEADS // HG
WINDOW = 64
EXPERTS = 8
ROWS = 256
XT = 2 * N_TOK // ROWS + EXPERTS
EPS = 1e-5
NEG = -1e30
SLOTS = 6
KROWS = SLOTS * HD
KAUG = KROWS + 3
QK = 4
HALF = 512
HT = HALF // P


def constants():
    r = np.arange(P)
    out = {}
    out["c_ident"] = np.eye(P, dtype=np.float32)
    out["c_heads"] = (r[:, None] // HD == r[None, :] // HD).astype(np.float32)
    out["c_swap"] = ((r[:, None] ^ 1) == r[None, :]).astype(np.float32)
    q, k = r[:, None], r[None, :]
    causal = np.where(k <= q, 0.0, NEG).astype(np.float32)
    out["c_causal"] = np.stack([causal, causal.T], 1)
    prev = np.where(q - (k - P) < WINDOW, 0.0, NEG)
    diag = np.where((k <= q) & (q - k < WINDOW), 0.0, NEG)
    out["c_window"] = np.stack([np.concatenate([prev, diag], 1), np.concatenate([diag.T, prev.T], 1)], 1).astype(np.float32)
    out["c_iota"] = np.tile(np.arange(64, dtype=np.float32), (P, 1))
    out["c_before"] = (r[:, None] < r[None, :]).astype(np.float32)
    inv = (1.0 / np.float32(10000.0) ** (np.arange(0, HD, 2, dtype=np.float32) / np.float32(HD))).astype(np.float32)
    ang = (np.arange(L, dtype=np.float32)[None, :] * inv[(r % HD) // 2][:, None]).astype(np.float32)
    sign = np.where(r % 2 == 0, -1.0, 1.0).astype(np.float32)[:, None]
    out["c_rope"] = np.stack([np.cos(ang), np.sin(ang) * sign], 1).astype(np.float32)
    return out


class Program:

    def __init__(self, nc, dram, out):
        self.nc, self.dram, self.out = nc, dram, out
        self.ctx = ExitStack()

    def sb(self, ctx, name, shape, dt=F32):
        return ctx.enter_context(self.nc.sbuf_tensor(name, shape, dt))

    def ps(self, ctx, name, shape, dt=F32):
        return ctx.enter_context(self.nc.psum_tensor(name, shape, dt))

    def sem(self, ctx, name):
        handle = ctx.enter_context(self.nc.semaphore(name))
        ctx.callback(lambda: self.nc.gpsimd.sem_clear(handle))
        return handle

    def build(self, stop=None):
        with self.ctx as ctx:
            self.resident(ctx)
            self.setup()
            for layer in (0, 1):
                self.project(layer)
                with ExitStack() as hold:
                    self.attn = self.sb(hold, f"attn{layer}", [P, TILES, D])
                    self.attend(layer)
                    self.out_project(layer)
                if stop == f"attn{layer}":
                    break
                self.moe(layer)
                if stop == f"moe{layer}":
                    break
            self.store()

    def resident(self, ctx):
        self.x = self.sb(ctx, "x_res", [P, TILES, D])
        self.ident = self.sb(ctx, "ident", [P, P])
        self.ident_bf = self.sb(ctx, "ident_bf", [P, P], BF16)
        self.ident_h = self.sb(ctx, "ident_h", [P, P], F16)
        self.causal = self.sb(ctx, "causal", [P, 2, P], BF16)
        self.window = self.sb(ctx, "window", [P, 2, 2 * P], BF16)
        self.mod_col = self.sb(ctx, "mod_col", [P, 2, 12, B])
        nc = self.nc
        keep = lambda n: ctx.enter_context(nc.semaphore(n))
        self.zero_out, self.sent, self.got_in = keep("zero_out"), [keep("sent0"), keep("sent1")], [keep(f"got_in{i}") for i in range(4)]
        self.mod_d = nc.dram_tensor("mod_d", (P, 2, 4, B, D), F32, kind="Internal").ap()
        self.parts_d = nc.dram_tensor("parts_d", (2, 3, QK * P, N_TOK), BF16, kind="Internal").ap()
        self.v_d = nc.dram_tensor("v_d", (2, N_TOK, 2 * D), F32, kind="Internal").ap()

    def setup(self):
        nc, d = self.nc, self.dram
        with ExitStack() as ctx:
            cT = self.sb(ctx, "cT", [P, 2, DC, B])
            sT = self.sb(ctx, "sT", [P, 2, DC, B])
            sgm = self.sb(ctx, "sgm", [P, 2, DC, B])
            sbc = self.sb(ctx, "sbc", [P, 2, DC, B, P])
            wmod = self.sb(ctx, "wmod", [P, 2, DC, 6 * D])
            stage = self.sb(ctx, "stage", [P, 6 * P])
            gtmp = self.sb(ctx, "gtmp", [P, 2, D])
            mod_row = self.sb(ctx, "mod_row", [P, 2, 4, B, D])
            mod_out = self.sem(ctx, "mod_out")
            ones = self.sb(ctx, "ones", [P, P])
            pcol = self.ps(ctx, "pcol", [P, 2, 512])
            prow = self.ps(ctx, "prow", [P, 4, 512])
            x_in = self.sem(ctx, "x_in")
            mod_in = self.sem(ctx, "mod_in")
            const_in = self.sem(ctx, "const_in")
            cast = self.sem(ctx, "cast")
            ones_set = self.sem(ctx, "ones_set")
            sig = self.sem(ctx, "sig")
            silu = self.sem(ctx, "silu")
            spread = self.sem(ctx, "spread")
            col_mm = self.sem(ctx, "col_mm")
            row_mm = self.sem(ctx, "row_mm")
            row_ev = self.sem(ctx, "row_ev")
            mod_ch = self.sem(ctx, "mod_ch")
            with nc.Block() as block:
                @block.sync
                def _(sp):
                    for l in range(2):
                        for c in range(DC):
                            with nc.allow_non_contiguous_dma(reason="a small transposed load"):
                                sp.dma_start(cT[:, l, c, :], d[f"L{l}_c"][:, c * P:(c + 1) * P].rearrange("b p -> p b")).then_inc(mod_in, 16)
                        sp.dma_start(wmod[:, l, :, :], d[f"L{l}_wmod"].rearrange("(c p) n -> p c n", p=P)).then_inc(mod_in, 16)
                    sp.dma_start(self.ident[:, :], d["c_ident"]).then_inc(const_in, 16)
                    sp.dma_start(stage[:, 0:2 * P], d["c_causal"].rearrange("p a n -> p (a n)")).then_inc(const_in, 16)
                    sp.dma_start(stage[:, 2 * P:6 * P], d["c_window"].rearrange("p a n -> p (a n)")).then_inc(const_in, 16)
                    sp.dma_start(self.x[:, :, :], d["L0_attn_x"].rearrange("b (t p) d -> p (b t) d", p=P)).then_inc(x_in, 16)
                    sp.wait_ge(row_ev, 16)
                    sp.dma_start(self.mod_d, mod_row[:, :, :, :, :]).then_inc(mod_out, 16)
                    sp.wait_ge(mod_out, 16)
                    sp.wait_ge(x_in, 16)

                @block.gpsimd
                def _(pool):
                    pool.memset(ones[:, :], 1.0).then_inc(ones_set, 1)
                    pool.wait_ge(const_in, 48)
                    pool.tensor_copy(self.ident_bf[:, :], self.ident[:, :]).then_inc(cast, 1)
                    pool.tensor_copy(self.ident_h[:, :], self.ident[:, :]).then_inc(cast, 1)
                    pool.tensor_copy(self.causal[:, :, :].rearrange("p a n -> p (a n)"), stage[:, 0:2 * P]).then_inc(cast, 1)
                    pool.tensor_copy(self.window[:, :, :].rearrange("p a n -> p (a n)"), stage[:, 2 * P:6 * P]).then_inc(cast, 1)

                @block.scalar
                def _(act):
                    act.wait_ge(mod_in, 16 * 6)
                    nc.scalar.activation(sgm[:, :, :, :], cT[:, :, :, :], ACT.Sigmoid).then_inc(sig, 1)

                @block.vector
                def _(dve):
                    dve.wait_ge(sig, 1)
                    nc.vector.tensor_tensor(sT[:, :, :, :], cT[:, :, :, :], sgm[:, :, :, :], ALU.mult).then_inc(silu, 1)
                    dve.wait_ge(silu, 1)
                    dve.wait_ge(ones_set, 1)
                    for l in range(2):
                        for c in range(DC):
                            for b in range(B):
                                nc.vector.tensor_scalar(sbc[:, l, c, b, :], ones[:, :], sT[:, l, c, b:b + 1], None, ALU.mult).then_inc(spread, 1)
                    for l in range(2):
                        dve.wait_ge(col_mm, l + 1)
                        cols = pcol[:, l, 0:12 * B].rearrange("p (m b) -> p m b", b=B)
                        nc.vector.tensor_copy(self.mod_col[:, l, :, :], cols).then_inc(mod_ch, 1)
                        dve.wait_ge(mod_ch, 2 * l + 1)
                        ca = self.mod_col[:, l, :, :].rearrange("p (g six) b -> p g six b", six=6)[:, :, 2:4, :]
                        nc.vector.tensor_scalar(ca, ca, 1.0, None, ALU.add).then_inc(mod_ch, 1)
                    n = 0
                    for l in range(2):
                        for kind in range(4):
                            for bp in range(B // 2):
                                dve.wait_ge(row_mm, n + 1)
                                src = prow[:, n % 4, :].rearrange("p (b d) -> p b d", d=D)
                                dst = mod_row[:, l, kind, 2 * bp:2 * bp + 2, :]
                                if kind >= 2:
                                    nc.vector.tensor_scalar(dst, src, float(kind - 2), None, ALU.add).then_inc(row_ev, 1)
                                else:
                                    dve.wait_ge(row_ev, n)
                                    m = 4 + 3 * (l * 4 + kind * 2 + bp)
                                    nc.vector.tensor_scalar(gtmp[:, :, :], src, 0.0, 2.0, ALU.is_ge, ALU.mult).then_inc(mod_ch, 1)
                                    dve.wait_ge(mod_ch, m + 1)
                                    nc.vector.tensor_scalar(gtmp[:, :, :], gtmp[:, :, :], -1.0, None, ALU.add).then_inc(mod_ch, 1)
                                    dve.wait_ge(mod_ch, m + 2)
                                    nc.vector.tensor_tensor(dst, gtmp[:, :, :], src, ALU.mult).then_inc(mod_ch, 1)
                                    dve.wait_ge(mod_ch, m + 3)
                                    nc.vector.scalar_tensor_tensor(out=dst, in0=dst, scalar=0.25, in1=gtmp[:, :, :], op0=ALU.max, op1=ALU.mult).then_inc(row_ev, 1)
                                n += 1

                @block.tensor
                def _(pe):
                    pe.wait_ge(silu, 1)
                    for l in range(2):
                        for m in range(12):
                            for c in range(DC):
                                mm = nc.tensor.matmul(pcol[:, l, m * B:(m + 1) * B], wmod[:, l, c, m * P:(m + 1) * P], sT[:, l, c, :],
                                                      start=(c == 0), stop=(c == DC - 1))
                        mm.then_inc(col_mm, 1)
                    pe.wait_ge(spread, 2 * DC * B)
                    n = 0
                    for l in range(2):
                        for kind, at in enumerate((2, 5, 3, 4)):
                            for bp in range(B // 2):
                                if n >= 4:
                                    pe.wait_ge(row_ev, n - 3)
                                for bb in range(2):
                                    for c in range(DC):
                                        mm = nc.tensor.matmul(prow[:, n % 4, bb * D:(bb + 1) * D], sbc[:, l, c, 2 * bp + bb, :],
                                                              wmod[:, l, c, at * D:(at + 1) * D], start=(c == 0), stop=(c == DC - 1))
                                mm.then_inc(row_mm, 1)
                                n += 1

    def project(self, layer):
        nc, d = self.nc, self.dram
        rope = layer == 1
        with ExitStack() as ctx:
            T = f"p{layer}_"
            sb = lambda n, s, t=F32: self.sb(ctx, T + n, s, t)
            sem = lambda n: self.sem(ctx, T + n)
            HEADS_CH = P // HD
            w = sb("w", [P, DC, 3 * D])
            bias = sb("bias", [P, QK])
            nw = sb("nw", [P, 2])
            bv = sb("bv", [P, D])
            aux = sb("aux", [P, P])
            cs = sb("cs", [P, 2, L]) if rope else None
            stats = sb("stats", [P, 2, nc.vector.BN_STATS_DIM])
            mv = sb("mv", [P, 4, 2])
            sd = sb("sd", [P, 4])
            rstd = sb("rstd", [P, 4])
            eps = sb("eps", [P, 1])
            modb = sb("modb", [P, 2, DC])
            xn = sb("xn", [P, 4, D])
            hT = sb("hT", [P, 2, DC, HALF])
            raw = sb("raw", [P, 2, HALF]) if not rope else None
            u = sb("u", [P, 4, HALF])
            side = sb("side", [P, 2, HALF])
            rn = sb("rn", [P, 2, HALF]) if rope else sb("rn", [P, 4, HT * HEADS_CH])
            wide = sb("wide", [P, HALF]) if not rope else None
            un = sb("un", [P, 4, HALF])
            rem = sb("rem", [P, 2, HALF])
            part = sb("part", [P, 4, 3, HALF], BF16)
            vt = sb("vt", [P, 2, HT, HEADS, 2 * HD])
            ptr = self.ps(ctx, T + "ptr", [P, 2, 512])
            pqk = self.ps(ctx, T + "pqk", [P, 2, 512])
            pax = self.ps(ctx, T + "pax", [P, 2, 512])
            pv = self.ps(ctx, T + "pv", [P, 2, 512])
            w_in, vt_set = sem("w_in"), sem("vt_set")
            stats_ready, stats_seen, mv_ready, sd_ready, rstd_ready = (sem(n) for n in ("stats_ready", "stats_seen", "mv_ready", "sd_ready", "rstd_ready"))
            xn_ready, tr_done, mod_ready, h_ready, qk_done, v_done, v_ready = (sem(n) for n in ("xn_ready", "tr_done", "mod_ready", "h_ready", "qk_done", "v_done", "v_ready"))
            raw_ready, u_ready, side_ready, aux_done, mean_ready, rn_ready = (sem(n) for n in ("raw_ready", "u_ready", "side_ready", "aux_done", "mean_ready", "rn_ready"))
            rms_ready, wide_ready, spread_done = sem("rms_ready"), sem("wide_ready"), sem("spread_done")
            un_ready, hi_ready, rem_ready, mid_ready, lo_ready = (sem(n) for n in ("un_ready", "hi_ready", "rem_ready", "mid_ready", "lo_ready"))
            part_out = [sem(f"part_out{i}") for i in range(4)]
            v_out = [sem("v_out0"), sem("v_out1")]
            constants_in = 16 * (9 if not rope else 5)

            UNITS = 2 * QK
            AHEAD = 6
            HIGH = 3 if rope else 5
            LAST = HIGH + 2

            def unit(b, k, behind):
                q = k - behind
                if q < 0:
                    b, q = b - 1, q + UNITS
                elif q >= UNITS:
                    b, q = b + 1, q - UNITS
                if isinstance(b, int) and not 0 <= b < B:
                    return None
                return b, q

            def run(eng, slot):
                for k in range(-AHEAD, UNITS):
                    slot(0, k)
                with eng.Fori(1, B - 1) as b:
                    for k in range(UNITS):
                        slot(b, k)
                for k in range(UNITS + LAST + 1):
                    slot(B - 1, k)

            used = lambda count: not isinstance(count, int) or count > 0

            with nc.Block() as block:
                @block.sync
                def _(sp):
                    with nc.allow_non_contiguous_dma(reason="bias and norm columns"):
                        if rope:
                            sp.dma_start(w[:, :, :], d["L1_attn_Wqkv"].rearrange("(c p) n -> p c n", p=P)).then_inc(w_in, 16)
                            sp.dma_start(bias[:, :], d["L1_attn_bqkv"][0:2 * D].rearrange("(c p) -> p c", p=P)).then_inc(w_in, 16)
                            sp.dma_start(bv[:, :], d["L1_attn_bqkv"][2 * D:3 * D].partition_broadcast(P)).then_inc(w_in, 16)
                            sp.dma_start(cs[:, :, :], d["c_rope"]).then_inc(w_in, 16)
                            sp.dma_start(aux[:, :], d["c_swap"]).then_inc(w_in, 16)
                        else:
                            for j, n in enumerate("qkv"):
                                sp.dma_start(w[:, :, j * D:(j + 1) * D], d[f"L0_attn_w{n}_wT"].rearrange("(c p) n -> p c n", p=P)).then_inc(w_in, 16)
                            for j, n in enumerate("qk"):
                                sp.dma_start(bias[:, 2 * j:2 * j + 2], d[f"L0_attn_w{n}_b"].rearrange("(c p) -> p c", p=P)).then_inc(w_in, 16)
                            sp.dma_start(bv[:, :], d["L0_attn_wv_b"].partition_broadcast(P)).then_inc(w_in, 16)
                            sp.dma_start(nw[:, 0:1], d["qn_rep"].rearrange("(p a) -> p a", a=1)).then_inc(w_in, 16)
                            sp.dma_start(nw[:, 1:2], d["kn_rep"].rearrange("(p a) -> p a", a=1)).then_inc(w_in, 16)
                            sp.dma_start(aux[:, :], d["c_heads"]).then_inc(w_in, 16)
                    pd = self.parts_d[layer].rearrange("s (c p) n -> p c s n", p=P)
                    vd = self.v_d[layer].rearrange("(t p) n -> p t n", p=P)

                    def slot(b, k):
                        if at := unit(b, k, 1):
                            n, q = UNITS * at[0] + at[1], at[1]
                            if q % QK == QK - 1:
                                sp.wait_ge(v_ready, n + 1)
                                sp.dma_start(vd[:, bass.ds(n - QK + 1, HT), :], vt[:, q // QK, :, :, :].rearrange("p t h e -> p t (h e)")).then_inc(v_out[q // QK], 16)
                        if at := unit(b, k, LAST):
                            n, q = UNITS * at[0] + at[1], at[1]
                            sp.wait_ge(lo_ready, n + 1)
                            sp.dma_start(pd[:, q % QK, :, bass.ds((2 * at[0] + q // QK) * HALF, HALF)], part[:, q % 4, :, :]).then_inc(part_out[q % 4], 16)

                    run(sp, slot)
                    for half in range(2):
                        sp.wait_ge(v_out[half], 16 * B)
                    for i in range(4):
                        sp.wait_ge(part_out[i], 16 * 2 * B)

                @block.gpsimd
                def _(pool):
                    pool.memset(vt[:, :, :, :, HD + 1:2 * HD], 0.0).then_inc(vt_set, 1)
                    pool.memset(vt[:, :, :, :, HD:HD + 1], 1.0).then_inc(vt_set, 1)
                    pool.memset(eps[:, :], EPS).then_inc(vt_set, 1)
                    pool.wait_ge(w_in, constants_in)

                    def slot(b, k):
                        if not rope and (at := unit(b, k, 1)):
                            n, q = UNITS * at[0] + at[1], at[1]
                            pool.wait_ge(u_ready, n + 1)
                            if used(n - 1):
                                pool.wait_ge(aux_done, n - 1)
                            nc.gpsimd.tensor_tensor(side[:, q % 2, :], u[:, q % 4, :], u[:, q % 4, :], ALU.mult).then_inc(side_ready, 1)
                        if rope and (at := unit(b, k, 1)):
                            n, q = UNITS * at[0] + at[1], at[1]
                            half = q // QK
                            pool.wait_ge(u_ready, n + 1)
                            if used(n - 1):
                                pool.wait_ge(un_ready, n - 1)
                            nc.gpsimd.tensor_tensor(side[:, q % 2, :], u[:, q % 4, :], cs[:, 0, half * HALF:(half + 1) * HALF], ALU.mult).then_inc(side_ready, 1)
                        if at := unit(b, k, LAST):
                            n, q = UNITS * at[0] + at[1], at[1]
                            pool.wait_ge(mid_ready, n + 1)
                            nc.gpsimd.tensor_tensor(part[:, q % 4, 2, :], rem[:, q % 2, :], part[:, q % 4, 1, :], ALU.subtract).then_inc(lo_ready, 1)

                    run(pool, slot)

                @block.vector
                def _(dve):
                    dve.wait_ge(w_in, constants_in)
                    dve.wait_ge(vt_set, 2)

                    def slot(b, k):
                        norm = unit(b, k, -AHEAD)
                        if norm:
                            n, q = UNITS * norm[0] + norm[1], norm[1]
                            nc.vector.bn_stats(stats[:, q % 2, :], self.x[:, bass.ds(n, 1), :].rearrange("p a d -> p (a d)")).then_inc(stats_ready, 1)
                        if not rope and (at := unit(b, k, 5)):
                            n, q = UNITS * at[0] + at[1], at[1]
                            ch = q % QK
                            dve.wait_ge(spread_done, n + 1)
                            if used(n - 3):
                                dve.wait_ge(rem_ready, n - 3)
                            nc.vector.scalar_tensor_tensor(out=un[:, q % 4, :], in0=u[:, q % 4, :], scalar=nw[:, ch // 2:ch // 2 + 1], in1=pax[:, 1, :],
                                                           op0=ALU.mult, op1=ALU.mult).then_inc(un_ready, 1)
                        if at := unit(b, k, 1):
                            n, q = UNITS * at[0] + at[1], at[1]
                            half, t = q // QK, q % QK
                            dve.wait_ge(v_done, n + 1)
                            if t == 0 and used(at[0]):
                                dve.wait_ge(v_out[half], 16 * at[0])
                            nc.vector.tensor_tensor(vt[:, half, t, :, 0:HD], pv[:, q % 2, 0:D].rearrange("p (h e) -> p h e", e=HD),
                                                    bv[:, :].rearrange("p (h e) -> p h e", e=HD), ALU.add).then_inc(v_ready, 1)
                            if not rope:
                                dve.wait_ge(raw_ready, n + 1)
                                if used(n - 3):
                                    dve.wait_ge(un_ready, n - 3)
                                nc.vector.tensor_scalar(u[:, q % 4, :], raw[:, q % 2, :], 1e4, -1e4, ALU.min, ALU.max).then_inc(u_ready, 1)
                        if norm:
                            n, q = UNITS * norm[0] + norm[1], norm[1]
                            dve.wait_ge(stats_ready, n + 1)
                            dve.sem_inc(stats_seen, 1)
                            nc.vector.bn_aggr(mv[:, q % 4, :], stats[:, q % 2, :]).then_inc(mv_ready, 1)
                        if at := unit(b, k, HIGH + 1):
                            n, q = UNITS * at[0] + at[1], at[1]
                            dve.wait_ge(hi_ready, n + 1)
                            if used(n - 1):
                                dve.wait_ge(lo_ready, n - 1)
                            nc.vector.tensor_tensor(rem[:, q % 2, :], un[:, q % 4, :], part[:, q % 4, 0, :], ALU.subtract).then_inc(rem_ready, 1)
                        if at := unit(b, k, 2):
                            n, q = UNITS * at[0] + at[1], at[1]
                            half = q // QK
                            dve.wait_ge(aux_done, n + 1)
                            if not rope:
                                nc.vector.tensor_scalar(rn[:, q % 4, :], pax[:, 0, 0:HT * HEADS_CH], 1.0 / HD, EPS, ALU.mult, ALU.max).then_inc(mean_ready, 1)
                            else:
                                nc.vector.tensor_tensor(rn[:, q % 2, :], pax[:, q % 2, :], cs[:, 1, half * HALF:(half + 1) * HALF], ALU.mult).then_inc(mean_ready, 1)
                        if not rope and (at := unit(b, k, 3)):
                            n, q = UNITS * at[0] + at[1], at[1]
                            dve.wait_ge(rms_ready, n + 1)
                            nc.vector.reciprocal(rn[:, q % 4, :], rn[:, q % 4, :]).then_inc(rn_ready, 1)
                        if at := unit(b, k, 1 - AHEAD):
                            n, q = UNITS * at[0] + at[1], at[1]
                            dve.wait_ge(sd_ready, n + 1)
                            nc.vector.reciprocal(rstd[:, q % 4:q % 4 + 1], sd[:, q % 4:q % 4 + 1]).then_inc(rstd_ready, 1)
                        if rope and (at := unit(b, k, 2)):
                            n, q = UNITS * at[0] + at[1], at[1]
                            dve.wait_ge(side_ready, n + 1)
                            dve.wait_ge(mean_ready, n + 1)
                            if used(n - 3):
                                dve.wait_ge(rem_ready, n - 3)
                            nc.vector.tensor_tensor(un[:, q % 4, :], side[:, q % 2, :], rn[:, q % 2, :], ALU.add).then_inc(un_ready, 1)
                        if at := unit(b, k, 1 - AHEAD):
                            n, q = UNITS * at[0] + at[1], at[1]
                            dve.wait_ge(rstd_ready, n + 1)
                            if used(n - 3):
                                dve.wait_ge(tr_done, n - 3)
                            nc.vector.tensor_scalar(xn[:, q % 4, :], self.x[:, bass.ds(n, 1), :].rearrange("p a d -> p (a d)"), mv[:, q % 4, 0:1], rstd[:, q % 4:q % 4 + 1],
                                                    ALU.subtract, ALU.mult).then_inc(xn_ready, 1)

                    run(dve, slot)

                @block.scalar
                def _(act):
                    act.wait_ge(w_in, constants_in)
                    act.wait_ge(vt_set, 3)

                    def slot(b, k):
                        if not rope and (at := unit(b, k, 4)):
                            n, q = UNITS * at[0] + at[1], at[1]
                            act.wait_ge(rn_ready, n + 1)
                            if used(n):
                                act.wait_ge(spread_done, n)
                            nc.scalar.activation(wide[:, :].rearrange("p (g e) -> p g e", e=HD), rn[:, q % 4, :].unsqueeze(2).broadcast_to([P, HT * HEADS_CH, HD]),
                                                 ACT.Copy).then_inc(wide_ready, 1)
                        if not rope and (at := unit(b, k, 3)):
                            n, q = UNITS * at[0] + at[1], at[1]
                            act.wait_ge(mean_ready, n + 1)
                            nc.scalar.activation(rn[:, q % 4, :], rn[:, q % 4, :], ACT.Sqrt, bias=eps[:, :]).then_inc(rms_ready, 1)
                        if at := unit(b, k, 1 - AHEAD):
                            n, q = UNITS * at[0] + at[1], at[1]
                            act.wait_ge(mv_ready, n + 1)
                            nc.scalar.activation(sd[:, q % 4:q % 4 + 1], mv[:, q % 4, 1:2], ACT.Sqrt, bias=eps[:, :]).then_inc(sd_ready, 1)
                        if at := unit(b, k, 2 - AHEAD):
                            n, q = UNITS * at[0] + at[1], at[1]
                            half, t = q // HT, q % HT
                            if q == 0:
                                if used(n):
                                    act.wait_ge(h_ready, n)
                                for j in range(2):
                                    nc.scalar.activation(modb[:, j, :], self.mod_col[:, layer, 2 * j:2 * j + 2, bass.ds(at[0], 1)].rearrange("p c a -> p (c a)"),
                                                         ACT.Copy).then_inc(mod_ready, 1)
                                act.wait_ge(mod_ready, 2 * at[0] + 2)
                            act.wait_ge(tr_done, n + 1)
                            for c in range(DC):
                                a = nc.scalar.activation(hT[:, half, c, t * P:(t + 1) * P], ptr[:, q % 2, c * P:(c + 1) * P], ACT.Identity,
                                                         bias=modb[:, 0, c:c + 1], scale=modb[:, 1, c:c + 1])
                            a.then_inc(h_ready, 1)
                        if at := unit(b, k, 0):
                            n, q = UNITS * at[0] + at[1], at[1]
                            ch = q % QK
                            act.wait_ge(qk_done, n + 1)
                            if not rope:
                                if used(n - 1):
                                    act.wait_ge(u_ready, n - 1)
                                nc.scalar.activation(raw[:, q % 2, :], pqk[:, q % 2, :], ACT.Identity, bias=bias[:, ch:ch + 1]).then_inc(raw_ready, 1)
                            else:
                                if used(n - 3):
                                    act.wait_ge(un_ready, n - 3)
                                nc.scalar.activation(u[:, q % 4, :], pqk[:, q % 2, :], ACT.Identity, bias=bias[:, ch:ch + 1]).then_inc(u_ready, 1)
                        if at := unit(b, k, HIGH):
                            n, q = UNITS * at[0] + at[1], at[1]
                            act.wait_ge(un_ready, n + 1)
                            left = 2 * at[0] + q // 4
                            if used(left):
                                act.wait_ge(part_out[q % 4], 16 * left)
                            nc.scalar.activation(part[:, q % 4, 0, :], un[:, q % 4, :], ACT.Copy).then_inc(hi_ready, 1)
                        if at := unit(b, k, HIGH + 1):
                            n, q = UNITS * at[0] + at[1], at[1]
                            act.wait_ge(rem_ready, n + 1)
                            nc.scalar.activation(part[:, q % 4, 1, :], rem[:, q % 2, :], ACT.Copy).then_inc(mid_ready, 1)

                    run(act, slot)

                @block.tensor
                def _(pe):
                    pe.wait_ge(w_in, constants_in)

                    def slot(b, k):
                        if at := unit(b, k, 2 - AHEAD):
                            n, q = UNITS * at[0] + at[1], at[1]
                            pe.wait_ge(xn_ready, n + 1)
                            if used(n - 1):
                                pe.wait_ge(h_ready, n - 1)
                            for c in range(DC):
                                tr = nc.tensor.transpose(ptr[:, q % 2, c * P:(c + 1) * P], xn[:, q % 4, c * P:(c + 1) * P], self.ident[:, :])
                            tr.then_inc(tr_done, 1)
                        if rope and (at := unit(b, k, 1)):
                            n, q = UNITS * at[0] + at[1], at[1]
                            pe.wait_ge(u_ready, n + 1)
                            if used(n - 1):
                                pe.wait_ge(mean_ready, n - 1)
                            nc.tensor.matmul(pax[:, q % 2, :], aux[:, :], u[:, q % 4, :], start=True, stop=True).then_inc(aux_done, 1)
                        if not rope and (at := unit(b, k, 2)):
                            n, q = UNITS * at[0] + at[1], at[1]
                            pe.wait_ge(side_ready, n + 1)
                            if used(n):
                                pe.wait_ge(mean_ready, n)
                            for t in range(HT):
                                mm = nc.tensor.matmul(pax[:, 0, t * HEADS_CH:(t + 1) * HEADS_CH], side[:, q % 2, t * P:(t + 1) * P],
                                                      aux[:, :].rearrange("p (h e) -> p h e", e=HD)[:, :, 0], start=True, stop=True)
                            mm.then_inc(aux_done, 1)
                        if at := unit(b, k, 0):
                            n, q = UNITS * at[0] + at[1], at[1]
                            half, ch = q // QK, q % QK
                            if ch == 0:
                                pe.wait_ge(h_ready, n + HT)
                            if used(n - 1):
                                if rope:
                                    pe.wait_ge(u_ready, n - 1)
                                else:
                                    pe.wait_ge(raw_ready, n - 1)
                            for c in range(DC):
                                mm = nc.tensor.matmul(pqk[:, q % 2, :], w[:, c, ch * P:(ch + 1) * P], hT[:, half, c, :], start=(c == 0), stop=(c == DC - 1))
                            mm.then_inc(qk_done, 1)
                            if used(n - 1):
                                pe.wait_ge(v_ready, n - 1)
                            for c in range(DC):
                                mm = nc.tensor.matmul(pv[:, q % 2, 0:D], hT[:, half, c, ch * P:(ch + 1) * P], w[:, c, 2 * D:3 * D], start=(c == 0), stop=(c == DC - 1))
                            mm.then_inc(v_done, 1)
                        if not rope and (at := unit(b, k, 4)):
                            n, q = UNITS * at[0] + at[1], at[1]
                            pe.wait_ge(wide_ready, n + 1)
                            if used(n):
                                pe.wait_ge(un_ready, n)
                            for t in range(HT):
                                mm = nc.tensor.matmul(pax[:, 1, t * P:(t + 1) * P], wide[:, t * P:(t + 1) * P], self.ident[:, :], start=True, stop=True)
                            mm.then_inc(spread_done, 1)

                    run(pe, slot)

    def max_units(self, layer):
        out = []
        for i in range(TPB):
            if layer == 0:
                ks = list(range(max(0, i - 1), i + 1))
                for h0 in range(0, HG, 4 // len(ks)):
                    out.append((i, range(h0, h0 + 4 // len(ks)), ks, 0))
            else:
                n = i + 1
                per = 4 if n == 1 else 2 if n == 2 else 1
                for h0 in range(0, HG, per):
                    out.append((i, range(h0, h0 + per), list(range(0, min(n, 4))), 0))
                    if n > 4:
                        out.append((i, range(h0, h0 + per), list(range(4, n)), 1))
        return out

    def exp_units(self, layer):
        out = []
        for c in range(2):
            unit = []
            for j in range(TPB):
                lo, hi = j, (TPB if layer else j + 2)
                lo, hi = max(lo, 4 * c), min(hi, 4 * c + 4)
                if lo < hi:
                    unit.append((j, (lo - 4 * c) * P, (hi - 4 * c) * P))
            out.append(unit)
        return out

    def attend(self, layer):
        nc = self.nc
        with ExitStack() as ctx:
            T = f"a{layer}_"
            SETS = 4
            sb = lambda n, s, t=F32: self.sb(ctx, T + n, s, t)
            sem = lambda n: self.sem(ctx, T + n)
            Ks = [sb(f"Ks{i}", [KAUG, HG, L], BF16) for i in range(SETS)]
            Qs = [sb(f"Qs{i}", [KAUG, HG, L], BF16) for i in range(SETS)]
            V4 = [sb(f"V4{i}", [P, TPB, HG, 2 * HD]) for i in range(SETS)]
            NP = 4
            probs = sb("probs", [P, NP, 2, HALF])
            mx = sb("mx", [P, 2, HG, TPB])
            nm = sb("nm", [P, HG * TPB])
            nmr = sb("nmr", [HG * TPB, P])
            nmp = sb("nmp", [HG * TPB, 3, P], BF16)
            oT = sb("oT", [P, HALF])
            rden = sb("rden", [P, 4, HG])
            pst = self.ps(ctx, T + "pst", [P, 4, 512])
            pmx = self.ps(ctx, T + "pmx", [P, 2, 512])
            pacc = self.ps(ctx, T + "pacc", [P, 512])
            pms = self.ps(ctx, T + "pms", [P, 512])
            ones_set = sem("ones_set")
            kq_in = [sem(f"kq_in{i}") for i in range(SETS)]
            max_in = [sem(f"max_in{i}") for i in range(SETS)]
            s_done, m_done, nm_ch, nm_ready, nmT_done, nmp_ready = (sem(n) for n in ("s_done", "m_done", "nm_ch", "nm_ready", "nmT_done", "nmp_ready"))
            st_done, exp_done, pv_done, acc_out, oT_done, norm_ch, norm_done = (sem(n) for n in ("st_done", "exp_done", "pv_done", "acc_out", "oT_done", "norm_ch", "norm_done"))
            nm_mid = sem("nm_mid")
            step_over = sem("step_over")
            maxu = self.max_units(layer)
            NM = len(maxu)
            halves = self.exp_units(layer)
            expu = [(c, k, j, q0, q1, pr) for c in range(2) for k, (j, q0, q1) in enumerate(halves[c]) for pr in range(2)]
            NE = len(expu)
            NV = NE // 2
            mask = self.causal if layer else self.window
            loads = 2 * SLOTS + 1
            SLOT_Q, SLOT_K = (0, 0, 0, 1, 1, 2), (0, 1, 2, 0, 1, 0)

            def load(sp, par, b, hg):
                pd = self.parts_d[layer]
                row = lambda base: bass.ds(hg * (HG * HD) + base, HG * HD)
                for dst, base, slots in ((Qs[par], 0, SLOT_Q), (Ks[par], D, SLOT_K)):
                    for s, part in enumerate(slots):
                        src = pd[part, row(base), bass.ds(b * L, L)].rearrange("(g e) n -> e g n", e=HD)
                        sp.dma_start(dst[s * HD:(s + 1) * HD, :, :], src).then_inc(kq_in[par], 16)
                vsrc = self.v_d[layer][bass.ds(b * L, L), bass.ds(hg * (HG * 2 * HD), HG * 2 * HD)].rearrange("(t p) n -> p t n", p=P)
                sp.dma_start(V4[par][:, :, :, :].rearrange("p t h e -> p t (h e)"), vsrc).then_inc(kq_in[par], 16)

            def send_max(sp, par, s):
                sp.wait_ge(nmp_ready, s + 1)
                for p in range(3):
                    sp.dma_start(Qs[par][KROWS + p:KROWS + p + 1, :, :].rearrange("a h (i q) -> a (h i) q", q=P), nmp[:, p, :]).then_inc(max_in[par], 16)

            def pe_max(pe, par, s, u):
                i, hs, ks, part = maxu[u]
                if u >= 2:
                    pe.wait_ge(m_done, NM * s + u - 1)
                cols = len(ks) * P
                for n, h in enumerate(hs):
                    o = n * cols
                    diag = i in ks
                    mm = nc.tensor.matmul(pmx[:, u % 2, o:o + cols], Qs[par][0:KROWS, h, i * P:(i + 1) * P],
                                          Ks[par][0:KROWS, h, ks[0] * P:ks[0] * P + cols], start=True, stop=not diag, skip_group_check=True)
                    if diag and layer:
                        mm = nc.tensor.matmul(pmx[:, u % 2, o + cols - P:o + cols], self.ident_bf[:, :], mask[:, 0, :], start=False, stop=True, skip_group_check=True)
                    elif diag:
                        mm = nc.tensor.matmul(pmx[:, u % 2, o:o + cols], self.ident_bf[:, :], mask[:, 0, 2 * P - cols:2 * P], start=False, stop=True, skip_group_check=True)
                mm.then_inc(s_done, 1)

            def pe_nmT(pe, s):
                pe.wait_ge(nm_ready, s + 1)
                nc.tensor.transpose(pms[0:HG * TPB, 0:P], nm[:, :], self.ident[:, :]).then_inc(nmT_done, 1)

            def pe_st(pe, par, s, u):
                c, k, j, q0, q1, pr = expu[u]
                if u >= 2:
                    pe.wait_ge(exp_done, NE * s + u - 1)
                for hh in range(2):
                    h = 2 * pr + hh
                    out = pst[:, 2 * (u % 2) + hh, :]
                    g0, g1 = c * HALF + q0, c * HALF + q1
                    diag = j * P - c * HALF if layer else q0
                    masked = (0 <= diag) if layer else True
                    mm = nc.tensor.matmul(out[:, q0:q1], Ks[par][:, h, j * P:(j + 1) * P], Qs[par][:, h, g0:g1], start=True, stop=not masked, skip_group_check=True)
                    if masked and layer:
                        mm = nc.tensor.matmul(out[:, diag:diag + P], self.ident_bf[:, :], mask[:, 1, :], start=False, stop=True, skip_group_check=True)
                    elif masked:
                        m0 = g0 - j * P
                        mm = nc.tensor.matmul(out[:, q0:q1], self.ident_bf[:, :], mask[:, 1, m0:m0 + q1 - q0], start=False, stop=True, skip_group_check=True)
                mm.then_inc(st_done, 1)

            def pe_pv(pe, par, s, v):
                c, k, j, q0, q1, _ = expu[2 * v]
                pe.wait_ge(exp_done, NE * s + 2 * v + 2)
                if k == 0 and v > 0:
                    pe.wait_ge(acc_out, 2 * s + 1)
                for h in range(HG):
                    mm = nc.tensor.matmul(pacc[32 * h:32 * h + 32, q0:q1], V4[par][:, j, h, :], probs[:, (2 * v + h // 2) % NP, h % 2, q0:q1],
                                          start=(k == 0), stop=(k == len(halves[c]) - 1), skip_group_check=True)
                mm.then_inc(pv_done, 1)

            def pe_oT(pe, s, c):
                pe.wait_ge(acc_out, 2 * s + c + 1)
                for t in range(4):
                    tr = nc.tensor.transpose(pms[:, t * P:(t + 1) * P], oT[:, t * P:(t + 1) * P], self.ident[:, :])
                tr.then_inc(oT_done, 1)

            seq = []
            for v in range(NV):
                seq += [("st", 2 * v), ("st", 2 * v + 1)]
                if v:
                    seq.append(("pv", v - 1))
                if v == len(halves[0]) + 1:
                    seq.append(("oT", 0))
            seq.append(("pv", NV - 1))
            m_end = len(seq) - 11 if layer else len(seq) - 9
            plan, m = [], 0
            for n, item in enumerate(seq):
                plan.append(item)
                while m < min(NM, (n + 1) * NM // m_end):
                    plan.append(("max", m))
                    m += 1
                if n == m_end + 1:
                    plan.append(("nmT", 0))
            plan.append(("oT", 1))
            assert m == NM and plan.index(("oT", 0)) < plan.index(("nmT", 0))

            def pe_body(pe, par, s, maxes):
                for kind, a in plan:
                    if kind == "st":
                        pe_st(pe, par, s, a)
                    elif kind == "pv":
                        pe_pv(pe, par, s, a)
                    elif kind == "oT":
                        pe.wait_ge(norm_done, 2 * s + a + 1)
                        if a == 1 and maxes:
                            pe.wait_ge(nmp_ready, s + 2)
                        pe_oT(pe, s, a)
                    elif maxes and kind == "max":
                        pe_max(pe, (par + 1) % SETS, s + 1, a)
                    elif maxes and kind == "nmT":
                        pe.wait_ge(norm_done, 2 * s + 2)
                        pe_nmT(pe, s + 1)

            def dve_max(dve, s, u):
                i, hs, ks, part = maxu[u]
                dve.wait_ge(s_done, NM * s + u + 1)
                cols = len(ks) * P
                src = pmx[:, u % 2, 0:len(hs) * cols].rearrange("p (h n) -> p h n", n=cols)
                nc.vector.tensor_reduce(mx[:, part, hs[0]:hs[0] + len(hs), i], src, AX.X, ALU.max).then_inc(m_done, 1)

            def dve_nm(dve, s):
                dve.wait_ge(m_done, NM * s + NM)
                if layer:
                    nc.vector.tensor_tensor(mx[:, 0, :, 4:8], mx[:, 0, :, 4:8], mx[:, 1, :, 4:8], ALU.max).then_inc(nm_ch, 1)
                    dve.wait_ge(nm_ch, 3 * s + 1)
                c0 = 3 * s + 1 if layer else 2 * s
                nc.vector.tensor_scalar(nm[:, :], mx[:, 0, :, :].rearrange("p h i -> p (h i)"), -1.0, None, ALU.mult).then_inc(nm_ready, 1)
                dve.wait_ge(nmT_done, s + 1)
                src = pms[0:HG * TPB, 0:P]
                nc.vector.tensor_copy(nmp[:, 0, :], src).then_inc(nm_ch, 1)
                dve.wait_ge(nm_ch, c0 + 1)
                nc.vector.tensor_tensor(nmr[:, :], src, nmp[:, 0, :], ALU.subtract).then_inc(nm_ch, 1)
                dve.wait_ge(nm_ch, c0 + 2)
                nc.vector.tensor_copy(nmp[:, 1, :], nmr[:, :]).then_inc(nm_mid, 1)
                dve.wait_ge(nm_mid, s + 1)
                nc.vector.tensor_tensor(nmp[:, 2, :], nmr[:, :], nmp[:, 1, :], ALU.subtract).then_inc(nmp_ready, 1)

            def dve_norm(dve, s, c, tile, col):
                dve.wait_ge(oT_done, 2 * s + c + 1)
                src = pms[:, :].rearrange("p (t h e) -> p t h e", t=4, e=2 * HD)
                nc.vector.reciprocal(rden[:, :, :], src[:, :, :, HD]).then_inc(norm_ch, 1)
                dve.wait_ge(norm_ch, 2 * s + c + 1)
                dst = self.attn[:, bass.ds(tile, 4), bass.ds(col, HG * HD)].rearrange("p t (h e) -> p t h e", e=HD)
                nc.vector.tensor_tensor(dst, src[:, :, :, 0:HD], rden[:, :, :].unsqueeze(3).broadcast_to([P, 4, HG, HD]), ALU.mult).then_inc(norm_done, 1)

            def dve_step(dve, s, tile, col, maxes):
                for kind, a in plan:
                    if kind == "oT":
                        dve_norm(dve, s, a, tile + 4 * a, col)
                    elif maxes and kind == "max":
                        dve_max(dve, s + 1, a)
                    elif maxes and kind == "nmT":
                        dve_nm(dve, s + 1)

            def act_step(act, s):
                for u, (c, k, j, q0, q1, pr) in enumerate(expu):
                    act.wait_ge(st_done, NE * s + u + 1)
                    if u >= NP:
                        act.wait_ge(pv_done, NV * s + (u - NP) // 2 + 1)
                    bank = 2 * (u % 2)
                    nc.scalar.activation(probs[:, u % NP, :, q0:q1], pst[:, bank:bank + 2, q0:q1], ACT.Exp, scale=HD ** -0.5).then_inc(exp_done, 1)
                    if u in (2 * len(halves[0]) + 1, NE - 1):
                        c_ = 0 if u < NE - 1 else 1
                        act.wait_ge(pv_done, NV * s + (len(halves[0]) if c_ == 0 else NV))
                        nc.scalar.activation(oT[:, :], pacc[:, :], ACT.Copy).then_inc(acc_out, 1)

            with nc.Block() as block:
                @block.gpsimd
                def _(pool):
                    for i in range(SETS):
                        pool.memset(Ks[i][KROWS:KAUG, :, :], 1.0).then_inc(ones_set, 1)

                @block.sync
                def _(sp):
                    for hg in range(SETS - 1):
                        load(sp, hg, 0, hg)
                    send_max(sp, 0, 0)
                    with sp.Fori(0, B - 1) as b:
                        for hg in range(SETS):
                            s = SETS * b + hg
                            if hg == 0:
                                load(sp, SETS - 1, b, SETS - 1)
                            else:
                                load(sp, hg - 1, b + 1, hg - 1)
                            send_max(sp, (hg + 1) % SETS, s + 1)
                            sp.wait_ge(pv_done, NV * s + NV)
                            sp.sem_inc(step_over, 1)
                    load(sp, SETS - 1, B - 1, SETS - 1)
                    for s in range(STEPS - SETS, STEPS - 1):
                        send_max(sp, (s + 1) % SETS, s + 1)

                @block.tensor
                def _(pe):
                    pe.wait_ge(ones_set, SETS)
                    pe.wait_ge(kq_in[0], 16 * loads)
                    for u in range(NM):
                        pe_max(pe, 0, 0, u)
                    pe_nmT(pe, 0)

                    def turn(b, last):
                        for hg in range(SETS):
                            pe.wait_ge(max_in[hg], 48 * b + 48)
                            nxt = (hg + 1) % SETS
                            maxes = not (last and nxt == 0)
                            if maxes:
                                pe.wait_ge(kq_in[nxt], 16 * loads * (b + (nxt == 0)) + 16 * loads)
                            pe_body(pe, hg, SETS * b + hg, maxes)

                    with pe.Fori(0, B - 1) as b:
                        turn(b, False)
                    turn(B - 1, True)

                @block.vector
                def _(dve):
                    for u in range(NM):
                        dve_max(dve, 0, u)
                    dve_nm(dve, 0)
                    dve.sem_inc(norm_done, 1)

                    def turn(b, last):
                        for hg in range(SETS):
                            dve_step(dve, SETS * b + hg, b * TPB, hg * (HG * HD), not (last and hg == SETS - 1))

                    with dve.Fori(0, B - 1) as b:
                        turn(b, False)
                    turn(B - 1, True)

                @block.scalar
                def _(act):
                    with act.Fori(0, B) as b:
                        for hg in range(SETS):
                            act_step(act, SETS * b + hg)

    def out_project(self, layer):
        nc, d = self.nc, self.dram
        with ExitStack() as ctx:
            T = f"o{layer}_"
            sb = lambda n, s, t=F32: self.sb(ctx, T + n, s, t)
            sem = lambda n: self.sem(ctx, T + n)
            wo = sb("wo", [P, DC, D])
            bo = sb("bo", [P, D])
            at = sb("at", [P, 2, D])
            aT = sb("aT", [P, 2, DC, P])
            y = sb("y", [P, 2, D])
            gate = sb("gate", [P, B, D])
            ptr = self.ps(ctx, T + "ptr", [P, 2, 512])
            py = self.ps(ctx, T + "py", [P, 2, 512])
            w_in, copied, tr_done, aT_ready, y_done, y_ch, x_done = (sem(n) for n in ("w_in", "copied", "tr_done", "aT_ready", "y_done", "y_ch", "x_done"))
            wname, bname = ("L0_attn_wo_wT", "L0_attn_wo_b") if layer == 0 else ("L1_attn_Wproj", "L1_attn_bproj")
            with nc.Block() as block:
                @block.sync
                def _(sp):
                    sp.dma_start(wo[:, :, :], d[wname].rearrange("(c p) n -> p c n", p=P)).then_inc(w_in, 16)
                    sp.dma_start(bo[:, :], d[bname].partition_broadcast(P)).then_inc(w_in, 16)
                    sp.dma_start(gate[:, :, :], self.mod_d[:, layer, 0, :, :]).then_inc(w_in, 16)

                @block.scalar
                def _(act):
                    with act.Fori(0, TILES // 2) as r:
                        for par in range(2):
                            t = 2 * r + par
                            nc.scalar.activation(at[:, par, :], self.attn[:, bass.ds(t, 1), :].rearrange("p a d -> p (a d)"), ACT.Copy).then_inc(copied, 1)
                            act.wait_ge(tr_done, t + 1)
                            nc.scalar.activation(aT[:, par, :, :].rearrange("p c n -> p (c n)"), ptr[:, par, 0:D], ACT.Copy).then_inc(aT_ready, 1)

                @block.tensor
                def _(pe):
                    pe.wait_ge(w_in, 48)
                    with pe.Fori(0, TILES // 2) as r:
                        for par in range(2):
                            t = 2 * r + par
                            pe.wait_ge(copied, t + 1)
                            for c in range(DC):
                                tr = nc.tensor.transpose(ptr[:, par, c * P:(c + 1) * P], at[:, par, c * P:(c + 1) * P], self.ident[:, :])
                            tr.then_inc(tr_done, 1)
                            pe.wait_ge(aT_ready, t + 1)
                            pe.wait_ge(x_done, t + 1)
                            for c in range(DC):
                                mm = nc.tensor.matmul(py[:, par, 0:D], aT[:, par, c, :], wo[:, c, :], start=(c == 0), stop=(c == DC - 1))
                            mm.then_inc(y_done, 1)

                @block.vector
                def _(dve):
                    dve.wait_ge(w_in, 48)
                    dve.sem_inc(x_done, 2)
                    with dve.Fori(0, B) as b:
                        with dve.Fori(0, TPB // 2) as r:
                            for par in range(2):
                                t = b * TPB + 2 * r + par
                                dve.wait_ge(y_done, t + 1)
                                nc.vector.tensor_tensor(y[:, par, :], py[:, par, 0:D], bo[:, :], ALU.add).then_inc(y_ch, 1)
                                dve.wait_ge(y_ch, 2 * t + 1)
                                ga = gate[:, bass.ds(b, 1), :].rearrange("p a d -> p (a d)")
                                nc.vector.tensor_tensor(y[:, par, :], y[:, par, :], ga, ALU.mult).then_inc(y_ch, 1)
                                dve.wait_ge(y_ch, 2 * t + 2)
                                xt = self.x[:, bass.ds(t, 1), :].rearrange("p a d -> p (a d)")
                                nc.vector.tensor_tensor(xt, xt, y[:, par, :], ALU.add).then_inc(x_done, 1)

    def moe(self, layer):
        nc = self.nc
        with ExitStack() as ctx:
            T = f"m{layer}_"
            self.T = T
            self.H = 1024 if layer == 0 else 512
            self.NH = self.H // P
            NH = self.NH
            self.w1 = self.sb(ctx, T + "w1", [P, EXPERTS, DC, 2, self.H], F16)
            self.w2 = self.sb(ctx, T + "w2", [P, EXPERTS, NH, 2, D], F16)
            self.s1 = self.sb(ctx, T + "s1", [P, EXPERTS, NH])
            self.b1 = self.sb(ctx, T + "b1", [P, EXPERTS, NH])
            self.gw = self.sb(ctx, T + "gw", [P, DC, EXPERTS])
            self.gs = self.sb(ctx, T + "gs", [P, EXPERTS])
            self.gb = self.sb(ctx, T + "gb", [P, EXPERTS])
            self.slot = self.sb(ctx, T + "slot", [P, 2, TILES], U32)
            self.wt = self.sb(ctx, T + "wt", [P, 2, TILES])
            self.owner = self.sb(ctx, T + "owner", [P, XT], I32)
            self.xs_d = nc.dram_tensor(T + "xs_d", (XT * ROWS, 2 * D), F16, kind="Internal").ap()
            self.ys_d = nc.dram_tensor(T + "ys_d", (XT * ROWS, D), F32, kind="Internal").ap()
            self.moe_weights(layer)
            with ExitStack() as inner:
                self.zh = self.sb(inner, T + "zh", [P, TILES, 2, D], F16)
                self.lg = self.sb(inner, T + "lg", [P, TILES, EXPERTS])
                self.moe_input(layer)
                self.moe_route(layer)
                self.moe_scatter(layer)
            self.moe_tiles(layer)
            self.moe_combine(layer)

    def moe_weights(self, layer):
        nc, d, T, H, NH = self.nc, self.dram, self.T, self.H, self.NH
        normed = layer == 0
        w1_src = d["L0_w1T"] if normed else d["L1_ffn_W1"]
        w2_src = d["L0_w2T"] if normed else d["L1_ffn_W2"]
        with ExitStack() as ctx:
            sb = lambda n, s, t=F32: self.sb(ctx, T + n, s, t)
            sem = lambda n: self.sem(ctx, T + n)
            st1 = sb("st1", [P, DC, H])
            st2 = sb("st2", [P, NH, D])
            sq = sb("sq", [P, 2048])
            rt = sb("rt", [P, D])
            g2 = sb("g2", [P, D])
            ones = sb("ones", [P, P])
            g1 = sb("g1", [P, EXPERTS, NH])
            gg = sb("gg", [P, EXPERTS])
            zero = sb("zero", [P, 2 * D], F16)
            pss = self.ps(ctx, T + "pss", [P, 512])
            pbc = self.ps(ctx, T + "pbc", [P, 512])
            pgs = self.ps(ctx, T + "pgs", [P, 512])
            small_in, w1_in, w2_in, g2_in, ones_set = (sem(n) for n in ("small_in", "w1_in", "w2_in", "g2_in", "ones_set"))
            sq1, ss1, sq2, ss2, root, w2_scaled, hi1, lo1, hi2, lo2, ch, gsq, gss, groot, zeroed = (
                sem(n) for n in ("sq1", "ss1", "sq2", "ss2", "root", "w2_scaled", "hi1", "lo1", "hi2", "lo2", "wch", "gsq", "gss", "groot", "zeroed"))
            zero_out, sqrt1_done = self.zero_out, sem("sqrt1_done")
            smalls = 16 * (5 if normed else 3)
            with nc.Block() as block:
                @block.sync
                def _(sp):
                    sp.dma_start(self.b1[:, :, :], d[f"L{layer}_b1c"]).then_inc(small_in, 16)
                    sp.dma_start(self.gw[:, :, :], d["L0_gateT" if normed else "L1_ffn_rW"].rearrange("(c p) e -> p c e", p=P)).then_inc(small_in, 16)
                    sp.dma_start(self.gb[:, :], d["L0_ffn_gate_b" if normed else "L1_ffn_rb"].partition_broadcast(P)).then_inc(small_in, 16)
                    if normed:
                        sp.dma_start(g1[:, :, :], d["L0_g1c"]).then_inc(small_in, 16)
                        sp.dma_start(gg[:, :], d["L0_ffn_gate_g"].partition_broadcast(P)).then_inc(small_in, 16)
                    sp.sem_inc(lo1, 1)
                    sp.sem_inc(lo2, 1)
                    with sp.Fori(0, EXPERTS) as e:
                        sp.wait_ge(lo1, e + 1)
                        sp.dma_start(st1[:, :, :], w1_src[bass.ds(e, 1), :, :].rearrange("a (c p) n -> p (a c) n", p=P)).then_inc(w1_in, 16)
                        sp.wait_ge(lo2, e + 1)
                        sp.dma_start(st2[:, :, :], w2_src[bass.ds(e, 1), :, :].rearrange("a (c p) n -> p (a c) n", p=P)).then_inc(w2_in, 16)
                        if normed:
                            sp.dma_start(g2[:, :], d["L0_ffn_w2_g"][bass.ds(e, 1), :].rearrange("a n -> (a n)").partition_broadcast(P)).then_inc(g2_in, 16)

                @block.gpsimd
                def _(pool):
                    pool.memset(ones[:, :], 1.0).then_inc(ones_set, 1)
                    pool.memset(zero[:, :], 0.0).then_inc(zeroed, 1)
                    pool.wait_ge(zeroed, 1)
                    A = 16
                    for j in range(XT * ROWS // (A * P)):
                        dst = self.xs_d[j * A * P:(j + 1) * A * P, :].rearrange("(a p) n -> p a n", p=P)
                        pool.dma_start(dst, zero[:, :].unsqueeze(1).broadcast_to([P, A, 2 * D])).then_inc(zero_out, 16)
                    pool.wait_ge(zero_out, 16 * (XT * ROWS // (A * P)) * (layer + 1))

                @block.scalar
                def _(act):
                    if normed:
                        act.wait_ge(small_in, smalls)
                        nc.scalar.activation(sq[:, 0:DC * EXPERTS], self.gw[:, :, :].rearrange("p c e -> p (c e)"), ACT.Square).then_inc(gsq, 1)
                        act.wait_ge(gss, 1)
                        nc.scalar.activation(self.gs[:, :], pgs[:, 0:EXPERTS], ACT.Sqrt).then_inc(groot, 1)
                    with act.Fori(0, EXPERTS) as e:
                        act.wait_ge(w1_in, 16 * e + 16)
                        if normed:
                            nc.scalar.activation(sq[:, :], st1[:, :, :].rearrange("p c n -> p (c n)"), ACT.Square).then_inc(sq1, 1)
                        nc.scalar.activation(self.w1[:, bass.ds(e, 1), :, 0, :].rearrange("p a c n -> p (a c) n"), st1[:, :, :], ACT.Copy).then_inc(hi1, 1)
                        act.wait_ge(w2_in, 16 * e + 16)
                        if normed:
                            act.wait_ge(ss1, e + 1)
                            nc.scalar.activation(sq[:, :], st2[:, :, :].rearrange("p c n -> p (c n)"), ACT.Square).then_inc(sq2, 1)
                            act.wait_ge(ss2, e + 1)
                            nc.scalar.activation(rt[:, :], pbc[:, 0:D], ACT.Sqrt).then_inc(root, 1)
                            act.wait_ge(w2_scaled, e + 1)
                        nc.scalar.activation(self.w2[:, bass.ds(e, 1), :, 0, :].rearrange("p a c n -> p (a c) n"), st2[:, :, :], ACT.Copy).then_inc(hi2, 1)
                    if normed:
                        act.wait_ge(ss1, EXPERTS)
                        nc.scalar.activation(self.s1[:, :, :].rearrange("p e m -> p (e m)"), pss[:, 0:EXPERTS * NH], ACT.Sqrt).then_inc(sqrt1_done, 1)

                @block.tensor
                def _(pe):
                    if not normed:
                        return
                    pe.wait_ge(ones_set, 1)
                    pe.wait_ge(gsq, 1)
                    for c in range(DC):
                        mm = nc.tensor.matmul(pgs[:, 0:EXPERTS], ones[:, :], sq[:, c * EXPERTS:(c + 1) * EXPERTS], start=(c == 0), stop=(c == DC - 1))
                    mm.then_inc(gss, 1)
                    with pe.Fori(0, EXPERTS) as e:
                        pe.wait_ge(sq1, e + 1)
                        for m in range(NH):
                            for c in range(DC):
                                mm = nc.tensor.matmul(pss[:, bass.ds(e * NH + m, 1)], sq[:, c * H + m * P:c * H + m * P + P], ones[:, 0:1],
                                                      start=(c == 0), stop=(c == DC - 1), skip_group_check=True)
                        mm.then_inc(ss1, 1)
                        pe.wait_ge(sq2, e + 1)
                        for m in range(NH):
                            mm = nc.tensor.matmul(pbc[:, 0:D], ones[:, :], sq[:, m * D:(m + 1) * D], start=(m == 0), stop=(m == NH - 1))
                        mm.then_inc(ss2, 1)

                @block.vector
                def _(dve):
                    n = [0]

                    def link(ins):
                        n[0] += 1
                        ins.then_inc(ch, 1)
                        dve.wait_ge(ch, n[0])

                    dve.wait_ge(small_in, smalls)
                    if normed:
                        dve.wait_ge(groot, 1)
                        link(nc.vector.tensor_scalar(self.gs[:, :], self.gs[:, :], 1e-12, None, ALU.max))
                        link(nc.vector.reciprocal(self.gs[:, :], self.gs[:, :]))
                        link(nc.vector.tensor_tensor(self.gs[:, :], self.gs[:, :], gg[:, :], ALU.mult))
                    n0 = n[0]
                    with dve.Fori(0, EXPERTS) as e:
                        dve.wait_ge(hi1, e + 1)
                        w1e = lambda w: self.w1[:, bass.ds(e, 1), :, w, :].rearrange("p a c n -> p (a c) n")
                        w2e = lambda w: self.w2[:, bass.ds(e, 1), :, w, :].rearrange("p a c n -> p (a c) n")
                        nc.vector.tensor_tensor(w1e(1), st1[:, :, :], w1e(0), ALU.subtract).then_inc(lo1, 1)
                        if normed:
                            dve.wait_ge(root, e + 1)
                            nc.vector.tensor_scalar(rt[:, :], rt[:, :], 1e-12, None, ALU.max).then_inc(ch, 1)
                            dve.wait_ge(ch, n0 + 3 * e + 1)
                            nc.vector.reciprocal(rt[:, :], rt[:, :]).then_inc(ch, 1)
                            dve.wait_ge(ch, n0 + 3 * e + 2)
                            dve.wait_ge(g2_in, 16 * e + 16)
                            nc.vector.tensor_tensor(rt[:, :], rt[:, :], g2[:, :], ALU.mult).then_inc(ch, 1)
                            dve.wait_ge(ch, n0 + 3 * e + 3)
                            nc.vector.tensor_tensor(st2[:, :, :], st2[:, :, :], rt[:, :].unsqueeze(1).broadcast_to([P, NH, D]), ALU.mult).then_inc(w2_scaled, 1)
                        dve.wait_ge(hi2, e + 1)
                        nc.vector.tensor_tensor(w2e(1), st2[:, :, :], w2e(0), ALU.subtract).then_inc(lo2, 1)
                    if normed:
                        n[0] += 3 * EXPERTS
                        dve.wait_ge(sqrt1_done, 1)
                        s1 = self.s1[:, :, :]
                        link(nc.vector.tensor_scalar(s1, s1, 1e-12, None, ALU.max))
                        link(nc.vector.reciprocal(s1, s1))
                        link(nc.vector.tensor_tensor(s1, s1, g1[:, :, :], ALU.mult))

    def moe_input(self, layer):
        nc, d, T = self.nc, self.dram, self.T
        twice = layer == 1
        with ExitStack() as ctx:
            sb = lambda n, s, t=F32: self.sb(ctx, T + n, s, t)
            sem = lambda n: self.sem(ctx, T + n)
            rows = sb("rows", [P, 3 if twice else 2, D])
            lnr = sb("lnr", [P, 2, D]) if twice else None
            stats = sb("stats", [P, HT, nc.vector.BN_STATS_DIM])
            mv = sb("mv", [P, HT, 2])
            sd = sb("sd", [P, HT])
            rstd = sb("rstd", [P, HT])
            eps = sb("eps", [P, 1])
            z = sb("z", [P, HT, D])
            zT = sb("zT", [P, 2, DC, P])
            lt = sb("lt", [P, HT, EXPERTS])
            gh = sb("gh", [P, HT, D]) if twice else None
            ptr = self.ps(ctx, T + "ptr", [P, 2, 512])
            plg = self.ps(ctx, T + "plg", [P, 512])
            rows_in, lnr_in, eps_set, ch, var_ready, sd_ready, z_ready, tr_done, zT_ready, lg_done, lg_out, hi_done, lo_done = (
                sem(n) for n in ("rows_in", "lnr_in", "eps_set", "ich", "var_ready", "sd_ready", "z_ready", "tr_done", "zT_ready", "lg_done", "lg_out", "hi_done", "lo_done"))
            stats_seen = sem("stats_seen")
            NORMS = 2 if twice else 1
            ROWS_IN = 48 if twice else 32
            K = 2 * (3 * HT + 1) + 5 if twice else 3 * HT + 1 + 2
            with nc.Block() as block:
                @block.gpsimd
                def _(pool):
                    pool.memset(eps[:, :], EPS).then_inc(eps_set, 1)

                @block.sync
                def _(sp):
                    if twice:
                        sp.dma_start(lnr[:, 0, :], d["L1_ffn_ln_g"].partition_broadcast(P)).then_inc(lnr_in, 16)
                        sp.dma_start(lnr[:, 1, :], d["L1_ffn_ln_b"].partition_broadcast(P)).then_inc(lnr_in, 16)
                    sp.sem_inc(lo_done, 1)
                    with sp.Fori(0, B) as b:
                        sp.wait_ge(lo_done, 2 * b + 1)
                        for j, kind in enumerate((2, 3, 1) if twice else (2, 3)):
                            sp.dma_start(rows[:, j, :], self.mod_d[:, layer, kind, bass.ds(b, 1), :].rearrange("p a d -> p (a d)")).then_inc(rows_in, 16)

                @block.scalar
                def _(act):
                    act.wait_ge(eps_set, 1)
                    with act.Fori(0, 2 * B) as n:
                        for k in range(NORMS):
                            act.wait_ge(var_ready, NORMS * n + k + 1)
                            nc.scalar.activation(sd[:, :], mv[:, :, 1], ACT.Sqrt, bias=eps[:, :]).then_inc(sd_ready, 1)
                        act.wait_ge(z_ready, n + 1)
                        nc.scalar.activation(self.zh[:, bass.ds(HT * n, HT), 0, :], z[:, :, :], ACT.Copy).then_inc(hi_done, 1)
                        for t in range(HT):
                            act.wait_ge(tr_done, HT * n + t + 1)
                            nc.scalar.activation(zT[:, t % 2, :, :], ptr[:, t % 2, 0:D].rearrange("p (c n) -> p c n", c=DC), ACT.Copy).then_inc(zT_ready, 1)

                @block.tensor
                def _(pe):
                    with pe.Fori(0, 2 * B) as n:
                        pe.wait_ge(z_ready, n + 1)
                        for t in range(HT + 1):
                            if t < HT:
                                for c in range(DC):
                                    tr = nc.tensor.transpose(ptr[:, t % 2, c * P:(c + 1) * P], z[:, t, c * P:(c + 1) * P], self.ident[:, :])
                                tr.then_inc(tr_done, 1)
                            if t >= 1:
                                pe.wait_ge(zT_ready, HT * n + t)
                                for c in range(DC):
                                    mm = nc.tensor.matmul(plg[:, (t - 1) * EXPERTS:t * EXPERTS], zT[:, (t - 1) % 2, c, :], self.gw[:, c, :],
                                                          start=(c == 0), stop=(c == DC - 1), skip_group_check=True)
                        mm.then_inc(lg_done, 1)

                @block.vector
                def _(dve):
                    if twice:
                        dve.wait_ge(lnr_in, 32)
                    with dve.Fori(0, B) as b:
                        dve.wait_ge(rows_in, ROWS_IN * (b + 1))
                        for half in range(2):
                            n = 2 * b + half
                            cnt = [0]

                            def step(ins, wait=True):
                                cnt[0] += 1
                                ins.then_inc(ch, 1)
                                if wait:
                                    dve.wait_ge(ch, K * n + cnt[0])

                            xh = self.x[:, bass.ds(TPB * b + HT * half, HT), :]
                            row = lambda j, src=rows: src[:, j, :].unsqueeze(1).broadcast_to([P, HT, D])

                            def norm(k, src):
                                for t in range(HT):
                                    step(nc.vector.bn_stats(stats[:, t, :], src(t)), t == HT - 1)
                                dve.sem_inc(stats_seen, 1)
                                for t in range(HT):
                                    ins = nc.vector.bn_aggr(mv[:, t, :], stats[:, t, :])
                                    step(ins, t == HT - 1)
                                dve.sem_inc(var_ready, 1)
                                dve.wait_ge(sd_ready, NORMS * n + k + 1)
                                step(nc.vector.reciprocal(rstd[:, :], sd[:, :]))
                                for t in range(HT):
                                    step(nc.vector.tensor_scalar(z[:, t, :], src(t), mv[:, t, 0:1], rstd[:, t:t + 1], ALU.subtract, ALU.mult), t == HT - 1)

                            norm(0, lambda t: self.x[:, bass.ds(TPB * b + HT * half + t, 1), :].rearrange("p a d -> p (a d)"))
                            step(nc.vector.tensor_tensor(z[:, :, :], z[:, :, :], row(1), ALU.mult))
                            if not twice:
                                nc.vector.tensor_tensor(z[:, :, :], z[:, :, :], row(0), ALU.add).then_inc(z_ready, 1)
                                dve.wait_ge(z_ready, n + 1)
                            else:
                                step(nc.vector.tensor_tensor(z[:, :, :], z[:, :, :], row(0), ALU.add))
                                step(nc.vector.tensor_tensor(gh[:, :, :], z[:, :, :], row(2), ALU.mult))
                                step(nc.vector.tensor_tensor(xh, xh, gh[:, :, :], ALU.add))
                                norm(1, lambda t: z[:, t, :])
                                step(nc.vector.tensor_tensor(z[:, :, :], z[:, :, :], row(0, lnr), ALU.mult))
                                nc.vector.tensor_tensor(z[:, :, :], z[:, :, :], row(1, lnr), ALU.add).then_inc(z_ready, 1)
                                dve.wait_ge(z_ready, n + 1)
                            dve.wait_ge(hi_done, n + 1)
                            nc.vector.tensor_tensor(self.zh[:, bass.ds(TPB * b + HT * half, HT), 1, :], z[:, :, :],
                                                    self.zh[:, bass.ds(TPB * b + HT * half, HT), 0, :], ALU.subtract).then_inc(lo_done, 1)
                            dve.wait_ge(lg_done, n + 1)
                            out = self.lg[:, bass.ds(TPB * b + HT * half, HT), :]
                            src = plg[:, 0:HT * EXPERTS].rearrange("p (t e) -> p t e", e=EXPERTS)
                            erow = lambda a: a[:, :].unsqueeze(1).broadcast_to([P, HT, EXPERTS])
                            if not twice:
                                step(nc.vector.tensor_tensor(lt[:, :, :], src, erow(self.gs), ALU.mult))
                                nc.vector.tensor_tensor(out, lt[:, :, :], erow(self.gb), ALU.add).then_inc(lg_out, 1)
                            else:
                                nc.vector.tensor_tensor(out, src, erow(self.gb), ALU.add).then_inc(lg_out, 1)
                            assert cnt[0] == K

    def moe_route(self, layer):
        nc, d, T = self.nc, self.dram, self.T
        TE = TILES * EXPERTS
        with ExitStack() as ctx:
            sb = lambda n, s, t=F32: self.sb(ctx, T + n, s, t)
            sem = lambda n: self.sem(ctx, T + n)
            iota = sb("iota", [P, 64])
            low = sb("low", [P, P])
            ones = sb("rones", [P, TE])
            te = {n: sb("te_" + n, [P, TILES, EXPERTS]) for n in ("eq", "oh1", "oh2", "mask")}
            et = {n: sb("et_" + n, [P, EXPERTS, TILES]) for n in ("cnt", "sum", "slot")}
            best = sb("best", [P, 2, TILES])
            at = sb("at", [P, TILES])
            i99 = sb("i99", [P, EXPERTS])
            e8 = {n: sb("e8_" + n, [P, EXPERTS]) for n in ("prev", "n", "incl", "base")}
            M = N_TOK // ROWS
            work = sb("work", [P, max(TE, XT * (EXPERTS - 1))])
            te["tmp"] = work[:, 0:TE].rearrange("p (t e) -> p t e", e=EXPERTS)
            cmp16 = work[:, 0:EXPERTS * M].rearrange("p (e m) -> p e m", m=M)
            cmpj = work[:, 0:XT * (EXPERTS - 1)].rearrange("p (j e) -> p j e", e=EXPERTS - 1)
            thr = sb("thr", [P, N_TOK // ROWS])
            fl = sb("fl", [P, 2, TILES])
            oj = et["cnt"][:, :, :].rearrange("p e t -> p (e t)")[:, 0:XT]
            pw = self.ps(ctx, T + "pw", [P, 512])
            pc = self.ps(ctx, T + "pc", [P, 512])
            const_in, ones_set, mask_ready, sums, ch, shifted, ex_ready = (sem(n) for n in ("const_in", "rones_set", "mask_ready", "sums", "rch", "shifted", "ex_ready"))
            with nc.Block() as block:
                @block.sync
                def _(sp):
                    sp.dma_start(iota[:, :], d["c_iota"]).then_inc(const_in, 16)
                    sp.dma_start(low[:, :], d["c_before"]).then_inc(const_in, 16)

                @block.gpsimd
                def _(pool):
                    pool.memset(ones[:, :], 1.0).then_inc(ones_set, 1)

                @block.scalar
                def _(act):
                    if layer == 1:
                        act.wait_ge(shifted, 1)
                        nc.scalar.activation(te["tmp"][:, :, :], te["tmp"][:, :, :], ACT.Exp).then_inc(ex_ready, 1)

                @block.tensor
                def _(pe):
                    pe.wait_ge(const_in, 32)
                    pe.wait_ge(ones_set, 1)
                    pe.wait_ge(mask_ready, 1)
                    mask = te["mask"][:, :, :].rearrange("p t e -> p e t")
                    nc.tensor.matmul(pw[:, 0:TE], low[:, :], mask, start=True, stop=True)
                    nc.tensor.matmul(pc[:, 0:TE], ones[:, 0:P], mask, start=True, stop=True).then_inc(sums, 1)

                @block.vector
                def _(dve):
                    n = [0]

                    def link(ins):
                        n[0] += 1
                        ins.then_inc(ch, 1)
                        dve.wait_ge(ch, n[0])

                    tt, ts = nc.vector.tensor_tensor, nc.vector.tensor_scalar
                    lg = self.lg[:, :, :]
                    eq, oh1, oh2, mask, tmp = (te[k][:, :, :] for k in ("eq", "oh1", "oh2", "mask", "tmp"))
                    over_e = lambda a: a.unsqueeze(2).broadcast_to([P, TILES, EXPERTS])
                    over_t = lambda a: a.unsqueeze(1).broadcast_to([P, TILES, EXPERTS])
                    dve.wait_ge(const_in, 32)
                    dve.wait_ge(ones_set, 1)
                    link(ts(i99[:, :], iota[:, 0:EXPERTS], -99.0, None, ALU.add))

                    def choose(src, k, oh):
                        link(nc.vector.tensor_reduce(best[:, k, :], src, AX.X, ALU.max))
                        link(tt(eq, src, over_e(best[:, k, :]), ALU.is_equal))
                        link(tt(eq, eq, over_t(i99[:, :]), ALU.mult))
                        link(nc.vector.tensor_reduce(at[:, :], eq, AX.X, ALU.min))
                        link(tt(oh, over_t(i99[:, :]), over_e(at[:, :]), ALU.is_equal))

                    choose(lg, 0, oh1)
                    link(nc.vector.scalar_tensor_tensor(out=tmp, in0=oh1, scalar=-1e38, in1=lg, op0=ALU.mult, op1=ALU.add))
                    choose(tmp, 1, oh2)
                    tt(mask, oh1, oh2, ALU.add).then_inc(mask_ready, 1)
                    if layer == 1:
                        tt(tmp, lg, over_e(best[:, 0, :]), ALU.subtract).then_inc(shifted, 1)
                        dve.wait_ge(ex_ready, 1)
                        link(nc.vector.tensor_reduce(at[:, :], tmp, AX.X, ALU.add))
                        link(nc.vector.reciprocal(at[:, :], at[:, :]))
                        link(tt(tmp, tmp, over_e(at[:, :]), ALU.mult))
                        for k, oh in enumerate((oh1, oh2)):
                            link(tt(eq, tmp, oh, ALU.mult))
                            link(nc.vector.tensor_reduce(self.wt[:, k, :], eq, AX.X, ALU.add))
                        link(tt(at[:, :], self.wt[:, 0, :], self.wt[:, 1, :], ALU.add))
                        link(ts(at[:, :], at[:, :], 1e-8, None, ALU.max))
                        link(nc.vector.reciprocal(at[:, :], at[:, :]))
                        link(tt(self.wt[:, :, :], self.wt[:, :, :], at[:, :].unsqueeze(1).broadcast_to([P, 2, TILES]), ALU.mult))
                    dve.wait_ge(sums, 1)
                    cnt, tot, slot = (et[k][:, :, :] for k in ("cnt", "sum", "slot"))
                    flat = lambda a: a.rearrange("p e t -> p (e t)")
                    prev, ne, incl, base = (e8[k][:, :] for k in ("prev", "n", "incl", "base"))
                    link(nc.vector.tensor_copy(flat(cnt), pc[:, 0:TE]))
                    link(nc.vector.tensor_tensor_scan(flat(tot), ones[:, 0:TE], flat(cnt), 0.0, ALU.mult, ALU.add))
                    link(nc.vector.memset(prev, 0.0))
                    link(nc.vector.tensor_copy(e8["prev"][:, 1:EXPERTS], et["sum"][:, 0:EXPERTS - 1, TILES - 1]))
                    link(tt(ne, et["sum"][:, :, TILES - 1], prev, ALU.subtract))
                    link(ts(thr[:, :], iota[:, 0:M], float(ROWS), None, ALU.mult))
                    link(tt(cmp16[:, :, :], ne.unsqueeze(2).broadcast_to([P, EXPERTS, M]), thr[:, :].unsqueeze(1).broadcast_to([P, EXPERTS, M]), ALU.is_gt))
                    link(nc.vector.tensor_reduce(ne, cmp16[:, :, :], AX.X, ALU.add))
                    link(nc.vector.tensor_tensor_scan(incl, ones[:, 0:EXPERTS], ne, 0.0, ALU.mult, ALU.add))
                    link(tt(base, incl, ne, ALU.subtract))
                    link(nc.vector.scalar_tensor_tensor(out=base, in0=base, scalar=float(ROWS), in1=prev, op0=ALU.mult, op1=ALU.subtract))
                    link(tt(slot, tot, cnt, ALU.subtract))
                    link(tt(slot, slot, base.unsqueeze(2).broadcast_to([P, EXPERTS, TILES]), ALU.add))
                    link(tt(flat(slot), flat(slot), pw[:, 0:TE], ALU.add))
                    for k, oh in enumerate((oh1, oh2)):
                        link(tt(eq, oh, slot.rearrange("p e t -> p t e"), ALU.mult))
                        link(nc.vector.tensor_reduce(fl[:, k, :], eq, AX.X, ALU.add))
                    link(nc.vector.tensor_copy(self.slot[:, :, :], fl[:, :, :]))
                    E1 = EXPERTS - 1
                    link(tt(cmpj[:, :, :], e8["incl"][:, 0:E1].unsqueeze(1).broadcast_to([P, XT, E1]), iota[:, 0:XT].unsqueeze(2).broadcast_to([P, XT, E1]), ALU.is_le))
                    link(nc.vector.tensor_reduce(oj, cmpj[:, :, :], AX.X, ALU.add))
                    link(nc.vector.tensor_copy(self.owner[:, :], oj))

    def moe_scatter(self, layer):
        nc, T = self.nc, self.T
        with ExitStack() as ctx:
            sent = self.sent
            with nc.Block() as block:
                @block.gpsimd
                def _(pool):
                    for t in range(TILES):
                        for k in range(2):
                            pool.indirect_dma_start(self.xs_d[:, :], bass.IndirectOffsetOnAxis(ap=self.slot[:, k, t:t + 1], axis=0),
                                                    self.zh[:, t, :, :].rearrange("p a d -> p (a d)"), None).then_inc(sent[k], 16)
                    for k in range(2):
                        pool.wait_ge(sent[k], 16 * TILES * (layer + 1))

    def moe_tiles(self, layer):
        nc, d, T, H, NH = self.nc, self.dram, self.T, self.H, self.NH
        func = ACT.Silu if layer == 0 else ACT.Gelu
        PAIRS = ((0, 0), (0, 1), (1, 0))
        with ExitStack() as ctx:
            sb = lambda n, s, t=F32: self.sb(ctx, T + n, s, t)
            sem = lambda n: self.sem(ctx, T + n)
            b2 = sb("b2", [P, EXPERTS, D])
            xr = sb("xr", [P, 2, 2, 2 * D], F16)
            xT = sb("xT", [P, 2, 2, DC, ROWS], F16)
            hf = sb("hf", [P, 2, 2, ROWS])
            hh = sb("hh", [P, 2, NH, 2, ROWS], F16)
            y = sb("y", [P, 2, 2, D])
            pt = self.ps(ctx, T + "pt", [P, 2, 1024], F16)
            ph = self.ps(ctx, T + "ph", [P, 4, 512])
            py = self.ps(ctx, T + "py", [P, 2, 512])
            b2_in, tr_done, xT_ready, h_done, act_done, hi_done, lo_done, y_done, y_taken = (
                sem(n) for n in ("b2_in", "ttr_done", "xT_ready", "h_done", "act_done", "thi_done", "tlo_done", "y_done", "y_taken"))
            x_in = [sem(f"x_in{i}") for i in range(2)]
            y_out = [sem(f"y_out{i}") for i in range(2)]
            G = NH // 2
            with nc.Block() as block:
                @block.sync
                def _(sp):
                    sp.dma_start(b2[:, :, :], d[f"L{layer}_ffn_b2"].rearrange("e n -> (e n)").partition_broadcast(P).rearrange("p (e n) -> p e n", e=EXPERTS)).then_inc(b2_in, 16)
                    for par in range(2):
                        sp.sem_inc(y_out[par], 16)
                        sp.dma_start(xr[:, par, :, :], self.xs_d[par * ROWS:(par + 1) * ROWS, :].rearrange("(a p) n -> p a n", p=P)).then_inc(x_in[par], 16)

                    def turn(j, par, more):
                        if more:
                            sp.wait_ge(tr_done, j + 1)
                            sp.dma_start(xr[:, par, :, :], self.xs_d[bass.ds((j + 2) * ROWS, ROWS), :].rearrange("(a p) n -> p a n", p=P)).then_inc(x_in[par], 16)
                        sp.wait_ge(y_taken, 2 * j + 4)
                        sp.dma_start(self.ys_d[bass.ds(j * ROWS, ROWS), :].rearrange("(a p) n -> p a n", p=P), y[:, par, :, :]).then_inc(y_out[par], 16)

                    with sp.Fori(0, XT // 2 - 1) as r:
                        for par in range(2):
                            turn(2 * r + par, par, True)
                    for par in range(2):
                        turn(XT - 2 + par, par, False)
                        sp.wait_ge(y_out[par], 16 * (XT // 2) + 16)

                @block.tensor
                def _(pe):
                    def first(j, par, n_in):
                        e = nc.tensor.value_load(self.owner[0:1, bass.ds(j, 1)], min_val=0, max_val=EXPERTS - 1)
                        pe.wait_ge(x_in[par], n_in)
                        for hl in range(2):
                            for c in range(DC):
                                for a in range(2):
                                    o = ((hl * DC + c) * 2 + a) * P
                                    tr = nc.tensor.transpose(pt[:, par, o:o + P], xr[:, par, a, hl * D + c * P:hl * D + (c + 1) * P], self.ident_h[:, :])
                        tr.then_inc(tr_done, 1)
                        pe.wait_ge(xT_ready, j + 1)
                        for m in range(NH):
                            g, q = m // 2, m % 2
                            if q == 0:
                                pe.wait_ge(act_done, NH * j + m + 2)
                            for c in range(DC):
                                for i, (wp, xp) in enumerate(PAIRS):
                                    mm = nc.tensor.matmul(ph[:, (G * par + g) % 4, q * ROWS:(q + 1) * ROWS], self.w1[:, bass.ds(e, 1), c, wp, m * P:(m + 1) * P].rearrange("p a n -> p (a n)"),
                                                          xT[:, par, xp, c, :], start=(c == 0 and i == 0), stop=(c == DC - 1 and i == 2), skip_group_check=True)
                            mm.then_inc(h_done, 1)

                    def second(j, par):
                        e = nc.tensor.value_load(self.owner[0:1, bass.ds(j, 1)], min_val=0, max_val=EXPERTS - 1)
                        for a in range(2):
                            pe.wait_ge(y_taken, 2 * j + a + 1)
                            for m in range(NH):
                                if a == 0 and m % 2 == 0:
                                    pe.wait_ge(lo_done, G * j + m // 2 + 3)
                                for i, (wp, hp) in enumerate(PAIRS):
                                    mm = nc.tensor.matmul(py[:, a, 0:D], hh[:, par, m, hp, a * P:(a + 1) * P],
                                                          self.w2[:, bass.ds(e, 1), m, wp, :].rearrange("p a n -> p (a n)"), start=(m == 0 and i == 0), stop=(m == NH - 1 and i == 2))
                            mm.then_inc(y_done, 1)

                    first(0, 0, 16)
                    with pe.Fori(0, XT // 2 - 1) as r:
                        for par in range(2):
                            first(2 * r + par + 1, 1 - par, 16 * (r + par) + 16)
                            second(2 * r + par, par)
                    first(XT - 1, 1, 16 * (XT // 2))
                    second(XT - 2, 0)
                    second(XT - 1, 1)

                @block.scalar
                def _(act):
                    act.sem_inc(act_done, 8)
                    with act.Fori(0, XT // 2) as r:
                        for par in range(2):
                            j = 2 * r + par
                            e = nc.scalar.value_load(self.owner[0:1, bass.ds(j, 1)], min_val=0, max_val=EXPERTS - 1)
                            for m in range(NH):
                                g, q = m // 2, m % 2
                                if q == 0:
                                    act.wait_ge(h_done, NH * j + m + 2)
                                    act.wait_ge(lo_done, G * j + g + 1)
                                col = lambda a: a[:, bass.ds(e, 1), m:m + 1].rearrange("p a m -> p (a m)")
                                if layer == 0:
                                    nc.scalar.activation(hf[:, g % 2, q, :], ph[:, (G * par + g) % 4, q * ROWS:(q + 1) * ROWS], func, bias=col(self.b1), scale=col(self.s1)).then_inc(act_done, 1)
                                else:
                                    nc.scalar.activation(hf[:, g % 2, q, :], ph[:, (G * par + g) % 4, q * ROWS:(q + 1) * ROWS], func, bias=col(self.b1)).then_inc(act_done, 1)

                @block.vector
                def _(dve):
                    dve.sem_inc(lo_done, 2)
                    dve.sem_inc(y_taken, 2)
                    dve.wait_ge(b2_in, 16)

                    def out(j, par, n_out):
                        e = nc.vector.value_load(self.owner[0:1, bass.ds(j, 1)], min_val=0, max_val=EXPERTS - 1)
                        dve.wait_ge(y_out[par], n_out)
                        for a in range(2):
                            dve.wait_ge(y_done, 2 * j + a + 1)
                            nc.vector.tensor_tensor(y[:, par, a, :], py[:, a, 0:D], b2[:, bass.ds(e, 1), :].rearrange("p a n -> p (a n)"), ALU.add).then_inc(y_taken, 1)

                    def tile(j, par):
                        dve.wait_ge(tr_done, j + 1)
                        nc.vector.tensor_copy(xT[:, par, :, :, :].rearrange("p h c n -> p (h c n)"), pt[:, par, :]).then_inc(xT_ready, 1)
                        for g in range(G):
                            dve.wait_ge(act_done, NH * j + 2 * g + 2 + 8)
                            hi, lo = (hh[:, par, 2 * g:2 * g + 2, w, :] for w in range(2))
                            nc.vector.tensor_copy(hi, hf[:, g % 2, :, :]).then_inc(hi_done, 1)
                            dve.wait_ge(hi_done, G * j + g + 1)
                            nc.vector.tensor_tensor(lo, hf[:, g % 2, :, :], hi, ALU.subtract).then_inc(lo_done, 1)

                    tile(0, 0)
                    with dve.Fori(0, XT // 2 - 1) as r:
                        for par in range(2):
                            tile(2 * r + par + 1, 1 - par)
                            out(2 * r + par, par, 16 * r + 16)
                    tile(XT - 1, 1)
                    out(XT - 2, 0, 16 * (XT // 2))
                    out(XT - 1, 1, 16 * (XT // 2))

    def moe_combine(self, layer):
        nc, T = self.nc, self.T
        with ExitStack() as ctx:
            sb = lambda n, s, t=F32: self.sb(ctx, T + n, s, t)
            NG = len(self.got_in)
            gate = sb("gate", [P, B, D])
            got = sb("got", [P, NG, 2, D])
            gate_in = self.sem(ctx, T + "gate_in")
            got_in = self.got_in
            got0 = layer * 32 * (TILES // NG)
            ch, done = self.sem(ctx, T + "cch"), self.sem(ctx, T + "cdone")
            with nc.Block() as block:
                @block.sync
                def _(sp):
                    sp.dma_start(gate[:, :, :], self.mod_d[:, layer, 1, :, :]).then_inc(gate_in, 16)

                @block.gpsimd
                def _(pool):
                    for t in range(TILES):
                        if t >= NG:
                            pool.wait_ge(done, t - NG + 1)
                        for k in range(2):
                            pool.indirect_dma_start(got[:, t % NG, k, :], None, self.ys_d[:, :],
                                                    bass.IndirectOffsetOnAxis(ap=self.slot[:, k, t:t + 1], axis=0)).then_inc(got_in[t % NG], 16)

                @block.vector
                def _(dve):
                    n = [0]

                    def link(ins):
                        n[0] += 1
                        ins.then_inc(ch, 1)
                        dve.wait_ge(ch, n[0])

                    dve.wait_ge(gate_in, 16)
                    for t in range(TILES):
                        dve.wait_ge(got_in[t % NG], got0 + 32 * (t // NG) + 32)
                        g0, g1 = got[:, t % NG, 0, :], got[:, t % NG, 1, :]
                        if layer == 0:
                            link(nc.vector.tensor_tensor(g0, g0, g1, ALU.add))
                        else:
                            link(nc.vector.tensor_scalar(g0, g0, self.wt[:, 0, t:t + 1], None, ALU.mult))
                            link(nc.vector.scalar_tensor_tensor(out=g0, in0=g1, scalar=self.wt[:, 1, t:t + 1], in1=g0, op0=ALU.mult, op1=ALU.add))
                        link(nc.vector.tensor_tensor(g0, g0, gate[:, t // TPB, :], ALU.mult))
                        nc.vector.tensor_tensor(self.x[:, t, :], self.x[:, t, :], g0, ALU.add).then_inc(done, 1)


    def store(self):
        nc = self.nc
        with ExitStack() as ctx:
            stored = self.sem(ctx, "stored")
            with nc.Block() as block:
                @block.sync
                def _(sp):
                    sp.dma_start(self.out.rearrange("b (t p) d -> p (b t) d", p=P), self.x[:, :, :]).then_inc(stored, 16)
                    sp.wait_ge(stored, 16)


def host_layout(inputs):
    a = {n: np.ascontiguousarray(v) for n, v in inputs.items()}
    for n in "qkvo":
        a[f"L0_attn_w{n}_wT"] = np.ascontiguousarray(a.pop(f"L0_attn_w{n}_w").T)
    for n in "qk":
        a[f"{n}n_rep"] = np.tile(a.pop(f"L0_attn_{n}n_w"), P // HD)
    columns = lambda v: np.ascontiguousarray(v.reshape(EXPERTS, -1, P).transpose(2, 0, 1))
    a["L0_gateT"] = np.ascontiguousarray(a.pop("L0_ffn_gate_v").T)
    a["L0_w1T"] = np.ascontiguousarray(a.pop("L0_ffn_w1_v").transpose(0, 2, 1))
    a["L0_w2T"] = np.ascontiguousarray(a.pop("L0_ffn_w2_v").transpose(0, 2, 1))
    a["L0_b1c"], a["L0_g1c"], a["L1_b1c"] = columns(a.pop("L0_ffn_b1")), columns(a.pop("L0_ffn_w1_g")), columns(a.pop("L1_ffn_b1"))
    a.update(constants())
    return a


def kernel(**inputs):
    import concourse.bacc as bacc
    from concourse.bass_utils import run_bass_kernel_spmd

    nc = bacc.Bacc("TRN2", target_bir_lowering=False, num_devices=1)
    arrays = host_layout(inputs)
    dram = {n: nc.dram_tensor(n, a.shape, mybir.dt.from_np(a.dtype), kind="ExternalInput").ap() for n, a in arrays.items()}
    out = nc.dram_tensor("out", (B, L, D), F32, kind="ExternalOutput").ap()
    Program(nc, dram, out).build()
    return run_bass_kernel_spmd(nc, [arrays], core_ids=[0]).results[0]["out"]
```

```python
from contextlib import ExitStack

import numpy as np

import concourse.bass as bass
from concourse import mybir

ACT = mybir.ActivationFunctionType
ALU = mybir.AluOpType
AX = mybir.AxisListType
F32 = mybir.dt.float32
BF16 = mybir.dt.bfloat16
F16 = mybir.dt.float16
U32 = mybir.dt.uint32
I32 = mybir.dt.int32

P = 128
B, L, D = 4, 1024, 256
LAYERS = 2
N_TOK = B * L
TILES = N_TOK // P
TPB = L // P
DC = D // P
HEADS, HD = 16, 16
HG = 4
STEPS = B * HEADS // HG
WINDOW = 64
EXPERTS = 8
ROWS = 256
XT = 2 * N_TOK // ROWS + EXPERTS - 1
EPS = 1e-5
NEG = -1e30
SLOTS = 6
KROWS = SLOTS * HD
KAUG = KROWS + 3
QK = 4
HALF = 512
HT = HALF // P


def constants():
    r = np.arange(P)
    out = {}
    out["c_ident"] = np.eye(P, dtype=np.float32)
    out["c_heads"] = (r[:, None] // HD == r[None, :] // HD).astype(np.float32)
    out["c_swap"] = ((r[:, None] ^ 1) == r[None, :]).astype(np.float32)
    q, k = r[:, None], r[None, :]
    causal = np.where(k <= q, 0.0, NEG).astype(np.float32)
    out["c_causal"] = np.stack([causal, causal.T], 1)
    prev = np.where(q - (k - P) < WINDOW, 0.0, NEG)
    diag = np.where((k <= q) & (q - k < WINDOW), 0.0, NEG)
    out["c_window"] = np.stack([np.concatenate([prev, diag], 1), np.concatenate([diag.T, prev.T], 1)], 1).astype(np.float32)
    out["c_iota"] = np.tile(np.arange(64, dtype=np.float32), (P, 1))
    out["c_before"] = (r[:, None] < r[None, :]).astype(np.float32)
    inv = (1.0 / np.float32(10000.0) ** (np.arange(0, HD, 2, dtype=np.float32) / np.float32(HD))).astype(np.float32)
    ang = (np.arange(L, dtype=np.float32)[None, :] * inv[(r % HD) // 2][:, None]).astype(np.float32)
    sign = np.where(r % 2 == 0, -1.0, 1.0).astype(np.float32)[:, None]
    out["c_rope"] = np.stack([np.cos(ang), np.sin(ang) * sign], 1).astype(np.float32)
    return out


def unit_at(b, k, behind, per):
    q = k - behind
    b, q = b + q // per, q % per
    if isinstance(b, int) and not 0 <= b < B:
        return None
    return b, q


def used(count):
    return not isinstance(count, int) or count > 0


class Program:

    def __init__(self, nc, dram, out):
        self.nc, self.dram, self.out = nc, dram, out
        self.ctx = ExitStack()

    def sb(self, ctx, name, shape, dt=F32):
        return ctx.enter_context(self.nc.sbuf_tensor(name, shape, dt))

    def ps(self, ctx, name, shape, dt=F32):
        return ctx.enter_context(self.nc.psum_tensor(name, shape, dt))

    def sem(self, ctx, name):
        handle = ctx.enter_context(self.nc.semaphore(name))
        ctx.callback(lambda: self.nc.gpsimd.sem_clear(handle))
        return handle

    def build(self):
        with self.ctx as ctx:
            self.resident(ctx)
            self.setup()
            for layer in range(LAYERS):
                self.project(layer)
                with ExitStack() as hold:
                    self.attn = self.sb(hold, f"attn{layer}", [P, TILES, D])
                    self.attend(layer)
                    self.out_project(layer)
                self.moe(layer)

    def resident(self, ctx):
        self.x = self.sb(ctx, "x_res", [P, TILES, D])
        self.ident = self.sb(ctx, "ident", [P, P])
        self.ident_bf = self.sb(ctx, "ident_bf", [P, P], BF16)
        self.ident_h = self.sb(ctx, "ident_h", [P, P], F16)
        self.causal = self.sb(ctx, "causal", [P, 2, P], BF16)
        self.window = self.sb(ctx, "window", [P, 2, 2 * P], BF16)
        self.mod_col = self.sb(ctx, "mod_col", [P, 2, 12, B])
        nc = self.nc
        keep = lambda n: ctx.enter_context(nc.semaphore(n))
        self.zero_out, self.sent, self.got_in = keep("zero_out"), [keep("sent0"), keep("sent1")], [keep(f"got_in{i}") for i in range(4)]
        self.mod_d = nc.dram_tensor("mod_d", (2, 4, B, D), F32, kind="Internal").ap()
        self.parts_d = nc.dram_tensor("parts_d", (2, 3, QK * P, N_TOK), BF16, kind="Internal").ap()
        self.v_d = nc.dram_tensor("v_d", (2, N_TOK, 2 * D), F32, kind="Internal").ap()
        self.x_d = nc.dram_tensor("x_d", (N_TOK, D), F32, kind="Internal").ap()
        self.xs_d = [nc.dram_tensor(f"xs_d{i}", (XT * ROWS, 2 * D), F16, kind="Internal").ap() for i in range(2)]

    def setup(self):
        nc, d = self.nc, self.dram
        with ExitStack() as ctx:
            cT = self.sb(ctx, "cT", [P, 2, DC, B])
            sT = self.sb(ctx, "sT", [P, 2, DC, B])
            sgm = self.sb(ctx, "sgm", [P, 2, DC, B])
            wmod = self.sb(ctx, "wmod", [P, 2, DC, 6 * D])
            stage = self.sb(ctx, "stage", [P, 6 * P])
            mod = self.sb(ctx, "mod", [B, 2, 6 * D])
            sign = self.sb(ctx, "sign", [B, 2, 2, D])
            mod_row = self.sb(ctx, "mod_row", [B, 2, 4, D])
            mod_out = self.sem(ctx, "mod_out")
            pcol = self.ps(ctx, "pcol", [P, 2, 512])
            prow = self.ps(ctx, "prow", [P, 2, 3, 512])
            x_in = self.sem(ctx, "x_in")
            mod_in = self.sem(ctx, "mod_in")
            const_in = self.sem(ctx, "const_in")
            cast = self.sem(ctx, "cast")
            sig = self.sem(ctx, "sig")
            silu = self.sem(ctx, "silu")
            col_mm = self.sem(ctx, "col_mm")
            row_mm = self.sem(ctx, "row_mm")
            mod_ready, gate_ch, row_ready = (self.sem(ctx, n) for n in ("mod_ready", "gate_ch", "row_ready"))
            mod_ch = self.sem(ctx, "mod_ch")
            with nc.Block() as block:
                @block.sync
                def _(sp):
                    for l in range(2):
                        for c in range(DC):
                            with nc.allow_non_contiguous_dma(reason="a small transposed load"):
                                sp.dma_start(cT[:, l, c, :], d[f"L{l}_c"][:, c * P:(c + 1) * P].rearrange("b p -> p b")).then_inc(mod_in, 16)
                        sp.dma_start(wmod[:, l, :, :], d[f"L{l}_wmod"].rearrange("(c p) n -> p c n", p=P)).then_inc(mod_in, 16)
                    sp.dma_start(self.ident[:, :], d["c_ident"]).then_inc(const_in, 16)
                    sp.dma_start(stage[:, 0:2 * P], d["c_causal"].rearrange("p a n -> p (a n)")).then_inc(const_in, 16)
                    sp.dma_start(stage[:, 2 * P:6 * P], d["c_window"].rearrange("p a n -> p (a n)")).then_inc(const_in, 16)
                    sp.dma_start(self.x[:, :, :], d["L0_attn_x"].rearrange("b (t p) d -> p (b t) d", p=P)).then_inc(x_in, 16)
                    sp.wait_ge(row_ready, 6)
                    sp.dma_start(self.mod_d.rearrange("l k b d -> b l k d"), mod_row[:, :, :, :]).then_inc(mod_out, 16)
                    sp.wait_ge(mod_out, 16)
                    sp.wait_ge(x_in, 16)

                @block.gpsimd
                def _(pool):
                    pool.wait_ge(const_in, 48)
                    pool.tensor_copy(self.ident_bf[:, :], self.ident[:, :]).then_inc(cast, 1)
                    pool.tensor_copy(self.ident_h[:, :], self.ident[:, :]).then_inc(cast, 1)
                    pool.tensor_copy(self.causal[:, :, :].rearrange("p a n -> p (a n)"), stage[:, 0:2 * P]).then_inc(cast, 1)
                    pool.tensor_copy(self.window[:, :, :].rearrange("p a n -> p (a n)"), stage[:, 2 * P:6 * P]).then_inc(cast, 1)

                @block.scalar
                def _(act):
                    act.wait_ge(mod_in, 16 * 6)
                    nc.scalar.activation(sgm[:, :, :, :], cT[:, :, :, :], ACT.Sigmoid).then_inc(sig, 1)

                @block.vector
                def _(dve):
                    dve.wait_ge(sig, 1)
                    nc.vector.tensor_tensor(sT[:, :, :, :], cT[:, :, :, :], sgm[:, :, :, :], ALU.mult).then_inc(silu, 1)
                    for l in range(2):
                        dve.wait_ge(row_mm, l + 1)
                        nc.vector.tensor_copy(mod[:, l, :], prow[0:B, l, :, :].rearrange("b j n -> b (j n)")).then_inc(mod_ready, 1)
                        dve.wait_ge(mod_ready, l + 1)
                        kind = mod[:, l, :].rearrange("b (k d) -> b k d", d=D)
                        nc.vector.tensor_copy(mod_row[:, l, 2, :], kind[:, 3, :]).then_inc(row_ready, 1)
                        nc.vector.tensor_scalar(mod_row[:, l, 3, :], kind[:, 4, :], 1.0, None, ALU.add).then_inc(row_ready, 1)
                        g, s, out = kind[:, 2:6:3, :], sign[:, l, :, :], mod_row[:, l, 0:2, :]
                        nc.vector.tensor_scalar(s, g, 0.0, 2.0, ALU.is_ge, ALU.mult).then_inc(gate_ch, 1)
                        dve.wait_ge(gate_ch, 3 * l + 1)
                        nc.vector.tensor_scalar(s, s, -1.0, None, ALU.add).then_inc(gate_ch, 1)
                        dve.wait_ge(gate_ch, 3 * l + 2)
                        nc.vector.tensor_tensor(out, s, g, ALU.mult).then_inc(gate_ch, 1)
                        dve.wait_ge(gate_ch, 3 * l + 3)
                        nc.vector.scalar_tensor_tensor(out=out, in0=out, scalar=0.25, in1=s, op0=ALU.max, op1=ALU.mult).then_inc(row_ready, 1)
                    for l in range(2):
                        dve.wait_ge(col_mm, l + 1)
                        cols = pcol[:, l, 0:12 * B].rearrange("p (m b) -> p m b", b=B)
                        nc.vector.tensor_copy(self.mod_col[:, l, :, :], cols).then_inc(mod_ch, 1)
                        dve.wait_ge(mod_ch, 2 * l + 1)
                        ca = self.mod_col[:, l, :, :].rearrange("p (g six) b -> p g six b", six=6)[:, :, 2:4, :]
                        nc.vector.tensor_scalar(ca, ca, 1.0, None, ALU.add).then_inc(mod_ch, 1)

                @block.tensor
                def _(pe):
                    pe.wait_ge(silu, 1)
                    for l in range(2):
                        for j in range(3):
                            for c in range(DC):
                                mm = nc.tensor.matmul(prow[0:B, l, j, :], sT[:, l, c, :], wmod[:, l, c, j * 512:(j + 1) * 512], start=(c == 0), stop=(c == DC - 1))
                        mm.then_inc(row_mm, 1)
                    pe.wait_ge(const_in, 48)
                    for l in range(2):
                        pe.wait_ge(mod_ready, l + 1)
                        for m in range(12):
                            tr = nc.tensor.transpose(pcol[:, l, m * B:(m + 1) * B], mod[:, l, m * P:(m + 1) * P], self.ident[0:B, 0:B])
                        tr.then_inc(col_mm, 1)

    def project(self, layer):
        nc, d = self.nc, self.dram
        rope = layer == 1
        with ExitStack() as ctx:
            T = f"p{layer}_"
            sb = lambda n, s, t=F32: self.sb(ctx, T + n, s, t)
            sem = lambda n: self.sem(ctx, T + n)
            HEADS_CH = P // HD
            w = sb("w", [P, DC, 3 * D])
            bias = sb("bias", [P, QK])
            nw = sb("nw", [P, 2])
            bv = sb("bv", [P, D])
            aux = sb("aux", [P, P])
            cs = sb("cs", [P, 2, L]) if rope else None
            stats = sb("stats", [P, 2, nc.vector.BN_STATS_DIM])
            mv = sb("mv", [P, 4, 2])
            sd = sb("sd", [P, 4])
            rstd = sb("rstd", [P, 4])
            eps = sb("eps", [P, 1])
            modb = sb("modb", [P, 2, DC])
            xn = sb("xn", [P, 4, D])
            hT = sb("hT", [P, 2, DC, HALF])
            raw = sb("raw", [P, 2, HALF]) if not rope else None
            u = sb("u", [P, 4, HALF])
            side = sb("side", [P, 2, HALF])
            rn = sb("rn", [P, 2, HALF]) if rope else sb("rn", [P, 4, HT * HEADS_CH])
            wide = sb("wide", [P, HALF]) if not rope else None
            un = sb("un", [P, 4, HALF])
            rem = sb("rem", [P, 2, HALF])
            part = sb("part", [P, 4, 3, HALF], BF16)
            vt = sb("vt", [P, 2, HT, HEADS, 2 * HD])
            ptr = self.ps(ctx, T + "ptr", [P, 2, 512])
            pqk = self.ps(ctx, T + "pqk", [P, 2, 512])
            pax = self.ps(ctx, T + "pax", [P, 2, 512])
            pv = self.ps(ctx, T + "pv", [P, 2, 512])
            w_in, vt_set = sem("w_in"), sem("vt_set")
            stats_ready, stats_seen, mv_ready, sd_ready, rstd_ready = (sem(n) for n in ("stats_ready", "stats_seen", "mv_ready", "sd_ready", "rstd_ready"))
            xn_ready, tr_done, mod_ready, h_ready, qk_done, v_done, v_ready = (sem(n) for n in ("xn_ready", "tr_done", "mod_ready", "h_ready", "qk_done", "v_done", "v_ready"))
            raw_ready, u_ready, side_ready, aux_done, mean_ready, rn_ready = (sem(n) for n in ("raw_ready", "u_ready", "side_ready", "aux_done", "mean_ready", "rn_ready"))
            rms_ready, wide_ready, spread_done = sem("rms_ready"), sem("wide_ready"), sem("spread_done")
            un_ready, hi_ready, rem_ready, mid_ready, lo_ready = (sem(n) for n in ("un_ready", "hi_ready", "rem_ready", "mid_ready", "lo_ready"))
            part_out = [sem(f"part_out{i}") for i in range(4)]
            v_out = [sem("v_out0"), sem("v_out1")]
            constants_in = 16 * (9 if not rope else 5)

            UNITS = 2 * QK
            AHEAD = 6
            HIGH = 3 if rope else 5
            LAST = HIGH + 2

            unit = lambda b, k, behind: unit_at(b, k, behind, UNITS)

            def run(eng, slot):
                for k in range(-AHEAD, UNITS):
                    slot(0, k)
                with eng.Fori(1, B - 1) as b:
                    for k in range(UNITS):
                        slot(b, k)
                for k in range(UNITS + LAST + 1):
                    slot(B - 1, k)

            with nc.Block() as block:
                @block.sync
                def _(sp):
                    with nc.allow_non_contiguous_dma(reason="bias and norm columns"):
                        if rope:
                            sp.dma_start(w[:, :, :], d["L1_attn_Wqkv"].rearrange("(c p) n -> p c n", p=P)).then_inc(w_in, 16)
                            sp.dma_start(bias[:, :], d["L1_attn_bqkv"][0:2 * D].rearrange("(c p) -> p c", p=P)).then_inc(w_in, 16)
                            sp.dma_start(bv[:, :], d["L1_attn_bqkv"][2 * D:3 * D].partition_broadcast(P)).then_inc(w_in, 16)
                            sp.dma_start(cs[:, :, :], d["c_rope"]).then_inc(w_in, 16)
                            sp.dma_start(aux[:, :], d["c_swap"]).then_inc(w_in, 16)
                        else:
                            for j, n in enumerate("qkv"):
                                sp.dma_start(w[:, :, j * D:(j + 1) * D], d[f"L0_attn_w{n}_wT"].rearrange("(c p) n -> p c n", p=P)).then_inc(w_in, 16)
                            for j, n in enumerate("qk"):
                                sp.dma_start(bias[:, 2 * j:2 * j + 2], d[f"L0_attn_w{n}_b"].rearrange("(c p) -> p c", p=P)).then_inc(w_in, 16)
                            sp.dma_start(bv[:, :], d["L0_attn_wv_b"].partition_broadcast(P)).then_inc(w_in, 16)
                            sp.dma_start(nw[:, 0:1], d["qn_rep"].rearrange("(p a) -> p a", a=1)).then_inc(w_in, 16)
                            sp.dma_start(nw[:, 1:2], d["kn_rep"].rearrange("(p a) -> p a", a=1)).then_inc(w_in, 16)
                            sp.dma_start(aux[:, :], d["c_heads"]).then_inc(w_in, 16)
                    pd = self.parts_d[layer].rearrange("s (c p) n -> p c s n", p=P)
                    vd = self.v_d[layer].rearrange("(t p) n -> p t n", p=P)

                    def slot(b, k):
                        if at := unit(b, k, 1):
                            n, q = UNITS * at[0] + at[1], at[1]
                            if q % QK == QK - 1:
                                sp.wait_ge(v_ready, n + 1)
                                sp.dma_start(vd[:, bass.ds(n - QK + 1, HT), :], vt[:, q // QK, :, :, :].rearrange("p t h e -> p t (h e)")).then_inc(v_out[q // QK], 16)
                        if at := unit(b, k, LAST):
                            n, q = UNITS * at[0] + at[1], at[1]
                            sp.wait_ge(lo_ready, n + 1)
                            sp.dma_start(pd[:, q % QK, :, bass.ds((2 * at[0] + q // QK) * HALF, HALF)], part[:, q % 4, :, :]).then_inc(part_out[q % 4], 16)

                    run(sp, slot)
                    for half in range(2):
                        sp.wait_ge(v_out[half], 16 * B)
                    for i in range(4):
                        sp.wait_ge(part_out[i], 16 * 2 * B)

                @block.gpsimd
                def _(pool):
                    pool.memset(vt[:, :, :, :, HD + 1:2 * HD], 0.0).then_inc(vt_set, 1)
                    pool.memset(vt[:, :, :, :, HD:HD + 1], 1.0).then_inc(vt_set, 1)
                    pool.memset(eps[:, :], EPS).then_inc(vt_set, 1)
                    pool.wait_ge(w_in, constants_in)

                    def slot(b, k):
                        if not rope and (at := unit(b, k, 1)):
                            n, q = UNITS * at[0] + at[1], at[1]
                            pool.wait_ge(u_ready, n + 1)
                            if used(n - 1):
                                pool.wait_ge(aux_done, n - 1)
                            nc.gpsimd.tensor_tensor(side[:, q % 2, :], u[:, q % 4, :], u[:, q % 4, :], ALU.mult).then_inc(side_ready, 1)
                        if rope and (at := unit(b, k, 1)):
                            n, q = UNITS * at[0] + at[1], at[1]
                            half = q // QK
                            pool.wait_ge(u_ready, n + 1)
                            if used(n - 1):
                                pool.wait_ge(un_ready, n - 1)
                            nc.gpsimd.tensor_tensor(side[:, q % 2, :], u[:, q % 4, :], cs[:, 0, half * HALF:(half + 1) * HALF], ALU.mult).then_inc(side_ready, 1)
                        if at := unit(b, k, LAST):
                            n, q = UNITS * at[0] + at[1], at[1]
                            pool.wait_ge(mid_ready, n + 1)
                            nc.gpsimd.tensor_tensor(part[:, q % 4, 2, :], rem[:, q % 2, :], part[:, q % 4, 1, :], ALU.subtract).then_inc(lo_ready, 1)

                    run(pool, slot)

                @block.vector
                def _(dve):
                    dve.wait_ge(w_in, constants_in)
                    dve.wait_ge(vt_set, 2)

                    def slot(b, k):
                        norm = unit(b, k, -AHEAD)
                        if norm:
                            n, q = UNITS * norm[0] + norm[1], norm[1]
                            nc.vector.bn_stats(stats[:, q % 2, :], self.x[:, bass.ds(n, 1), :].rearrange("p a d -> p (a d)")).then_inc(stats_ready, 1)
                        if not rope and (at := unit(b, k, 5)):
                            n, q = UNITS * at[0] + at[1], at[1]
                            ch = q % QK
                            dve.wait_ge(spread_done, n + 1)
                            if used(n - 3):
                                dve.wait_ge(rem_ready, n - 3)
                            nc.vector.scalar_tensor_tensor(out=un[:, q % 4, :], in0=u[:, q % 4, :], scalar=nw[:, ch // 2:ch // 2 + 1], in1=pax[:, 1, :],
                                                           op0=ALU.mult, op1=ALU.mult).then_inc(un_ready, 1)
                        if at := unit(b, k, 1):
                            n, q = UNITS * at[0] + at[1], at[1]
                            half, t = q // QK, q % QK
                            dve.wait_ge(v_done, n + 1)
                            if t == 0 and used(at[0]):
                                dve.wait_ge(v_out[half], 16 * at[0])
                            nc.vector.tensor_tensor(vt[:, half, t, :, 0:HD], pv[:, q % 2, 0:D].rearrange("p (h e) -> p h e", e=HD),
                                                    bv[:, :].rearrange("p (h e) -> p h e", e=HD), ALU.add).then_inc(v_ready, 1)
                            if not rope:
                                dve.wait_ge(raw_ready, n + 1)
                                if used(n - 3):
                                    dve.wait_ge(un_ready, n - 3)
                                nc.vector.tensor_scalar(u[:, q % 4, :], raw[:, q % 2, :], 1e4, -1e4, ALU.min, ALU.max).then_inc(u_ready, 1)
                        if norm:
                            n, q = UNITS * norm[0] + norm[1], norm[1]
                            dve.wait_ge(stats_ready, n + 1)
                            dve.sem_inc(stats_seen, 1)
                            nc.vector.bn_aggr(mv[:, q % 4, :], stats[:, q % 2, :]).then_inc(mv_ready, 1)
                        if at := unit(b, k, HIGH + 1):
                            n, q = UNITS * at[0] + at[1], at[1]
                            dve.wait_ge(hi_ready, n + 1)
                            if used(n - 1):
                                dve.wait_ge(lo_ready, n - 1)
                            nc.vector.tensor_tensor(rem[:, q % 2, :], un[:, q % 4, :], part[:, q % 4, 0, :], ALU.subtract).then_inc(rem_ready, 1)
                        if at := unit(b, k, 2):
                            n, q = UNITS * at[0] + at[1], at[1]
                            half = q // QK
                            dve.wait_ge(aux_done, n + 1)
                            if not rope:
                                nc.vector.tensor_scalar(rn[:, q % 4, :], pax[:, 0, 0:HT * HEADS_CH], 1.0 / HD, EPS, ALU.mult, ALU.max).then_inc(mean_ready, 1)
                            else:
                                nc.vector.tensor_tensor(rn[:, q % 2, :], pax[:, q % 2, :], cs[:, 1, half * HALF:(half + 1) * HALF], ALU.mult).then_inc(mean_ready, 1)
                        if not rope and (at := unit(b, k, 3)):
                            n, q = UNITS * at[0] + at[1], at[1]
                            dve.wait_ge(rms_ready, n + 1)
                            nc.vector.reciprocal(rn[:, q % 4, :], rn[:, q % 4, :]).then_inc(rn_ready, 1)
                        if at := unit(b, k, 1 - AHEAD):
                            n, q = UNITS * at[0] + at[1], at[1]
                            dve.wait_ge(sd_ready, n + 1)
                            nc.vector.reciprocal(rstd[:, q % 4:q % 4 + 1], sd[:, q % 4:q % 4 + 1]).then_inc(rstd_ready, 1)
                        if rope and (at := unit(b, k, 2)):
                            n, q = UNITS * at[0] + at[1], at[1]
                            dve.wait_ge(side_ready, n + 1)
                            dve.wait_ge(mean_ready, n + 1)
                            if used(n - 3):
                                dve.wait_ge(rem_ready, n - 3)
                            nc.vector.tensor_tensor(un[:, q % 4, :], side[:, q % 2, :], rn[:, q % 2, :], ALU.add).then_inc(un_ready, 1)
                        if at := unit(b, k, 1 - AHEAD):
                            n, q = UNITS * at[0] + at[1], at[1]
                            dve.wait_ge(rstd_ready, n + 1)
                            if used(n - 3):
                                dve.wait_ge(tr_done, n - 3)
                            nc.vector.tensor_scalar(xn[:, q % 4, :], self.x[:, bass.ds(n, 1), :].rearrange("p a d -> p (a d)"), mv[:, q % 4, 0:1], rstd[:, q % 4:q % 4 + 1],
                                                    ALU.subtract, ALU.mult).then_inc(xn_ready, 1)

                    run(dve, slot)

                @block.scalar
                def _(act):
                    act.wait_ge(w_in, constants_in)
                    act.wait_ge(vt_set, 3)

                    def slot(b, k):
                        if not rope and (at := unit(b, k, 4)):
                            n, q = UNITS * at[0] + at[1], at[1]
                            act.wait_ge(rn_ready, n + 1)
                            if used(n):
                                act.wait_ge(spread_done, n)
                            nc.scalar.activation(wide[:, :].rearrange("p (g e) -> p g e", e=HD), rn[:, q % 4, :].unsqueeze(2).broadcast_to([P, HT * HEADS_CH, HD]),
                                                 ACT.Copy).then_inc(wide_ready, 1)
                        if not rope and (at := unit(b, k, 3)):
                            n, q = UNITS * at[0] + at[1], at[1]
                            act.wait_ge(mean_ready, n + 1)
                            nc.scalar.activation(rn[:, q % 4, :], rn[:, q % 4, :], ACT.Sqrt, bias=eps[:, :]).then_inc(rms_ready, 1)
                        if at := unit(b, k, 1 - AHEAD):
                            n, q = UNITS * at[0] + at[1], at[1]
                            act.wait_ge(mv_ready, n + 1)
                            nc.scalar.activation(sd[:, q % 4:q % 4 + 1], mv[:, q % 4, 1:2], ACT.Sqrt, bias=eps[:, :]).then_inc(sd_ready, 1)
                        if at := unit(b, k, 2 - AHEAD):
                            n, q = UNITS * at[0] + at[1], at[1]
                            half, t = q // HT, q % HT
                            if q == 0:
                                if used(n):
                                    act.wait_ge(h_ready, n)
                                for j in range(2):
                                    nc.scalar.activation(modb[:, j, :], self.mod_col[:, layer, 2 * j:2 * j + 2, bass.ds(at[0], 1)].rearrange("p c a -> p (c a)"),
                                                         ACT.Copy).then_inc(mod_ready, 1)
                                act.wait_ge(mod_ready, 2 * at[0] + 2)
                            act.wait_ge(tr_done, n + 1)
                            for c in range(DC):
                                a = nc.scalar.activation(hT[:, half, c, t * P:(t + 1) * P], ptr[:, q % 2, c * P:(c + 1) * P], ACT.Identity,
                                                         bias=modb[:, 0, c:c + 1], scale=modb[:, 1, c:c + 1])
                            a.then_inc(h_ready, 1)
                        if at := unit(b, k, 0):
                            n, q = UNITS * at[0] + at[1], at[1]
                            ch = q % QK
                            act.wait_ge(qk_done, n + 1)
                            if not rope:
                                if used(n - 1):
                                    act.wait_ge(u_ready, n - 1)
                                nc.scalar.activation(raw[:, q % 2, :], pqk[:, q % 2, :], ACT.Identity, bias=bias[:, ch:ch + 1]).then_inc(raw_ready, 1)
                            else:
                                if used(n - 3):
                                    act.wait_ge(un_ready, n - 3)
                                nc.scalar.activation(u[:, q % 4, :], pqk[:, q % 2, :], ACT.Identity, bias=bias[:, ch:ch + 1]).then_inc(u_ready, 1)
                        if at := unit(b, k, HIGH):
                            n, q = UNITS * at[0] + at[1], at[1]
                            act.wait_ge(un_ready, n + 1)
                            left = 2 * at[0] + q // 4
                            if used(left):
                                act.wait_ge(part_out[q % 4], 16 * left)
                            nc.scalar.activation(part[:, q % 4, 0, :], un[:, q % 4, :], ACT.Copy).then_inc(hi_ready, 1)
                        if at := unit(b, k, HIGH + 1):
                            n, q = UNITS * at[0] + at[1], at[1]
                            act.wait_ge(rem_ready, n + 1)
                            nc.scalar.activation(part[:, q % 4, 1, :], rem[:, q % 2, :], ACT.Copy).then_inc(mid_ready, 1)

                    run(act, slot)

                @block.tensor
                def _(pe):
                    pe.wait_ge(w_in, constants_in)

                    def slot(b, k):
                        if at := unit(b, k, 2 - AHEAD):
                            n, q = UNITS * at[0] + at[1], at[1]
                            pe.wait_ge(xn_ready, n + 1)
                            if used(n - 1):
                                pe.wait_ge(h_ready, n - 1)
                            for c in range(DC):
                                tr = nc.tensor.transpose(ptr[:, q % 2, c * P:(c + 1) * P], xn[:, q % 4, c * P:(c + 1) * P], self.ident[:, :])
                            tr.then_inc(tr_done, 1)
                        if rope and (at := unit(b, k, 1)):
                            n, q = UNITS * at[0] + at[1], at[1]
                            pe.wait_ge(u_ready, n + 1)
                            if used(n - 1):
                                pe.wait_ge(mean_ready, n - 1)
                            nc.tensor.matmul(pax[:, q % 2, :], aux[:, :], u[:, q % 4, :], start=True, stop=True).then_inc(aux_done, 1)
                        if not rope and (at := unit(b, k, 2)):
                            n, q = UNITS * at[0] + at[1], at[1]
                            pe.wait_ge(side_ready, n + 1)
                            if used(n):
                                pe.wait_ge(mean_ready, n)
                            for t in range(HT):
                                mm = nc.tensor.matmul(pax[:, 0, t * HEADS_CH:(t + 1) * HEADS_CH], side[:, q % 2, t * P:(t + 1) * P],
                                                      aux[:, :].rearrange("p (h e) -> p h e", e=HD)[:, :, 0], start=True, stop=True)
                            mm.then_inc(aux_done, 1)
                        if at := unit(b, k, 0):
                            n, q = UNITS * at[0] + at[1], at[1]
                            half, ch = q // QK, q % QK
                            if ch == 0:
                                pe.wait_ge(h_ready, n + HT)
                            if used(n - 1):
                                if rope:
                                    pe.wait_ge(u_ready, n - 1)
                                else:
                                    pe.wait_ge(raw_ready, n - 1)
                            for c in range(DC):
                                mm = nc.tensor.matmul(pqk[:, q % 2, :], w[:, c, ch * P:(ch + 1) * P], hT[:, half, c, :], start=(c == 0), stop=(c == DC - 1))
                            mm.then_inc(qk_done, 1)
                            if used(n - 1):
                                pe.wait_ge(v_ready, n - 1)
                            for c in range(DC):
                                mm = nc.tensor.matmul(pv[:, q % 2, 0:D], hT[:, half, c, ch * P:(ch + 1) * P], w[:, c, 2 * D:3 * D], start=(c == 0), stop=(c == DC - 1))
                            mm.then_inc(v_done, 1)
                        if not rope and (at := unit(b, k, 4)):
                            n, q = UNITS * at[0] + at[1], at[1]
                            pe.wait_ge(wide_ready, n + 1)
                            if used(n):
                                pe.wait_ge(un_ready, n)
                            for t in range(HT):
                                mm = nc.tensor.matmul(pax[:, 1, t * P:(t + 1) * P], wide[:, t * P:(t + 1) * P], self.ident[:, :], start=True, stop=True)
                            mm.then_inc(spread_done, 1)

                    run(pe, slot)

    def max_units(self, layer):
        out = []
        for i in range(TPB):
            if layer == 0:
                ks = list(range(max(0, i - 1), i + 1))
                for h0 in range(0, HG, 4 // len(ks)):
                    out.append((i, range(h0, h0 + 4 // len(ks)), ks, 0))
            else:
                n = i + 1
                per = 4 if n == 1 else 2 if n == 2 else 1
                for h0 in range(0, HG, per):
                    out.append((i, range(h0, h0 + per), list(range(0, min(n, 4))), 0))
                    if n > 4:
                        out.append((i, range(h0, h0 + per), list(range(4, n)), 1))
        return out

    def exp_units(self, layer):
        out = []
        for c in range(2):
            unit = []
            for j in range(TPB):
                lo, hi = j, (TPB if layer else j + 2)
                lo, hi = max(lo, 4 * c), min(hi, 4 * c + 4)
                if lo < hi:
                    unit.append((j, (lo - 4 * c) * P, (hi - 4 * c) * P))
            out.append(unit)
        return out

    def attend(self, layer):
        nc = self.nc
        with ExitStack() as ctx:
            T = f"a{layer}_"
            SETS = 4
            sb = lambda n, s, t=F32: self.sb(ctx, T + n, s, t)
            sem = lambda n: self.sem(ctx, T + n)
            Ks = [sb(f"Ks{i}", [KAUG, HG, L], BF16) for i in range(SETS)]
            Qs = [sb(f"Qs{i}", [KAUG, HG, L], BF16) for i in range(SETS)]
            V4 = [sb(f"V4{i}", [P, TPB, HG, 2 * HD]) for i in range(SETS)]
            probs = sb("probs", [P, 2, HG, HALF])
            mx = sb("mx", [P, 2, HG, TPB])
            nm = sb("nm", [P, HG * TPB])
            nmr = sb("nmr", [HG * TPB, P])
            nmp = sb("nmp", [HG * TPB, 3, P], BF16)
            oT = sb("oT", [P, HALF])
            rden = sb("rden", [P, 4, HG])
            NB = 3
            pst = self.ps(ctx, T + "pst", [P, NB, 512])
            pmx = self.ps(ctx, T + "pmx", [P, NB, 512])
            pacc = self.ps(ctx, T + "pacc", [P, 512])
            pms = self.ps(ctx, T + "pms", [P, 512])
            ones_set = sem("ones_set")
            kq_in = [sem(f"kq_in{i}") for i in range(SETS)]
            max_in = [sem(f"max_in{i}") for i in range(SETS)]
            s_done, m_done, nm_ch, nm_ready, nmT_done, nmp_ready = (sem(n) for n in ("s_done", "m_done", "nm_ch", "nm_ready", "nmT_done", "nmp_ready"))
            st_done, exp_done, pv_done, acc_out, oT_done, norm_ch, norm_done = (sem(n) for n in ("st_done", "exp_done", "pv_done", "acc_out", "oT_done", "norm_ch", "norm_done"))
            nm_mid = sem("nm_mid")
            zero, zeroed = sb("zero", [P, 2 * D], F16), sem("zeroed")
            step_over = sem("step_over")
            maxu = self.max_units(layer)
            NM = len(maxu)
            halves = self.exp_units(layer)
            expu = [(c, k, j, q0, q1, h) for c in range(2) for k, (j, q0, q1) in enumerate(halves[c]) for h in range(HG)]
            NE = len(expu)
            NV = NE // HG
            assert SETS * NV % 2 == 0 and NE % NB == 0
            mask = self.causal if layer else self.window
            loads = 2 * SLOTS + 1
            SLOT_Q, SLOT_K = (0, 0, 0, 1, 1, 2), (0, 1, 2, 0, 1, 0)

            def load(sp, par, b, hg):
                pd = self.parts_d[layer]
                row = lambda base: bass.ds(hg * (HG * HD) + base, HG * HD)
                for dst, base, slots in ((Qs[par], 0, SLOT_Q), (Ks[par], D, SLOT_K)):
                    for s, part in enumerate(slots):
                        src = pd[part, row(base), bass.ds(b * L, L)].rearrange("(g e) n -> e g n", e=HD)
                        sp.dma_start(dst[s * HD:(s + 1) * HD, :, :], src).then_inc(kq_in[par], 16)
                vsrc = self.v_d[layer][bass.ds(b * L, L), bass.ds(hg * (HG * 2 * HD), HG * 2 * HD)].rearrange("(t p) n -> p t n", p=P)
                sp.dma_start(V4[par][:, :, :, :].rearrange("p t h e -> p t (h e)"), vsrc).then_inc(kq_in[par], 16)

            def send_max(eng, par, s):
                eng.wait_ge(nmp_ready, s + 1)
                for p in range(3):
                    eng.dma_start(Qs[par][KROWS + p:KROWS + p + 1, :, :].rearrange("a h (i q) -> a (h i) q", q=P), nmp[:, p, :]).then_inc(max_in[par], 16)

            def pe_max(pe, par, s, u):
                i, hs, ks, part = maxu[u]
                if u >= NB:
                    pe.wait_ge(m_done, NM * s + u - NB + 1)
                cols = len(ks) * P
                for n, h in enumerate(hs):
                    o = n * cols
                    diag = i in ks
                    mm = nc.tensor.matmul(pmx[:, u % NB, o:o + cols], Qs[par][0:KROWS, h, i * P:(i + 1) * P],
                                          Ks[par][0:KROWS, h, ks[0] * P:ks[0] * P + cols], start=True, stop=not diag, skip_group_check=True)
                    if diag and layer:
                        mm = nc.tensor.matmul(pmx[:, u % NB, o + cols - P:o + cols], self.ident_bf[:, :], mask[:, 0, :], start=False, stop=True, skip_group_check=True)
                    elif diag:
                        mm = nc.tensor.matmul(pmx[:, u % NB, o:o + cols], self.ident_bf[:, :], mask[:, 0, 2 * P - cols:2 * P], start=False, stop=True, skip_group_check=True)
                mm.then_inc(s_done, 1)

            def pe_nmT(pe, s):
                pe.wait_ge(nm_ready, s + 1)
                nc.tensor.transpose(pms[0:HG * TPB, 0:P], nm[:, :], self.ident[:, :]).then_inc(nmT_done, 1)

            def pe_st(pe, par, s, u):
                c, k, j, q0, q1, h = expu[u]
                if used(NE * s + u - NB + 1):
                    pe.wait_ge(exp_done, NE * s + u - NB + 1)
                out = pst[:, u % NB, :]
                g0, g1 = c * HALF + q0, c * HALF + q1
                diag = j * P - c * HALF if layer else q0
                masked = (0 <= diag) if layer else True
                mm = nc.tensor.matmul(out[:, q0:q1], Ks[par][:, h, j * P:(j + 1) * P], Qs[par][:, h, g0:g1], start=True, stop=not masked, skip_group_check=True)
                if masked and layer:
                    mm = nc.tensor.matmul(out[:, diag:diag + P], self.ident_bf[:, :], mask[:, 1, :], start=False, stop=True, skip_group_check=True)
                elif masked:
                    m0 = g0 - j * P
                    mm = nc.tensor.matmul(out[:, q0:q1], self.ident_bf[:, :], mask[:, 1, m0:m0 + q1 - q0], start=False, stop=True, skip_group_check=True)
                mm.then_inc(st_done, 1)

            def pe_pv(pe, par, s, v, hs):
                c, k, j, q0, q1, _ = expu[HG * v]
                pe.wait_ge(exp_done, NE * s + HG * v + hs[-1] + 1)
                if k == 0 and hs[0] == 0 and used(2 * s + c):
                    pe.wait_ge(acc_out, 2 * s + c)
                for h in hs:
                    mm = nc.tensor.matmul(pacc[32 * h:32 * h + 32, q0:q1], V4[par][:, j, h, :], probs[:, (par * NV + v) % 2, h, q0:q1],
                                          start=(k == 0), stop=(k == len(halves[c]) - 1), skip_group_check=True)
                if hs[-1] == HG - 1:
                    mm.then_inc(pv_done, 1)

            def pe_oT(pe, s, c):
                pe.wait_ge(acc_out, 2 * s + c + 1)
                for t in range(4):
                    tr = nc.tensor.transpose(pms[:, t * P:(t + 1) * P], oT[:, t * P:(t + 1) * P], self.ident[:, :])
                tr.then_inc(oT_done, 1)

            seq = []
            for v in range(NV + 1):
                for hs in ((0, 1), (2, 3)):
                    if v < NV:
                        seq += [("st", HG * v + h) for h in hs]
                    if v:
                        seq.append(("pv", (v - 1, hs)))
                if v == 0:
                    seq.insert(HG, ("oT", 1))
                if v == len(halves[0]) + 1:
                    seq.append(("oT", 0))
            m_end = int(len(seq) * (0.68 if layer else 0.6))
            plan, m = [], 0
            for n, item in enumerate(seq):
                plan.append(item)
                while m < min(NM, (n + 1) * NM // m_end):
                    plan.append(("max", m))
                    m += 1
                if n == m_end + 2:
                    plan.append(("nmT", 0))
            assert m == NM and plan.index(("oT", 0)) < plan.index(("nmT", 0))

            def pe_body(pe, par, s, maxes):
                for kind, a in plan:
                    if kind == "st":
                        pe_st(pe, par, s, a)
                    elif kind == "pv":
                        pe_pv(pe, par, s, *a)
                    elif kind == "oT" and used(s + 1 - a):
                        pe.wait_ge(norm_done, 2 * s + 1 - a)
                        pe_oT(pe, s - a, a)
                    elif maxes and kind == "max":
                        pe_max(pe, (par + 1) % SETS, s + 1, a)
                    elif maxes and kind == "nmT":
                        pe.wait_ge(norm_done, 2 * s + 2)
                        pe_nmT(pe, s + 1)

            def dve_max(dve, s, u):
                i, hs, ks, part = maxu[u]
                dve.wait_ge(s_done, NM * s + u + 1)
                cols = len(ks) * P
                src = pmx[:, u % NB, 0:len(hs) * cols].rearrange("p (h n) -> p h n", n=cols)
                nc.vector.tensor_reduce(mx[:, part, hs[0]:hs[0] + len(hs), i], src, AX.X, ALU.max).then_inc(m_done, 1)

            def dve_nm(dve, s):
                dve.wait_ge(m_done, NM * s + NM)
                if layer:
                    nc.vector.tensor_tensor(mx[:, 0, :, 4:8], mx[:, 0, :, 4:8], mx[:, 1, :, 4:8], ALU.max).then_inc(nm_ch, 1)
                    dve.wait_ge(nm_ch, 3 * s + 1)
                c0 = 3 * s + 1 if layer else 2 * s
                nc.vector.tensor_scalar(nm[:, :], mx[:, 0, :, :].rearrange("p h i -> p (h i)"), -1.0, None, ALU.mult).then_inc(nm_ready, 1)
                dve.wait_ge(nmT_done, s + 1)
                src = pms[0:HG * TPB, 0:P]
                nc.vector.tensor_copy(nmp[:, 0, :], src).then_inc(nm_ch, 1)
                dve.wait_ge(nm_ch, c0 + 1)
                nc.vector.tensor_tensor(nmr[:, :], src, nmp[:, 0, :], ALU.subtract).then_inc(nm_ch, 1)
                dve.wait_ge(nm_ch, c0 + 2)
                nc.vector.tensor_copy(nmp[:, 1, :], nmr[:, :]).then_inc(nm_mid, 1)
                dve.wait_ge(nm_mid, s + 1)
                nc.vector.tensor_tensor(nmp[:, 2, :], nmr[:, :], nmp[:, 1, :], ALU.subtract).then_inc(nmp_ready, 1)

            def dve_norm(dve, s, c, tile, col):
                dve.wait_ge(oT_done, 2 * s + c + 1)
                src = pms[:, :].rearrange("p (t h e) -> p t h e", t=4, e=2 * HD)
                nc.vector.reciprocal(rden[:, :, :], src[:, :, :, HD]).then_inc(norm_ch, 1)
                dve.wait_ge(norm_ch, 2 * s + c + 1)
                dst = self.attn[:, bass.ds(tile, 4), bass.ds(col, HG * HD)].rearrange("p t (h e) -> p t h e", e=HD)
                nc.vector.tensor_tensor(dst, src[:, :, :, 0:HD], rden[:, :, :].unsqueeze(3).broadcast_to([P, 4, HG, HD]), ALU.mult).then_inc(norm_done, 1)

            def dve_step(dve, hg, s, b, maxes):
                for kind, a in plan:
                    if kind == "oT" and used(s + 1 - a):
                        ub, uh = unit_at(b, hg, a, SETS)
                        dve_norm(dve, s - a, a, TPB * ub + 4 * a, uh * HG * HD)
                    elif maxes and kind == "max":
                        dve_max(dve, s + 1, a)
                    elif maxes and kind == "nmT":
                        dve_nm(dve, s + 1)

            def act_sums(act, s, c):
                act.wait_ge(pv_done, NV * s + (len(halves[0]), NV)[c])
                if used(2 * s + c):
                    act.wait_ge(oT_done, 2 * s + c)
                nc.scalar.activation(oT[:, :], pacc[:, :], ACT.Copy).then_inc(acc_out, 1)

            def act_step(act, hg, s):
                for u, (c, k, j, q0, q1, h) in enumerate(expu):
                    v = u // HG
                    act.wait_ge(st_done, NE * s + u + 1)
                    if h == 0 and used(NV * s + v - 1):
                        act.wait_ge(pv_done, NV * s + v - 1)
                    nc.scalar.activation(probs[:, (hg * NV + v) % 2, h, q0:q1], pst[:, u % NB, q0:q1], ACT.Exp, scale=HD ** -0.5).then_inc(exp_done, 1)
                    if u == 1 and used(s):
                        act_sums(act, s - 1, 1)
                    if u == HG * len(halves[0]) + HG - 1:
                        act_sums(act, s, 0)

            with nc.Block() as block:
                @block.gpsimd
                def _(pool):
                    for i in range(SETS):
                        pool.memset(Ks[i][KROWS:KAUG, :, :], 1.0).then_inc(ones_set, 1)
                    pool.wait_ge(ones_set, SETS)
                    pool.memset(zero[:, :], 0.0).then_inc(zeroed, 1)
                    pool.wait_ge(zeroed, 1)
                    A = 6
                    assert XT * ROWS % (A * P) == 0 and XT * ROWS // (A * P) < STEPS
                    for j in range(XT * ROWS // (A * P)):
                        pool.wait_ge(pv_done, NV * (j + 1))
                        dst = self.xs_d[layer][j * A * P:(j + 1) * A * P, :].rearrange("(a p) n -> p a n", p=P)
                        pool.dma_start(dst, zero[:, :].unsqueeze(1).broadcast_to([P, A, 2 * D])).then_inc(self.zero_out, 16)
                    pool.wait_ge(self.zero_out, 16 * (XT * ROWS // (A * P)) * (layer + 1))

                @block.sync
                def _(sp):
                    for hg in range(SETS - 1):
                        if hg > 0:
                            sp.wait_ge(kq_in[hg - 1], 16 * loads)
                        load(sp, hg, 0, hg)
                    with sp.Fori(0, B - 1) as b:
                        for hg in range(SETS):
                            s = SETS * b + hg
                            if hg == 0:
                                load(sp, SETS - 1, b, SETS - 1)
                            else:
                                load(sp, hg - 1, b + 1, hg - 1)
                            send_max(sp, (hg + 1) % SETS, s + 1)
                            sp.wait_ge(pv_done, NV * s + NV)
                            sp.sem_inc(step_over, 1)
                    load(sp, SETS - 1, B - 1, SETS - 1)
                    for s in range(STEPS - SETS, STEPS - 1):
                        send_max(sp, (s + 1) % SETS, s + 1)

                @block.tensor
                def _(pe):
                    pe.wait_ge(kq_in[0], 16 * loads)
                    for u in range(NM):
                        pe_max(pe, 0, 0, u)
                    pe_nmT(pe, 0)
                    pe.wait_ge(ones_set, SETS)

                    def turn(b, last):
                        for hg in range(SETS):
                            pe.wait_ge(max_in[hg], 48 * b + 48)
                            nxt = (hg + 1) % SETS
                            maxes = not (last and nxt == 0)
                            if maxes:
                                pe.wait_ge(kq_in[nxt], 16 * loads * (b + (nxt == 0)) + 16 * loads)
                            pe_body(pe, hg, SETS * b + hg, maxes)

                    turn(0, False)
                    with pe.Fori(1, B - 1) as b:
                        turn(b, False)
                    turn(B - 1, True)
                    pe.wait_ge(norm_done, 2 * STEPS)
                    pe_oT(pe, STEPS - 1, 1)

                @block.vector
                def _(dve):
                    for u in range(NM):
                        dve_max(dve, 0, u)
                    dve_nm(dve, 0)
                    dve.sem_inc(norm_done, 1)

                    def turn(b, last):
                        for hg in range(SETS):
                            dve_step(dve, hg, SETS * b + hg, b, not (last and hg == SETS - 1))

                    turn(0, False)
                    with dve.Fori(1, B - 1) as b:
                        turn(b, False)
                    turn(B - 1, True)
                    dve_norm(dve, STEPS - 1, 1, TPB * (B - 1) + 4, (SETS - 1) * HG * HD)

                @block.scalar
                def _(act):
                    send_max(act, 0, 0)
                    for hg in range(SETS):
                        act_step(act, hg, hg)
                    with act.Fori(1, B) as b:
                        for hg in range(SETS):
                            act_step(act, hg, SETS * b + hg)
                    act_sums(act, STEPS - 1, 1)

    def out_project(self, layer):
        nc, d = self.nc, self.dram
        with ExitStack() as ctx:
            T = f"o{layer}_"
            sb = lambda n, s, t=F32: self.sb(ctx, T + n, s, t)
            sem = lambda n: self.sem(ctx, T + n)
            wo = sb("wo", [P, DC, D])
            bo = sb("bo", [P, D])
            at = sb("at", [P, 2, 2, D])
            aT = sb("aT", [P, 2, 2, DC, P])
            y = sb("y", [P, 2, 2, D])
            gate = sb("gate", [P, B, D])
            ptr = self.ps(ctx, T + "ptr", [P, 2, 512])
            py = self.ps(ctx, T + "py", [P, 2, 512])
            w_in, copied, tr_done, aT_ready, y_done, y_ready, gated, x_done = (
                sem(n) for n in ("w_in", "copied", "tr_done", "aT_ready", "y_done", "y_ready", "gated", "x_done"))
            wname, bname = ("L0_attn_wo_wT", "L0_attn_wo_b") if layer == 0 else ("L1_attn_Wproj", "L1_attn_bproj")
            PER = TPB // 2
            pair = lambda a, n: a[:, bass.ds(2 * n, 2), :]

            def run(eng, slot):
                for k in range(-1, PER):
                    slot(0, k)
                with eng.Fori(1, B - 1) as b:
                    for k in range(PER):
                        slot(b, k)
                for k in range(PER + 2):
                    slot(B - 1, k)

            def at_unit(b, k, behind):
                u = unit_at(b, k, behind, PER)
                return u and (PER * u[0] + u[1], u[1] % 2, u[0])

            with nc.Block() as block:
                @block.sync
                def _(sp):
                    sp.dma_start(wo[:, :, :], d[wname].rearrange("(c p) n -> p c n", p=P)).then_inc(w_in, 16)
                    sp.dma_start(bo[:, :], d[bname].partition_broadcast(P)).then_inc(w_in, 16)
                    sp.dma_start(gate[:, :, :].rearrange("p b d -> p (b d)"), self.mod_d[layer, 0, :, :].rearrange("b d -> (b d)").partition_broadcast(P)).then_inc(w_in, 16)

                @block.scalar
                def _(act):
                    def slot(b, k):
                        if u := at_unit(b, k, -1):
                            n, h, _ = u
                            if used(n - 1):
                                act.wait_ge(tr_done, n - 1)
                            nc.scalar.activation(at[:, h, :, :], pair(self.attn, n), ACT.Copy).then_inc(copied, 1)
                        if u := at_unit(b, k, 0):
                            n, h, _ = u
                            act.wait_ge(tr_done, n + 1)
                            if used(n - 1):
                                act.wait_ge(y_done, n - 1)
                            nc.scalar.activation(aT[:, h, :, :, :].rearrange("p t c n -> p (t c n)"), ptr[:, h, :], ACT.Copy).then_inc(aT_ready, 1)

                    run(act, slot)

                @block.tensor
                def _(pe):
                    pe.wait_ge(w_in, 48)

                    def slot(b, k):
                        if u := at_unit(b, k, 0):
                            n, h, _ = u
                            pe.wait_ge(copied, n + 1)
                            if used(n - 1):
                                pe.wait_ge(aT_ready, n - 1)
                            for t in range(2):
                                for c in range(DC):
                                    tr = nc.tensor.transpose(ptr[:, h, (t * DC + c) * P:(t * DC + c + 1) * P], at[:, h, t, c * P:(c + 1) * P], self.ident[:, :])
                            tr.then_inc(tr_done, 1)
                        if u := at_unit(b, k, 1):
                            n, h, _ = u
                            pe.wait_ge(aT_ready, n + 1)
                            if used(n - 1):
                                pe.wait_ge(y_ready, n - 1)
                            for t in range(2):
                                for c in range(DC):
                                    mm = nc.tensor.matmul(py[:, h, t * D:(t + 1) * D], aT[:, h, t, c, :], wo[:, c, :], start=(c == 0), stop=(c == DC - 1))
                            mm.then_inc(y_done, 1)

                    run(pe, slot)

                @block.vector
                def _(dve):
                    dve.wait_ge(w_in, 48)

                    def slot(b, k):
                        if u := at_unit(b, k, 1):
                            n, h, ub = u
                            dve.wait_ge(y_done, n + 1)
                            if used(n - 1):
                                dve.wait_ge(x_done, n - 1)
                            nc.vector.tensor_tensor(y[:, h, :, :], py[:, h, :].rearrange("p (t n) -> p t n", t=2),
                                                    bo[:, :].unsqueeze(1).broadcast_to([P, 2, D]), ALU.add).then_inc(y_ready, 1)
                            dve.wait_ge(y_ready, n + 1)
                            nc.vector.tensor_tensor(y[:, h, :, :], y[:, h, :, :], gate[:, bass.ds(ub, 1), :].broadcast_to([P, 2, D]), ALU.mult).then_inc(gated, 1)
                            dve.wait_ge(gated, n + 1)
                            nc.vector.tensor_tensor(pair(self.x, n), pair(self.x, n), y[:, h, :, :], ALU.add).then_inc(x_done, 1)

                    run(dve, slot)

    def moe(self, layer):
        nc = self.nc
        with ExitStack() as ctx:
            T = f"m{layer}_"
            self.T = T
            self.H = 1024 if layer == 0 else 512
            self.NH = self.H // P
            NH = self.NH
            self.s1 = self.sb(ctx, T + "s1", [P, EXPERTS, NH])
            self.b1 = self.sb(ctx, T + "b1", [P, EXPERTS, NH])
            self.gw = self.sb(ctx, T + "gw", [P, DC, EXPERTS])
            self.gs = self.sb(ctx, T + "gs", [P, EXPERTS])
            self.gb = self.sb(ctx, T + "gb", [P, EXPERTS])
            self.slot = self.sb(ctx, T + "slot", [P, 2, TILES], U32)
            self.wt = self.sb(ctx, T + "wt", [P, 2, TILES])
            self.owner = self.sb(ctx, T + "owner", [P, XT], I32)
            self.ys_d = nc.dram_tensor(T + "ys_d", (XT * ROWS, D), F32, kind="Internal").ap()
            self.lg = self.sb(ctx, T + "lg", [P, TILES, EXPERTS])
            with ExitStack() as inner:
                self.zh = self.sb(inner, T + "zh", [P, TILES, 2, D], F16)
                self.moe_input(layer)
                self.moe_route(layer)
                self.w1 = self.sb(inner, T + "w1", [P, EXPERTS, DC, 2, self.H], F16)
                self.w2 = self.sb(inner, T + "w2", [P, EXPERTS, NH, 2, D], F16)
                if layer == 0:
                    self.s2 = self.sb(inner, T + "s2", [P, EXPERTS, D])
                self.moe_weights(layer)
                self.moe_tiles(layer)
            self.moe_combine(layer)

    def moe_weights(self, layer):
        nc, d, T, H, NH = self.nc, self.dram, self.T, self.H, self.NH
        normed = layer == 0
        w1_src = d["L0_w1T"] if normed else d["L1_ffn_W1"]
        w2_src = d["L0_w2T"] if normed else d["L1_ffn_W2"]
        with ExitStack() as ctx:
            sb = lambda n, s, t=F32: self.sb(ctx, T + n, s, t)
            sem = lambda n: self.sem(ctx, T + n)
            QT = TILES // 4
            assert DC * H <= QT * D and NH * D <= QT * D
            quarter = lambda i, n: self.x[:, i * QT:(i + 1) * QT, :].rearrange("p t d -> p (t d)")[:, 0:n]
            st1 = [quarter(i, DC * H).rearrange("p (c n) -> p c n", c=DC) for i in range(2)]
            st2 = quarter(2, NH * D).rearrange("p (c n) -> p c n", c=NH)
            HS = DC * H // 2
            sq = [quarter(3, DC * H)[:, i * HS:(i + 1) * HS] for i in range(2)]
            rt = sb("rt", [P, 2, D])
            ones = sb("ones", [P, P])
            EM = EXPERTS * NH
            lg = self.lg[:, :, :].rearrange("p t e -> p (t e)")
            g1 = lg[:, 0:EM].rearrange("p (e m) -> p e m", m=NH)
            sum1 = lg[:, EM:3 * EM].rearrange("p (c n) -> p c n", c=2)
            pss = self.ps(ctx, T + "pss", [P, 512])
            pbc = self.ps(ctx, T + "pbc", [P, 2, 512])
            g1_in, g2_in, w2_in, ones_set = (sem(n) for n in ("g1_in", "g2_in", "w2_in", "ones_set"))
            w1_in = [sem("w1_in0"), sem("w1_in1")]
            sum_ready = sem("sum_ready")
            sq1, ss1, sq2, ss2, root, rt_ch, s2_ready, hi1, lo1, hi2, lo2, ch, sqrt1_done = (
                sem(n) for n in ("sq1", "ss1", "sq2", "ss2", "root", "rt_ch", "s2_ready", "hi1", "lo1", "hi2", "lo2", "wch", "sqrt1_done"))
            sent = self.sent
            with nc.Block() as block:
                @block.gpsimd
                def _(pool):
                    pool.memset(ones[:, :], 1.0).then_inc(ones_set, 1)
                    for t in range(TILES):
                        for k in range(2):
                            pool.indirect_dma_start(self.xs_d[layer][:, :], bass.IndirectOffsetOnAxis(ap=self.slot[:, k, t:t + 1], axis=0),
                                                    self.zh[:, t, :, :].rearrange("p a d -> p (a d)"), None).then_inc(sent[k], 16)
                    for k in range(2):
                        pool.wait_ge(sent[k], 16 * TILES * (layer + 1))

                @block.sync
                def _(sp):
                    def load1(e, par):
                        sp.dma_start(st1[par], w1_src[bass.ds(e, 1), :, :].rearrange("a (c p) n -> p (a c) n", p=P)).then_inc(w1_in[par], 16)

                    def load2(e):
                        sp.dma_start(st2, w2_src[bass.ds(e, 1), :, :].rearrange("a (c p) n -> p (a c) n", p=P)).then_inc(w2_in, 16)

                    load1(0, 0)
                    load2(0)
                    load1(1, 1)
                    if normed:
                        sp.dma_start(g1[:, :, :], d["L0_g1c"]).then_inc(g1_in, 16)
                        sp.dma_start(self.s2[:, :, :], d["L0_ffn_w2_g"].rearrange("e n -> (e n)").partition_broadcast(P).rearrange("p (e n) -> p e n", e=EXPERTS)).then_inc(g2_in, 16)
                    with sp.Fori(0, EXPERTS // 2 - 1) as r:
                        for par in range(2):
                            e = 2 * r + par
                            sp.wait_ge(lo1, e + 1)
                            load1(e + 2, par)
                            sp.wait_ge(lo2, e + 1)
                            load2(e + 1)
                    sp.wait_ge(lo2, EXPERTS - 1)
                    load2(EXPERTS - 1)

                @block.scalar
                def _(act):
                    act.sem_inc(ss2, 2)
                    with act.Fori(0, EXPERTS // 2) as r:
                        for par in range(2):
                            e = 2 * r + par
                            act.wait_ge(w1_in[par], 16 * r + 16)
                            for i in range(2 if normed else 0):
                                act.wait_ge(ss2, 2 * e + i + 1)
                                nc.scalar.activation(sq[i], st1[par].rearrange("p c n -> p (c n)")[:, i * HS:(i + 1) * HS], ACT.Square).then_inc(sq1, 1)
                            nc.scalar.activation(self.w1[:, bass.ds(e, 1), :, 0, :].rearrange("p a c n -> p (a c) n"), st1[par], ACT.Copy).then_inc(hi1, 1)
                            act.wait_ge(w2_in, 16 * e + 16)
                            for i in range(2 if normed else 0):
                                act.wait_ge(ss1, 2 * e + i + 1)
                                nc.scalar.activation(sq[i], st2.rearrange("p c n -> p (c n)")[:, i * HS:(i + 1) * HS], ACT.Square).then_inc(sq2, 1)
                            nc.scalar.activation(self.w2[:, bass.ds(e, 1), :, 0, :].rearrange("p a c n -> p (a c) n"), st2, ACT.Copy).then_inc(hi2, 1)
                            if normed:
                                act.wait_ge(ss2, 2 * e + 4)
                                act.wait_ge(s2_ready, e + 1)
                                nc.scalar.activation(rt[:, par, :], pbc[:, par, 0:D], ACT.Sqrt).then_inc(root, 1)
                    if normed:
                        act.wait_ge(sum_ready, 2)
                        nc.scalar.activation(self.s1[:, :, :].rearrange("p e m -> p (e m)"), sum1[:, 0, :], ACT.Sqrt).then_inc(sqrt1_done, 1)

                @block.tensor
                def _(pe):
                    if not normed:
                        return
                    pe.wait_ge(ones_set, 1)
                    pe.sem_inc(root, 2)
                    with pe.Fori(0, EXPERTS // 2) as r:
                        for par in range(2):
                            e = 2 * r + par
                            assert H == HS and DC == 2
                            for c in range(DC):
                                pe.wait_ge(sq1, 2 * e + c + 1)
                                for m in range(NH):
                                    mm = nc.tensor.matmul(pss[:, bass.ds(c * EXPERTS * NH + e * NH + m, 1)], sq[c][:, m * P:m * P + P], ones[:, 0:1], start=True, stop=True)
                                mm.then_inc(ss1, 1)
                            pe.wait_ge(root, e + 1)
                            for m in range(NH):
                                i, o = m * D // HS, m * D % HS
                                if o == 0:
                                    pe.wait_ge(sq2, 2 * e + i + 1)
                                mm = nc.tensor.matmul(pbc[:, par, 0:D], ones[:, :], sq[i][:, o:o + D], start=(m == 0), stop=(m == NH - 1))
                                if o == HS - D:
                                    mm.then_inc(ss2, 1)

                @block.vector
                def _(dve):
                    if normed:
                        dve.wait_ge(g2_in, 16)
                        dve.sem_inc(s2_ready, 2)
                    with dve.Fori(0, EXPERTS // 2) as r:
                        for par in range(2):
                            e = 2 * r + par
                            w1e = lambda w: self.w1[:, bass.ds(e, 1), :, w, :].rearrange("p a c n -> p (a c) n")
                            w2e = lambda w: self.w2[:, bass.ds(e, 1), :, w, :].rearrange("p a c n -> p (a c) n")
                            dve.wait_ge(hi1, e + 1)
                            nc.vector.tensor_tensor(w1e(1), st1[par], w1e(0), ALU.subtract).then_inc(lo1, 1)
                            dve.wait_ge(hi2, e + 1)
                            nc.vector.tensor_tensor(w2e(1), st2, w2e(0), ALU.subtract).then_inc(lo2, 1)
                            if normed:
                                dve.wait_ge(root, e + 3)
                                nc.vector.tensor_scalar(rt[:, par, :], rt[:, par, :], 1e-12, None, ALU.max).then_inc(rt_ch, 1)
                                dve.wait_ge(rt_ch, 2 * e + 1)
                                nc.vector.reciprocal(rt[:, par, :], rt[:, par, :]).then_inc(rt_ch, 1)
                                dve.wait_ge(rt_ch, 2 * e + 2)
                                s2e = self.s2[:, bass.ds(e, 1), :].rearrange("p a n -> p (a n)")
                                nc.vector.tensor_tensor(s2e, s2e, rt[:, par, :], ALU.mult).then_inc(s2_ready, 1)
                    if normed:
                        dve.wait_ge(ss1, 2 * EXPERTS)
                        nc.vector.tensor_copy(sum1[:, :, :].rearrange("p c n -> p (c n)"), pss[:, 0:2 * EXPERTS * NH]).then_inc(sum_ready, 1)
                        dve.wait_ge(sum_ready, 1)
                        nc.vector.tensor_tensor(sum1[:, 0, :], sum1[:, 0, :], sum1[:, 1, :], ALU.add).then_inc(sum_ready, 1)
                        dve.wait_ge(sqrt1_done, 1)
                        dve.wait_ge(g1_in, 16)
                        s1 = self.s1[:, :, :]
                        nc.vector.tensor_scalar(s1, s1, 1e-12, None, ALU.max).then_inc(ch, 1)
                        dve.wait_ge(ch, 1)
                        nc.vector.reciprocal(s1, s1).then_inc(ch, 1)
                        dve.wait_ge(ch, 2)
                        nc.vector.tensor_tensor(s1, s1, g1[:, :, :], ALU.mult).then_inc(ch, 1)

    def moe_input(self, layer):
        nc, d, T = self.nc, self.dram, self.T
        twice = layer == 1
        with ExitStack() as ctx:
            sb = lambda n, s, t=F32: self.sb(ctx, T + n, s, t)
            sem = lambda n: self.sem(ctx, T + n)
            KINDS = (2, 3, 1) if twice else (2, 3)
            NORMS = 2 if twice else 1
            rows = sb("rows", [P, len(KINDS), B, D])
            lnr = sb("lnr", [P, 2, D]) if twice else None
            ones = sb("gones", [P, P])
            gg = sb("gg", [P, EXPERTS])
            gsq = sb("gsq", [P, DC, EXPERTS])
            eps = sb("eps", [P, 1])
            stats = sb("stats", [P, NORMS, HT, nc.vector.BN_STATS_DIM])
            mv = sb("mv", [P, NORMS, 2, HT, 2])
            sd = sb("sd", [P, NORMS, 2, HT])
            rstd = sb("rstd", [P, NORMS, 2, HT])
            shift = sb("shift", [P, NORMS, 2, HT])
            zs = sb("zs", [P, NORMS, 2, HT, D])
            gh = sb("gh", [P, 2, HT, D]) if twice else None
            zT = sb("zT", [P, 2, DC, P])
            lt = sb("lt", [P, 2, HT, EXPERTS])
            ptr = self.ps(ctx, T + "ptr", [P, 2, 512])
            plg = self.ps(ctx, T + "plg", [P, 2, 512])
            pgs = self.ps(ctx, T + "pgs", [P, 512])
            small_in, gsq_ready, gss_done, groot, gch, eps_set, rows_in, lnr_in, x_out = (
                sem(n) for n in ("small_in", "gsq", "gss", "groot", "gch", "eps_set", "rows_in", "lnr_in", "x_out"))
            stats_ready, stats_seen, mv_ready, sd_ready, rstd_ready, shift_ready, normed, scaled, z_ready = (
                [sem(f"{n}{i}") for i in range(NORMS)] for n in ("stats_ready", "stats_seen", "mv_ready", "sd_ready", "rstd_ready", "shift_ready", "normed", "scaled", "z_ready"))
            gh_ready, x_ready, tr_done, zT_ready, lg_done, lt_ready, lg_out, hi_done, lo_next, lo_done = (
                sem(n) for n in ("gh_ready", "x_ready", "tr_done", "zT_ready", "lg_done", "lt_ready", "lg_out", "hi_done", "lo_next", "lo_done"))
            SMALLS = 16 * (3 if twice else 4)

            PER = 2
            unit = lambda b, k, behind: unit_at(b, k, behind, PER)
            FINAL = NORMS

            def run(eng, slot):
                for b in range(2):
                    for k in range(PER):
                        slot(b, k)
                with eng.Fori(2, B) as b:
                    for k in range(PER):
                        slot(b, k)
                for k in range(PER, PER + FINAL + 1):
                    slot(B - 1, k)

            def at(b, k, behind):
                u = unit(b, k, behind)
                return u and (PER * u[0] + u[1], u[1], u[0])

            with nc.Block() as block:
                @block.gpsimd
                def _(pool):
                    pool.memset(eps[:, :], EPS).then_inc(eps_set, 1)
                    pool.memset(ones[:, :], 1.0).then_inc(eps_set, 1)

                    def slot(b, k):
                        if twice and (u := at(b, k, 1)):
                            n, h, ub = u
                            pool.wait_ge(z_ready[0], n + 1)
                            if used(n - 1):
                                pool.wait_ge(x_ready, n - 1)
                            pool.sem_inc(lo_next, 1)
                            nc.gpsimd.tensor_tensor(gh[:, h, :, :], zs[:, 0, h, :, :],
                                                    rows[:, 2, bass.ds(ub, 1), :].broadcast_to([P, HT, D]), ALU.mult).then_inc(gh_ready, 1)
                        if u := at(b, k, FINAL):
                            n, h, _ = u
                            pool.wait_ge(hi_done, n + 1)
                            pool.sem_inc(lo_next, 1)
                            nc.gpsimd.tensor_tensor(self.zh[:, bass.ds(HT * n, HT), 1, :], zs[:, NORMS - 1, h, :, :],
                                                    self.zh[:, bass.ds(HT * n, HT), 0, :], ALU.subtract).then_inc(lo_done, 1)

                    run(pool, slot)

                @block.sync
                def _(sp):
                    sp.dma_start(self.gw[:, :, :], d["L1_ffn_rW" if twice else "L0_gateT"].rearrange("(c p) e -> p c e", p=P)).then_inc(small_in, 16)
                    sp.dma_start(self.gb[:, :], d["L1_ffn_rb" if twice else "L0_ffn_gate_b"].partition_broadcast(P)).then_inc(small_in, 16)
                    sp.dma_start(self.b1[:, :, :], d[f"L{layer}_b1c"]).then_inc(small_in, 16)
                    if not twice:
                        sp.dma_start(gg[:, :], d["L0_ffn_gate_g"].partition_broadcast(P)).then_inc(small_in, 16)
                    for j, kind in enumerate(KINDS):
                        sp.dma_start(rows[:, j, :, :].rearrange("p b d -> p (b d)"), self.mod_d[layer, kind, :, :].rearrange("b d -> (b d)").partition_broadcast(P)).then_inc(rows_in, 16)
                    if twice:
                        sp.dma_start(lnr[:, 0, :], d["L1_ffn_ln_g"].partition_broadcast(P)).then_inc(lnr_in, 16)
                        sp.dma_start(lnr[:, 1, :], d["L1_ffn_ln_b"].partition_broadcast(P)).then_inc(lnr_in, 16)
                    with sp.Fori(0, B) as b:
                        if twice:
                            sp.wait_ge(x_ready, 2 * b + 2)
                        sp.dma_start(self.x_d.rearrange("(t p) d -> p t d", p=P)[:, bass.ds(TPB * b, TPB), :], self.x[:, bass.ds(TPB * b, TPB), :]).then_inc(x_out, 16)
                    sp.wait_ge(x_out, 16 * B)

                @block.scalar
                def _(act):
                    act.wait_ge(eps_set, 1)
                    if not twice:
                        act.wait_ge(small_in, SMALLS)
                        nc.scalar.activation(gsq[:, :, :], self.gw[:, :, :], ACT.Square).then_inc(gsq_ready, 1)
                        act.wait_ge(gss_done, 1)
                        nc.scalar.activation(self.gs[:, :], pgs[:, 0:EXPERTS], ACT.Sqrt).then_inc(groot, 1)

                    def slot(b, k):
                        for i in range(NORMS):
                            if u := at(b, k, i):
                                n, h, _ = u
                                act.wait_ge(mv_ready[i], n + 1)
                                nc.scalar.activation(sd[:, i, h, :], mv[:, i, h, :, 1], ACT.Sqrt, bias=eps[:, :]).then_inc(sd_ready[i], 1)
                                act.wait_ge(shift_ready[i], n + 1)
                                if used(n - 1):
                                    if i == NORMS - 1:
                                        act.wait_ge(tr_done, HT * (n - 1))
                                        act.wait_ge(lo_done, n - 1)
                                    else:
                                        act.wait_ge(normed[1], HT * (n - 1))
                                        act.wait_ge(gh_ready, n - 1)
                                for t in range(HT):
                                    src = self.x[:, bass.ds(HT * n + t, 1), :].rearrange("p a d -> p (a d)") if i == 0 else zs[:, 0, h, t, :]
                                    nc.scalar.activation(zs[:, i, h, t, :], src, ACT.Identity, bias=shift[:, i, h, t:t + 1], scale=rstd[:, i, h, t:t + 1]).then_inc(normed[i], 1)
                        if u := at(b, k, FINAL):
                            n, h, _ = u
                            act.wait_ge(z_ready[NORMS - 1], n + 1)
                            nc.scalar.activation(self.zh[:, bass.ds(HT * n, HT), 0, :], zs[:, NORMS - 1, h, :, :], ACT.Copy).then_inc(hi_done, 1)
                            for t in range(HT):
                                act.wait_ge(tr_done, HT * n + t + 1)
                                nc.scalar.activation(zT[:, t % 2, :, :], ptr[:, t % 2, 0:D].rearrange("p (c n) -> p c n", c=DC), ACT.Copy).then_inc(zT_ready, 1)

                    run(act, slot)

                @block.tensor
                def _(pe):
                    pe.wait_ge(small_in, SMALLS)
                    if not twice:
                        pe.wait_ge(eps_set, 2)
                        pe.wait_ge(gsq_ready, 1)
                        for c in range(DC):
                            mm = nc.tensor.matmul(pgs[:, 0:EXPERTS], ones[:, :], gsq[:, c, :], start=(c == 0), stop=(c == DC - 1))
                        mm.then_inc(gss_done, 1)

                    def slot(b, k):
                        if u := at(b, k, FINAL):
                            n, h, _ = u
                            pe.wait_ge(z_ready[NORMS - 1], n + 1)
                            if used(n - 1):
                                pe.wait_ge(lg_out, n - 1)
                            for t in range(HT + 1):
                                if t < HT:
                                    for c in range(DC):
                                        tr = nc.tensor.transpose(ptr[:, t % 2, c * P:(c + 1) * P], zs[:, NORMS - 1, h, t, c * P:(c + 1) * P], self.ident[:, :])
                                    tr.then_inc(tr_done, 1)
                                if t >= 1:
                                    pe.wait_ge(zT_ready, HT * n + t)
                                    for c in range(DC):
                                        mm = nc.tensor.matmul(plg[:, h, (t - 1) * EXPERTS:t * EXPERTS], zT[:, (t - 1) % 2, c, :], self.gw[:, c, :],
                                                              start=(c == 0), stop=(c == DC - 1), skip_group_check=True)
                            mm.then_inc(lg_done, 1)

                    run(pe, slot)

                @block.vector
                def _(dve):
                    dve.wait_ge(small_in, SMALLS)
                    dve.wait_ge(rows_in, 16 * len(KINDS))
                    if twice:
                        dve.wait_ge(lnr_in, 32)
                    else:
                        dve.wait_ge(groot, 1)
                        nc.vector.tensor_scalar(self.gs[:, :], self.gs[:, :], 1e-12, None, ALU.max).then_inc(gch, 1)
                        dve.wait_ge(gch, 1)
                        nc.vector.reciprocal(self.gs[:, :], self.gs[:, :]).then_inc(gch, 1)
                        dve.wait_ge(gch, 2)
                        nc.vector.tensor_tensor(self.gs[:, :], self.gs[:, :], gg[:, :], ALU.mult).then_inc(gch, 1)
                        dve.wait_ge(gch, 3)

                    def moments(i, n, h):
                        for t in range(HT):
                            src = self.x[:, bass.ds(HT * n + t, 1), :].rearrange("p a d -> p (a d)") if i == 0 else zs[:, 0, h, t, :]
                            nc.vector.bn_stats(stats[:, i, t, :], src).then_inc(stats_ready[i], 1)
                        dve.wait_ge(stats_ready[i], HT * n + HT)
                        dve.sem_inc(stats_seen[i], 1)
                        for t in range(HT):
                            a = nc.vector.bn_aggr(mv[:, i, h, t, :], stats[:, i, t, :])
                        a.then_inc(mv_ready[i], 1)

                    def inverse(i, n, h):
                        dve.wait_ge(sd_ready[i], n + 1)
                        nc.vector.reciprocal(rstd[:, i, h, :], sd[:, i, h, :]).then_inc(rstd_ready[i], 1)
                        dve.wait_ge(rstd_ready[i], n + 1)
                        nc.vector.scalar_tensor_tensor(out=shift[:, i, h, :], in0=mv[:, i, h, :, 0], scalar=-1.0, in1=rstd[:, i, h, :],
                                                       op0=ALU.mult, op1=ALU.mult).then_inc(shift_ready[i], 1)

                    def scale(i, n, h, ub):
                        z = zs[:, i, h, :, :]
                        if i == 0:
                            by, plus = (rows[:, j, bass.ds(ub, 1), :].broadcast_to([P, HT, D]) for j in (1, 0))
                        else:
                            by, plus = (lnr[:, j, :].unsqueeze(1).broadcast_to([P, HT, D]) for j in (0, 1))
                        dve.wait_ge(normed[i], HT * n + HT)
                        nc.vector.tensor_tensor(z, z, by, ALU.mult).then_inc(scaled[i], 1)
                        dve.wait_ge(scaled[i], n + 1)
                        nc.vector.tensor_tensor(z, z, plus, ALU.add).then_inc(z_ready[i], 1)

                    def slot(b, k):
                        if u := at(b, k, 0):
                            moments(0, *u[:2])
                        if u := at(b, k, 1):
                            scale(0, *u)
                        if u := at(b, k, 0):
                            inverse(0, *u[:2])
                        if twice:
                            if u := at(b, k, 1):
                                dve.wait_ge(z_ready[0], u[0] + 1)
                                moments(1, *u[:2])
                            if u := at(b, k, 2):
                                n, h, _ = u
                                scale(1, *u)
                                dve.wait_ge(gh_ready, n + 1)
                                xh = self.x[:, bass.ds(HT * n, HT), :]
                                nc.vector.tensor_tensor(xh, xh, gh[:, h, :, :], ALU.add).then_inc(x_ready, 1)
                            if u := at(b, k, 1):
                                inverse(1, *u[:2])
                        if u := at(b, k, FINAL + 1):
                            n, h, _ = u
                            dve.wait_ge(lg_done, n + 1)
                            out = self.lg[:, bass.ds(HT * n, HT), :]
                            src = plg[:, h, 0:HT * EXPERTS].rearrange("p (t e) -> p t e", e=EXPERTS)
                            erow = lambda a: a[:, :].unsqueeze(1).broadcast_to([P, HT, EXPERTS])
                            if not twice:
                                nc.vector.tensor_tensor(lt[:, h, :, :], src, erow(self.gs), ALU.mult).then_inc(lt_ready, 1)
                                dve.wait_ge(lt_ready, n + 1)
                                src = lt[:, h, :, :]
                            nc.vector.tensor_tensor(out, src, erow(self.gb), ALU.add).then_inc(lg_out, 1)

                    run(dve, slot)

    def moe_route(self, layer):
        nc, d, T = self.nc, self.dram, self.T
        TE = TILES * EXPERTS
        with ExitStack() as ctx:
            sb = lambda n, s, t=F32: self.sb(ctx, T + n, s, t)
            sem = lambda n: self.sem(ctx, T + n)
            iota = sb("iota", [P, 64])
            low = sb("low", [P, P])
            ones = sb("rones", [P, TE])
            te = {n: sb("te_" + n, [P, TILES, EXPERTS]) for n in ("eq", "oh1", "oh2", "mask")}
            et = {n: sb("et_" + n, [P, EXPERTS, TILES]) for n in ("cnt", "sum", "slot")}
            best = sb("best", [P, 2, TILES])
            at = sb("at", [P, TILES])
            i99 = sb("i99", [P, EXPERTS])
            e8 = {n: sb("e8_" + n, [P, EXPERTS]) for n in ("prev", "n", "incl", "base")}
            M = N_TOK // ROWS
            work = sb("work", [P, max(TE, XT * (EXPERTS - 1))])
            te["tmp"] = work[:, 0:TE].rearrange("p (t e) -> p t e", e=EXPERTS)
            cmp16 = work[:, 0:EXPERTS * M].rearrange("p (e m) -> p e m", m=M)
            cmpj = work[:, 0:XT * (EXPERTS - 1)].rearrange("p (j e) -> p j e", e=EXPERTS - 1)
            thr = sb("thr", [P, N_TOK // ROWS])
            fl = sb("fl", [P, 2, TILES])
            oj = et["cnt"][:, :, :].rearrange("p e t -> p (e t)")[:, 0:XT]
            pw = self.ps(ctx, T + "pw", [P, 512])
            pc = self.ps(ctx, T + "pc", [P, 512])
            const_in, ones_set, mask_ready, sums, ch, shifted, ex_ready = (sem(n) for n in ("const_in", "rones_set", "mask_ready", "sums", "rch", "shifted", "ex_ready"))
            with nc.Block() as block:
                @block.sync
                def _(sp):
                    sp.dma_start(iota[:, :], d["c_iota"]).then_inc(const_in, 16)
                    sp.dma_start(low[:, :], d["c_before"]).then_inc(const_in, 16)

                @block.gpsimd
                def _(pool):
                    pool.memset(ones[:, :], 1.0).then_inc(ones_set, 1)

                @block.scalar
                def _(act):
                    if layer == 1:
                        act.wait_ge(shifted, 1)
                        nc.scalar.activation(te["tmp"][:, :, :], te["tmp"][:, :, :], ACT.Exp).then_inc(ex_ready, 1)

                @block.tensor
                def _(pe):
                    pe.wait_ge(const_in, 32)
                    pe.wait_ge(ones_set, 1)
                    pe.wait_ge(mask_ready, 1)
                    mask = te["mask"][:, :, :].rearrange("p t e -> p e t")
                    nc.tensor.matmul(pw[:, 0:TE], low[:, :], mask, start=True, stop=True)
                    nc.tensor.matmul(pc[:, 0:TE], ones[:, 0:P], mask, start=True, stop=True).then_inc(sums, 1)

                @block.vector
                def _(dve):
                    n = [0]

                    def link(ins):
                        n[0] += 1
                        ins.then_inc(ch, 1)
                        dve.wait_ge(ch, n[0])

                    tt, ts = nc.vector.tensor_tensor, nc.vector.tensor_scalar
                    lg = self.lg[:, :, :]
                    eq, oh1, oh2, mask, tmp = (te[k][:, :, :] for k in ("eq", "oh1", "oh2", "mask", "tmp"))
                    over_e = lambda a: a.unsqueeze(2).broadcast_to([P, TILES, EXPERTS])
                    over_t = lambda a: a.unsqueeze(1).broadcast_to([P, TILES, EXPERTS])
                    dve.wait_ge(const_in, 32)
                    dve.wait_ge(ones_set, 1)
                    link(ts(i99[:, :], iota[:, 0:EXPERTS], -99.0, None, ALU.add))

                    def choose(src, k, oh):
                        link(nc.vector.tensor_reduce(best[:, k, :], src, AX.X, ALU.max))
                        link(tt(eq, src, over_e(best[:, k, :]), ALU.is_equal))
                        link(tt(eq, eq, over_t(i99[:, :]), ALU.mult))
                        link(nc.vector.tensor_reduce(at[:, :], eq, AX.X, ALU.min))
                        link(tt(oh, over_t(i99[:, :]), over_e(at[:, :]), ALU.is_equal))

                    choose(lg, 0, oh1)
                    link(nc.vector.scalar_tensor_tensor(out=tmp, in0=oh1, scalar=-1e38, in1=lg, op0=ALU.mult, op1=ALU.add))
                    choose(tmp, 1, oh2)
                    tt(mask, oh1, oh2, ALU.add).then_inc(mask_ready, 1)
                    if layer == 1:
                        tt(tmp, lg, over_e(best[:, 0, :]), ALU.subtract).then_inc(shifted, 1)
                        dve.wait_ge(ex_ready, 1)
                        link(nc.vector.tensor_reduce(at[:, :], tmp, AX.X, ALU.add))
                        link(nc.vector.reciprocal(at[:, :], at[:, :]))
                        link(tt(tmp, tmp, over_e(at[:, :]), ALU.mult))
                        for k, oh in enumerate((oh1, oh2)):
                            link(tt(eq, tmp, oh, ALU.mult))
                            link(nc.vector.tensor_reduce(self.wt[:, k, :], eq, AX.X, ALU.add))
                        link(tt(at[:, :], self.wt[:, 0, :], self.wt[:, 1, :], ALU.add))
                        link(ts(at[:, :], at[:, :], 1e-8, None, ALU.max))
                        link(nc.vector.reciprocal(at[:, :], at[:, :]))
                        link(tt(self.wt[:, :, :], self.wt[:, :, :], at[:, :].unsqueeze(1).broadcast_to([P, 2, TILES]), ALU.mult))
                    dve.wait_ge(sums, 1)
                    cnt, tot, slot = (et[k][:, :, :] for k in ("cnt", "sum", "slot"))
                    flat = lambda a: a.rearrange("p e t -> p (e t)")
                    prev, ne, incl, base = (e8[k][:, :] for k in ("prev", "n", "incl", "base"))
                    link(nc.vector.tensor_copy(flat(cnt), pc[:, 0:TE]))
                    link(nc.vector.tensor_tensor_scan(flat(tot), ones[:, 0:TE], flat(cnt), 0.0, ALU.mult, ALU.add))
                    link(nc.vector.memset(prev, 0.0))
                    link(nc.vector.tensor_copy(e8["prev"][:, 1:EXPERTS], et["sum"][:, 0:EXPERTS - 1, TILES - 1]))
                    link(tt(ne, et["sum"][:, :, TILES - 1], prev, ALU.subtract))
                    link(ts(thr[:, :], iota[:, 0:M], float(ROWS), None, ALU.mult))
                    link(tt(cmp16[:, :, :], ne.unsqueeze(2).broadcast_to([P, EXPERTS, M]), thr[:, :].unsqueeze(1).broadcast_to([P, EXPERTS, M]), ALU.is_gt))
                    link(nc.vector.tensor_reduce(ne, cmp16[:, :, :], AX.X, ALU.add))
                    link(nc.vector.tensor_tensor_scan(incl, ones[:, 0:EXPERTS], ne, 0.0, ALU.mult, ALU.add))
                    link(tt(base, incl, ne, ALU.subtract))
                    link(nc.vector.scalar_tensor_tensor(out=base, in0=base, scalar=float(ROWS), in1=prev, op0=ALU.mult, op1=ALU.subtract))
                    link(tt(slot, tot, cnt, ALU.subtract))
                    link(tt(slot, slot, base.unsqueeze(2).broadcast_to([P, EXPERTS, TILES]), ALU.add))
                    link(tt(flat(slot), flat(slot), pw[:, 0:TE], ALU.add))
                    for k, oh in enumerate((oh1, oh2)):
                        link(tt(eq, oh, slot.rearrange("p e t -> p t e"), ALU.mult))
                        link(nc.vector.tensor_reduce(fl[:, k, :], eq, AX.X, ALU.add))
                    link(nc.vector.tensor_copy(self.slot[:, :, :], fl[:, :, :]))
                    E1 = EXPERTS - 1
                    link(tt(cmpj[:, :, :], e8["incl"][:, 0:E1].unsqueeze(1).broadcast_to([P, XT, E1]), iota[:, 0:XT].unsqueeze(2).broadcast_to([P, XT, E1]), ALU.is_le))
                    link(nc.vector.tensor_reduce(oj, cmpj[:, :, :], AX.X, ALU.add))
                    link(nc.vector.tensor_copy(self.owner[:, :], oj))

    def moe_tiles(self, layer):
        nc, d, T, H, NH = self.nc, self.dram, self.T, self.H, self.NH
        func = ACT.Silu if layer == 0 else ACT.Gelu
        PAIRS = ((0, 0), (0, 1), (1, 0))
        with ExitStack() as ctx:
            sb = lambda n, s, t=F32: self.sb(ctx, T + n, s, t)
            sem = lambda n: self.sem(ctx, T + n)
            b2 = self.x[:, 0:EXPERTS, :]
            y = self.x[:, EXPERTS:EXPERTS + 4, :].rearrange("p (b a) d -> p b a d", b=2)
            ys = self.x[:, EXPERTS + 4:EXPERTS + 6, :]
            hf = self.x[:, EXPERTS + 6:EXPERTS + 10, :].rearrange("p (g q) n -> p g q n", g=2)
            zh, used_to = self.zh[:, :, :, :].rearrange("p t w d -> p (t w d)"), 0

            def half(n):
                nonlocal used_to
                used_to += n
                return zh[:, used_to - n:used_to]

            xr = half(2 * 2 * 2 * D).rearrange("p (b a n) -> p b a n", b=2, a=2)
            xT = half(2 * 2 * DC * ROWS).rearrange("p (b h c n) -> p b h c n", b=2, h=2, c=DC)
            hh = half(2 * NH * 2 * ROWS).rearrange("p (b m h n) -> p b m h n", b=2, m=NH, h=2)
            ys_ready = sem("ys_ready")
            pt = self.ps(ctx, T + "pt", [P, 2, 1024], F16)
            ph = self.ps(ctx, T + "ph", [P, 4, 512])
            py = self.ps(ctx, T + "py", [P, 2, 512])
            b2_in, tr_done, xT_ready, h_done, act_done, hi_done, lo_done, y_done, y_taken = (
                sem(n) for n in ("b2_in", "ttr_done", "xT_ready", "h_done", "act_done", "thi_done", "tlo_done", "y_done", "y_taken"))
            x_in = [sem(f"x_in{i}") for i in range(2)]
            y_out = [sem(f"y_out{i}") for i in range(2)]
            G = NH // 2
            with nc.Block() as block:
                @block.sync
                def _(sp):
                    sp.dma_start(b2[:, :, :], d[f"L{layer}_ffn_b2"].rearrange("e n -> (e n)").partition_broadcast(P).rearrange("p (e n) -> p e n", e=EXPERTS)).then_inc(b2_in, 16)
                    for par in range(2):
                        sp.sem_inc(y_out[par], 16)

                    def load(j, par):
                        sp.dma_start(xr[:, par, :, :], self.xs_d[layer][bass.ds(j * ROWS, ROWS), :].rearrange("(a p) n -> p a n", p=P)).then_inc(x_in[par], 16)

                    def turn(j, par, more):
                        if more:
                            sp.wait_ge(tr_done, j + 3)
                            load(j + 4, par)
                        sp.wait_ge(y_taken, 2 * j + 4)
                        sp.dma_start(self.ys_d[bass.ds(j * ROWS, ROWS), :].rearrange("(a p) n -> p a n", p=P), y[:, par, :, :]).then_inc(y_out[par], 16)

                    for j in range(4):
                        if j >= 2:
                            sp.wait_ge(tr_done, j - 1)
                        load(j, j % 2)
                    with sp.Fori(0, (XT - 4) // 2) as r:
                        for par in range(2):
                            turn(2 * r + par, par, True)
                    for j in range((XT - 4) // 2 * 2, XT):
                        turn(j, j % 2, j + 4 < XT)
                    for par in range(2):
                        sp.wait_ge(y_out[par], 16 * len(range(par, XT, 2)) + 16)

                @block.tensor
                def _(pe):
                    def turned(j, par, n_in):
                        pe.wait_ge(x_in[par], n_in)
                        for hl in range(2):
                            for c in range(DC):
                                for a in range(2):
                                    o = ((hl * DC + c) * 2 + a) * P
                                    tr = nc.tensor.transpose(pt[:, par, o:o + P], xr[:, par, a, hl * D + c * P:hl * D + (c + 1) * P], self.ident_h[:, :])
                        tr.then_inc(tr_done, 1)

                    def first(j, par):
                        e = nc.tensor.value_load(self.owner[0:1, bass.ds(j, 1)], min_val=0, max_val=EXPERTS - 1)
                        pe.wait_ge(xT_ready, j + 1)
                        for m in range(NH):
                            g, q = m // 2, m % 2
                            if q == 0:
                                pe.wait_ge(act_done, NH * j + m + 2)
                            for c in range(DC):
                                for i, (wp, xp) in enumerate(PAIRS):
                                    mm = nc.tensor.matmul(ph[:, (G * par + g) % 4, q * ROWS:(q + 1) * ROWS], self.w1[:, bass.ds(e, 1), c, wp, m * P:(m + 1) * P].rearrange("p a n -> p (a n)"),
                                                          xT[:, par, xp, c, :], start=(c == 0 and i == 0), stop=(c == DC - 1 and i == 2), skip_group_check=True)
                            mm.then_inc(h_done, 1)

                    def second(j, par):
                        e = nc.tensor.value_load(self.owner[0:1, bass.ds(j, 1)], min_val=0, max_val=EXPERTS - 1)
                        for a in range(2):
                            pe.wait_ge(y_taken, 2 * j + a + 1)
                            for m in range(NH):
                                if a == 0 and m % 2 == 0:
                                    pe.wait_ge(lo_done, G * j + m // 2 + 3)
                                for i, (wp, hp) in enumerate(PAIRS):
                                    mm = nc.tensor.matmul(py[:, a, 0:D], hh[:, par, m, hp, a * P:(a + 1) * P],
                                                          self.w2[:, bass.ds(e, 1), m, wp, :].rearrange("p a n -> p (a n)"), start=(m == 0 and i == 0), stop=(m == NH - 1 and i == 2))
                            mm.then_inc(y_done, 1)

                    turned(0, 0, 16)
                    turned(1, 1, 16)
                    first(0, 0)
                    with pe.Fori(0, (XT - 2) // 2) as r:
                        for par in range(2):
                            j = 2 * r + par
                            first(j + 1, 1 - par)
                            turned(j + 2, par, 16 * r + 32)
                            second(j, par)
                    for j in range((XT - 2) // 2 * 2, XT):
                        if j + 1 < XT:
                            first(j + 1, (j + 1) % 2)
                        if j + 2 < XT:
                            turned(j + 2, j % 2, 16 * (j // 2) + 32)
                        second(j, j % 2)

                @block.scalar
                def _(act):
                    act.sem_inc(act_done, 8)

                    def hidden(j, par):
                        e = nc.scalar.value_load(self.owner[0:1, bass.ds(j, 1)], min_val=0, max_val=EXPERTS - 1)
                        for m in range(NH):
                            g, q = m // 2, m % 2
                            if q == 0:
                                act.wait_ge(h_done, NH * j + m + 2)
                                act.wait_ge(lo_done, G * j + g + 1)
                            col = lambda a: a[:, bass.ds(e, 1), m:m + 1].rearrange("p a m -> p (a m)")
                            if layer == 0:
                                nc.scalar.activation(hf[:, g % 2, q, :], ph[:, (G * par + g) % 4, q * ROWS:(q + 1) * ROWS], func, bias=col(self.b1), scale=col(self.s1)).then_inc(act_done, 1)
                            else:
                                nc.scalar.activation(hf[:, g % 2, q, :], ph[:, (G * par + g) % 4, q * ROWS:(q + 1) * ROWS], func, bias=col(self.b1)).then_inc(act_done, 1)

                    with act.Fori(0, XT // 2) as r:
                        for par in range(2):
                            hidden(2 * r + par, par)
                    for j in range(XT // 2 * 2, XT):
                        hidden(j, j % 2)

                @block.vector
                def _(dve):
                    dve.sem_inc(lo_done, 2)
                    dve.sem_inc(y_taken, 2)
                    dve.wait_ge(b2_in, 16)

                    def out(j, par, n_out):
                        e = nc.vector.value_load(self.owner[0:1, bass.ds(j, 1)], min_val=0, max_val=EXPERTS - 1)
                        dve.wait_ge(y_out[par], n_out)
                        for a in range(2):
                            dve.wait_ge(y_done, 2 * j + a + 1)
                            src = py[:, a, 0:D]
                            if layer == 0:
                                nc.vector.tensor_tensor(ys[:, a, :], src, self.s2[:, bass.ds(e, 1), :].rearrange("p a n -> p (a n)"), ALU.mult).then_inc(ys_ready, 1)
                                dve.wait_ge(ys_ready, 2 * j + a + 1)
                                src = ys[:, a, :]
                            nc.vector.tensor_tensor(y[:, par, a, :], src, b2[:, bass.ds(e, 1), :].rearrange("p a n -> p (a n)"), ALU.add).then_inc(y_taken, 1)

                    def turned(j, par):
                        dve.wait_ge(tr_done, j + 1)
                        nc.vector.tensor_copy(xT[:, par, :, :, :].rearrange("p h c n -> p (h c n)"), pt[:, par, :]).then_inc(xT_ready, 1)

                    def tile(j, par):
                        for g in range(G):
                            dve.wait_ge(act_done, NH * j + 2 * g + 2 + 8)
                            hi, lo = (hh[:, par, 2 * g:2 * g + 2, w, :] for w in range(2))
                            nc.vector.tensor_copy(hi, hf[:, g % 2, :, :]).then_inc(hi_done, 1)
                            dve.wait_ge(hi_done, G * j + g + 1)
                            nc.vector.tensor_tensor(lo, hf[:, g % 2, :, :], hi, ALU.subtract).then_inc(lo_done, 1)

                    turned(0, 0)
                    turned(1, 1)
                    tile(0, 0)
                    with dve.Fori(0, (XT - 2) // 2) as r:
                        for par in range(2):
                            tile(2 * r + par + 1, 1 - par)
                            turned(2 * r + par + 2, par)
                            out(2 * r + par, par, 16 * r + 16)
                    for j in range((XT - 2) // 2 * 2, XT):
                        if j + 1 < XT:
                            tile(j + 1, (j + 1) % 2)
                        if j + 2 < XT:
                            turned(j + 2, j % 2)
                        out(j, j % 2, 16 * (j // 2) + 16)

    def moe_combine(self, layer):
        nc, T = self.nc, self.T
        with ExitStack() as ctx:
            sb = lambda n, s, t=F32: self.sb(ctx, T + n, s, t)
            NG = len(self.got_in)
            gate = sb("gate", [P, B, D])
            got = sb("got", [P, NG, 2, D])
            gate_in, stored = self.sem(ctx, T + "gate_in"), self.sem(ctx, T + "stored")
            x_in = [self.sem(ctx, T + f"x_back{b}") for b in range(B)]
            got_in = self.got_in
            got0 = layer * 32 * (TILES // NG)
            ch, done = self.sem(ctx, T + "cch"), self.sem(ctx, T + "cdone")
            with nc.Block() as block:
                @block.sync
                def _(sp):
                    sp.dma_start(gate[:, :, :].rearrange("p b d -> p (b d)"), self.mod_d[layer, 1, :, :].rearrange("b d -> (b d)").partition_broadcast(P)).then_inc(gate_in, 16)
                    for b in range(B):
                        xb = slice(b * TPB, (b + 1) * TPB)
                        sp.dma_start(self.x[:, xb, :], self.x_d.rearrange("(t p) d -> p t d", p=P)[:, xb, :]).then_inc(x_in[b], 16)
                    if layer == LAYERS - 1:
                        for n in range(2 * B):
                            sp.wait_ge(done, HT * (n + 1))
                            xh = slice(n * HT, (n + 1) * HT)
                            sp.dma_start(self.out.rearrange("b (t p) d -> p (b t) d", p=P)[:, xh, :], self.x[:, xh, :]).then_inc(stored, 16)
                        sp.wait_ge(stored, 16 * 2 * B)

                @block.gpsimd
                def _(pool):
                    for t in range(TILES):
                        if t >= NG:
                            pool.wait_ge(done, t - NG + 1)
                        for k in range(2):
                            pool.indirect_dma_start(got[:, t % NG, k, :], None, self.ys_d[:, :],
                                                    bass.IndirectOffsetOnAxis(ap=self.slot[:, k, t:t + 1], axis=0)).then_inc(got_in[t % NG], 16)

                @block.vector
                def _(dve):
                    n = [0]

                    def link(ins):
                        n[0] += 1
                        ins.then_inc(ch, 1)
                        dve.wait_ge(ch, n[0])

                    dve.wait_ge(gate_in, 16)
                    for t in range(TILES):
                        if t % TPB == 0:
                            dve.wait_ge(x_in[t // TPB], 16)
                        dve.wait_ge(got_in[t % NG], got0 + 32 * (t // NG) + 32)
                        g0, g1 = got[:, t % NG, 0, :], got[:, t % NG, 1, :]
                        if layer == 0:
                            link(nc.vector.tensor_tensor(g0, g0, g1, ALU.add))
                        else:
                            link(nc.vector.tensor_scalar(g0, g0, self.wt[:, 0, t:t + 1], None, ALU.mult))
                            link(nc.vector.scalar_tensor_tensor(out=g0, in0=g1, scalar=self.wt[:, 1, t:t + 1], in1=g0, op0=ALU.mult, op1=ALU.add))
                        link(nc.vector.tensor_tensor(g0, g0, gate[:, t // TPB, :], ALU.mult))
                        nc.vector.tensor_tensor(self.x[:, t, :], self.x[:, t, :], g0, ALU.add).then_inc(done, 1)


def host_layout(inputs):
    a = {n: np.ascontiguousarray(v) for n, v in inputs.items()}
    for n in "qkvo":
        a[f"L0_attn_w{n}_wT"] = np.ascontiguousarray(a.pop(f"L0_attn_w{n}_w").T)
    for n in "qk":
        a[f"{n}n_rep"] = np.tile(a.pop(f"L0_attn_{n}n_w"), P // HD)
    columns = lambda v: np.ascontiguousarray(v.reshape(EXPERTS, -1, P).transpose(2, 0, 1))
    a["L0_gateT"] = np.ascontiguousarray(a.pop("L0_ffn_gate_v").T)
    a["L0_w1T"] = np.ascontiguousarray(a.pop("L0_ffn_w1_v").transpose(0, 2, 1))
    a["L0_w2T"] = np.ascontiguousarray(a.pop("L0_ffn_w2_v").transpose(0, 2, 1))
    a["L0_b1c"], a["L0_g1c"], a["L1_b1c"] = columns(a.pop("L0_ffn_b1")), columns(a.pop("L0_ffn_w1_g")), columns(a.pop("L1_ffn_b1"))
    a.update(constants())
    return a


def kernel(**inputs):
    import concourse.bacc as bacc
    from concourse.bass_utils import run_bass_kernel_spmd

    nc = bacc.Bacc("TRN2", target_bir_lowering=False, num_devices=1)
    arrays = host_layout(inputs)
    dram = {n: nc.dram_tensor(n, a.shape, mybir.dt.from_np(a.dtype), kind="ExternalInput").ap() for n, a in arrays.items()}
    out = nc.dram_tensor("out", (B, L, D), F32, kind="ExternalOutput").ap()
    Program(nc, dram, out).build()
    return run_bass_kernel_spmd(nc, [arrays], core_ids=[0]).results[0]["out"]
```
